# Optimizing a Trainium2 kernel written in Bass

```python
import numpy as np
import jax
import jax.numpy as jnp

def _softmax(x, axis=-1):
    return jax.nn.softmax(x, axis=axis)

def _gelu(x):
    return jax.nn.gelu(x, approximate=True)

def _silu(x):
    return jax.nn.silu(x)

def _sigmoid(x):
    return jax.nn.sigmoid(x)

def _layernorm(x, axis=-1, eps=1e-05):
    m = jnp.mean(x, axis=axis, keepdims=True)
    v = jnp.var(x, axis=axis, keepdims=True)
    return (x - m) / jnp.sqrt(v + eps)

def _scatter_add(tgt, idx, src, axis=0):
    return tgt.at[idx].add(src)

def _segment_sum(src, seg, n):
    return jax.ops.segment_sum(src, seg, n)
kernel_name = 'mk_perceiver_d1_seqx_r2_9c17eb'

def setup_inputs(seed: int=0):
    np.random.seed(seed)
    _w = jnp.asarray

    def _rec_inputs():
        import jax
        import jax.numpy as jnp
        _rk = jax.random.key(seed)
        x = -0.0002928 + 1 * jax.random.normal(jax.random.fold_in(_rk, 1), (4, 128, 512), jnp.float32)
        _lenS = 128 - jax.random.randint(jax.random.fold_in(_rk, 7), (4,), 0, max(1, 128 // 4) + 1, jnp.int32)
        _lenS2 = 2048 - jax.random.randint(jax.random.fold_in(_rk, 8), (4,), 0, max(1, 2048 // 4) + 1, jnp.int32)
        _ctx_1024P = jax.random.normal(jax.random.fold_in(_rk, 11), (4, 16, 512), jnp.float32)
        _ctx_1024c = jax.random.dirichlet(jax.random.fold_in(_rk, 511), 0.3 * jnp.ones((16,), jnp.float32), (4, 2048))
        _ctx_1024t = jnp.einsum('bsk,bkd->bsd', _ctx_1024c, _ctx_1024P)
        _ctx_1024t = _ctx_1024t * jax.lax.rsqrt(jnp.mean(jnp.square(_ctx_1024t)) + 1e-12) * 0.953939
        ctx_1024 = -1.39393e-06 + 0.999914 * (_ctx_1024t + 0.3 * jax.random.normal(jax.random.fold_in(_rk, 611), (4, 2048, 512), jnp.float32))
        fside_1x1xSxS2_0 = 0.000376506 + 0.999991 * jax.random.normal(jax.random.fold_in(_rk, 12), (1, 1, 128, 2048), jnp.float32)
        return (x, ctx_1024, fside_1x1xSxS2_0)
    x, ctx_1024, fside_1x1xSxS2_0 = _rec_inputs()

    def _L0_xattn_setup():
        import jax, jax.numpy as jnp
        import numpy as np
        NUM_HEADS = 16
        KEY_DEPTH = 512

        def _split_heads(x, h):
            b, l, d = x.shape
            return x.reshape(b, l, h, d // h).transpose(0, 2, 1, 3)
        key = jax.random.key(seed)
        ks = jax.random.split(key, 7)
        B, L, D = (2, 1024, 512)
        scale = 1.0 / np.sqrt(D)
        return {'query_antecedent': jax.random.normal(ks[0], (B, L, D), jnp.float32), 'memory_antecedent': jax.random.normal(ks[1], (B, L, D), jnp.float32), 'bias': jax.random.normal(ks[2], (1, 1, L, L), jnp.float32), 'Wq': jax.random.normal(ks[3], (D, KEY_DEPTH), jnp.float32) * scale, 'Wk': jax.random.normal(ks[4], (D, KEY_DEPTH), jnp.float32) * scale, 'Wv': jax.random.normal(ks[5], (D, KEY_DEPTH), jnp.float32) * scale, 'Wo': jax.random.normal(ks[6], (KEY_DEPTH, D), jnp.float32) * scale}
    _L0_xattn_all = _L0_xattn_setup()
    _L0_xattn_in = {k: v for k, v in _L0_xattn_all.items() if k in ('Wq', 'Wk', 'Wv', 'Wo')}
    del _L0_xattn_all

    def _L0_attn_setup():
        import jax, jax.numpy as jnp
        import numpy as np
        EPS = 1e-06

        def rmsnorm(x, w, eps=EPS):
            return x * jax.lax.rsqrt(jnp.mean(x * x, axis=-1, keepdims=True) + eps) * w

        def bitlinear(x, w, eps=EPS):
            xn = x * jax.lax.rsqrt(jnp.mean(x * x, axis=-1, keepdims=True) + eps)
            s = 127.0 / jnp.clip(jnp.max(jnp.abs(xn), axis=-1, keepdims=True), 1e-05, None)
            xq = xn + jax.lax.stop_gradient(jnp.clip(jnp.round(xn * s), -128.0, 127.0) / s - xn)
            ws = 1.0 / jnp.clip(jnp.mean(jnp.abs(w)), 1e-05, None)
            wq = w + jax.lax.stop_gradient(jnp.clip(jnp.round(w * ws), -1.0, 1.0) / ws - w)
            return xq @ wq.T

        def swish(x):
            return x * jax.nn.sigmoid(x)

        def hgrn_scan(i, f):
            B, L, D = i.shape

            def step(h, xf):
                i_t, f_t = xf
                h = f_t * h + i_t
                return (h, h)
            _, o = jax.lax.scan(step, jnp.zeros((B, D), i.dtype), (i.swapaxes(0, 1), f.swapaxes(0, 1)))
            return o.swapaxes(0, 1)
        B, L, H = (4, 2048, 512)
        I = 1408
        key = jax.random.key(seed)
        ks = jax.random.split(key, 12)
        w = lambda k, o, i_: jax.random.normal(k, (o, i_), jnp.float32) * 0.02
        return {'hidden_states': jax.random.normal(ks[0], (B, L, H), jnp.float32), 'lower_bound': jax.random.uniform(ks[1], (H,), jnp.float32), 'attn_norm_w': jnp.ones((H,), jnp.float32), 'w_i': w(ks[2], H, H), 'w_f': w(ks[3], H, H), 'w_g': w(ks[4], H, H), 'g_norm_w': jnp.ones((H,), jnp.float32), 'w_o': w(ks[5], H, H), 'mlp_norm_w': jnp.ones((H,), jnp.float32), 'w_gate': w(ks[6], 2 * I, H), 'w_down': w(ks[7], H, I)}
    _L0_attn_all = _L0_attn_setup()
    _L0_attn_in = {k: v for k, v in _L0_attn_all.items() if k in ('lower_bound', 'attn_norm_w', 'w_i', 'w_f', 'w_g', 'g_norm_w', 'w_o', 'mlp_norm_w', 'w_gate', 'w_down')}
    del _L0_attn_all

    def _L0_ffn_setup():
        import jax, jax.numpy as jnp
        import numpy as np
        TOP_K = 2

        def _moe(x, Wr, br, W1, b1, W2, b2):
            B, S, D = x.shape
            E = Wr.shape[1]
            xt = x.reshape(-1, D)
            logits = xt @ Wr + br
            top_vals, top_idx = jax.lax.top_k(logits, TOP_K)
            mask = jnp.zeros_like(logits, dtype=bool).at[jnp.arange(xt.shape[0])[:, None], top_idx].set(True)
            sparse_logits = jnp.where(mask, logits, -jnp.inf)
            gate = jax.nn.softmax(sparse_logits, axis=-1)
            h = jax.nn.relu(jnp.einsum('td,edh->teh', xt, W1) + b1)
            y = jnp.einsum('teh,ehd->ted', h, W2) + b2
            out = jnp.einsum('ted,te->td', y, gate)
            return out.reshape(B, S, D)
        key = jax.random.key(seed)
        ks = jax.random.split(key, 5)
        B, S, D, E, H = (2, 1024, 512, 8, 2048)
        scale = 1.0 / np.sqrt(D)
        return {'x': jax.random.normal(ks[0], (B, S, D), dtype=jnp.float32), 'Wr': jax.random.normal(ks[1], (D, E), dtype=jnp.float32) * scale, 'br': jnp.zeros((E,), dtype=jnp.float32), 'W1': jax.random.normal(ks[2], (E, D, H), dtype=jnp.float32) * scale, 'b1': jnp.zeros((E, H), dtype=jnp.float32), 'W2': jax.random.normal(ks[3], (E, H, D), dtype=jnp.float32) * (1.0 / np.sqrt(H)), 'b2': jnp.zeros((E, D), dtype=jnp.float32)}
    _L0_ffn_all = _L0_ffn_setup()
    _L0_ffn_in = {k: v for k, v in _L0_ffn_all.items() if k in ('Wr', 'br', 'W1', 'b1', 'W2', 'b2')}
    del _L0_ffn_all
    return {'x': x, 'ctx_1024': ctx_1024, 'fside_1x1xSxS2_0': fside_1x1xSxS2_0, 'L0_xattn_Wq': _L0_xattn_in['Wq'], 'L0_xattn_Wk': _L0_xattn_in['Wk'], 'L0_xattn_Wv': _L0_xattn_in['Wv'], 'L0_xattn_Wo': _L0_xattn_in['Wo'], 'L0_attn_lower_bound': _L0_attn_in['lower_bound'], 'L0_attn_attn_norm_w': _L0_attn_in['attn_norm_w'], 'L0_attn_w_i': _L0_attn_in['w_i'], 'L0_attn_w_f': _L0_attn_in['w_f'], 'L0_attn_w_g': _L0_attn_in['w_g'], 'L0_attn_g_norm_w': _L0_attn_in['g_norm_w'], 'L0_attn_w_o': _L0_attn_in['w_o'], 'L0_attn_mlp_norm_w': _L0_attn_in['mlp_norm_w'], 'L0_attn_w_gate': _L0_attn_in['w_gate'], 'L0_attn_w_down': _L0_attn_in['w_down'], 'L0_ffn_Wr': _L0_ffn_in['Wr'], 'L0_ffn_br': _L0_ffn_in['br'], 'L0_ffn_W1': _L0_ffn_in['W1'], 'L0_ffn_b1': _L0_ffn_in['b1'], 'L0_ffn_W2': _L0_ffn_in['W2'], 'L0_ffn_b2': _L0_ffn_in['b2']}

def reference(x, ctx_1024, fside_1x1xSxS2_0, L0_xattn_Wq, L0_xattn_Wk, L0_xattn_Wv, L0_xattn_Wo, L0_attn_lower_bound, L0_attn_attn_norm_w, L0_attn_w_i, L0_attn_w_f, L0_attn_w_g, L0_attn_g_norm_w, L0_attn_w_o, L0_attn_mlp_norm_w, L0_attn_w_gate, L0_attn_w_down, L0_ffn_Wr, L0_ffn_br, L0_ffn_W1, L0_ffn_b1, L0_ffn_W2, L0_ffn_b2):
    import jax
    import jax.numpy as jnp

    def _L0_xattn_ref(query_antecedent, memory_antecedent, bias, Wq, Wk, Wv, Wo):
        import jax, jax.numpy as jnp
        import numpy as np
        NUM_HEADS = 16
        KEY_DEPTH = 512

        def _split_heads(x, h):
            b, l, d = x.shape
            return x.reshape(b, l, h, d // h).transpose(0, 2, 1, 3)
        h = NUM_HEADS
        d_head = KEY_DEPTH // h
        q = _split_heads(query_antecedent @ Wq, h) * d_head ** (-0.5)
        k = _split_heads(memory_antecedent @ Wk, h)
        v = _split_heads(memory_antecedent @ Wv, h)
        logits = jnp.einsum('bhqd,bhkd->bhqk', q, k) + bias
        weights = jax.nn.softmax(logits, axis=-1)
        x = jnp.einsum('bhqk,bhkd->bhqd', weights, v)
        b, _, l, d = x.shape
        x = x.transpose(0, 2, 1, 3).reshape(b, l, h * d)
        return x @ Wo

    def _L0_attn_ref(hidden_states, lower_bound, attn_norm_w, w_i, w_f, w_g, g_norm_w, w_o, mlp_norm_w, w_gate, w_down):
        import jax, jax.numpy as jnp
        import numpy as np
        EPS = 1e-06

        def rmsnorm(x, w, eps=EPS):
            return x * jax.lax.rsqrt(jnp.mean(x * x, axis=-1, keepdims=True) + eps) * w

        def bitlinear(x, w, eps=EPS):
            xn = x * jax.lax.rsqrt(jnp.mean(x * x, axis=-1, keepdims=True) + eps)
            s = 127.0 / jnp.clip(jnp.max(jnp.abs(xn), axis=-1, keepdims=True), 1e-05, None)
            xq = xn + jax.lax.stop_gradient(jnp.clip(jnp.round(xn * s), -128.0, 127.0) / s - xn)
            ws = 1.0 / jnp.clip(jnp.mean(jnp.abs(w)), 1e-05, None)
            wq = w + jax.lax.stop_gradient(jnp.clip(jnp.round(w * ws), -1.0, 1.0) / ws - w)
            return xq @ wq.T

        def swish(x):
            return x * jax.nn.sigmoid(x)

        def hgrn_scan(i, f):
            B, L, D = i.shape

            def step(h, xf):
                i_t, f_t = xf
                h = f_t * h + i_t
                return (h, h)
            _, o = jax.lax.scan(step, jnp.zeros((B, D), i.dtype), (i.swapaxes(0, 1), f.swapaxes(0, 1)))
            return o.swapaxes(0, 1)
        B, L, H = (4, 2048, 512)
        I = 1408
        residual = hidden_states
        x = rmsnorm(hidden_states, attn_norm_w)
        i = bitlinear(x, w_i)
        f = jax.nn.sigmoid(bitlinear(x, w_f))
        f = lower_bound + (1.0 - lower_bound) * f
        i = swish(i) * (1.0 - f)
        o = hgrn_scan(i, f)
        g = bitlinear(x, w_g)
        o = rmsnorm(o, g_norm_w) * swish(g)
        o = bitlinear(o, w_o)
        residual = o + residual
        h = rmsnorm(residual, mlp_norm_w)
        y = bitlinear(h, w_gate)
        gate, y = jnp.split(y, 2, axis=-1)
        z = bitlinear(swish(gate) * y, w_down)
        return residual + z

    def _L0_ffn_ref(x, Wr, br, W1, b1, W2, b2):
        import jax, jax.numpy as jnp
        import numpy as np
        TOP_K = 2

        def _moe(x, Wr, br, W1, b1, W2, b2):
            B, S, D = x.shape
            E = Wr.shape[1]
            xt = x.reshape(-1, D)
            logits = xt @ Wr + br
            top_vals, top_idx = jax.lax.top_k(logits, TOP_K)
            mask = jnp.zeros_like(logits, dtype=bool).at[jnp.arange(xt.shape[0])[:, None], top_idx].set(True)
            sparse_logits = jnp.where(mask, logits, -jnp.inf)
            gate = jax.nn.softmax(sparse_logits, axis=-1)
            h = jax.nn.relu(jnp.einsum('td,edh->teh', xt, W1) + b1)
            y = jnp.einsum('teh,ehd->ted', h, W2) + b2
            out = jnp.einsum('ted,te->td', y, gate)
            return out.reshape(B, S, D)
        return _moe(x, Wr, br, W1, b1, W2, b2)
    x = x + _L0_xattn_ref(_layernorm(x, axis=-1), ctx_1024, fside_1x1xSxS2_0, L0_xattn_Wq, L0_xattn_Wk, L0_xattn_Wv, L0_xattn_Wo)
    x = x + _L0_attn_ref(_layernorm(x, axis=-1), L0_attn_lower_bound, L0_attn_attn_norm_w, L0_attn_w_i, L0_attn_w_f, L0_attn_w_g, L0_attn_g_norm_w, L0_attn_w_o, L0_attn_mlp_norm_w, L0_attn_w_gate, L0_attn_w_down)
    x = x + _L0_ffn_ref(_layernorm(x, axis=-1), L0_ffn_Wr, L0_ffn_br, L0_ffn_W1, L0_ffn_b1, L0_ffn_W2, L0_ffn_b2)
    return x

_drawn_inputs = setup_inputs


def setup_inputs(seed=0):
    import zlib

    import numpy as np

    out = dict(_drawn_inputs(seed))
    spreads = {'L0_attn_attn_norm_w': (1.0, 0.2),
     'L0_attn_g_norm_w': (1.0, 0.2),
     'L0_attn_mlp_norm_w': (1.0, 0.2),
     'L0_ffn_br': (0.0, 0.1),
     'L0_ffn_b1': (0.0, 0.35),
     'L0_ffn_b2': (0.0, 0.1)}
    factors = {}
    for name, (base, spread) in spreads.items():
        noise = np.random.default_rng([zlib.crc32(name.encode()), seed]).standard_normal(out[name].shape)
        drawn = base * np.exp(spread * noise) if base else spread * noise
        out[name] = jnp.asarray(drawn.astype(out[name].dtype))
    for name, factor in factors.items():
        out[name] = (out[name] * factor).astype(out[name].dtype)
    return out
```

```python
from contextlib import ExitStack

import concourse.bass as bass
from concourse import mybir

F32 = mybir.dt.float32
F32R = mybir.dt.float32r
BF16 = mybir.dt.bfloat16
I32 = mybir.dt.int32
U32 = mybir.dt.uint32
ALU = mybir.AluOpType
ACT = mybir.ActivationFunctionType
AX = mybir.AxisListType

P = 128
B = 4
D = 512
DT = D // P
KEYS = 2048
HEADS = 16
DH = D // HEADS
QUAD = P // DH
CHUNK = 512
KTILES = KEYS // P
INNER = 1408
IT = INNER // P
CHUNKS = KEYS // CHUNK
BANK = 512
EXPERTS = 8
HID = 2048
HT = HID // P
SLOTS = 192
ROUNDS = -(-B * P // SLOTS)
ROUND_MAGIC = 1.5 * 2.0 ** 23
LOWEST = -3.0e38


class Signal:

    def __init__(self, sem):
        self.sem = sem
        self.count = 0


class Queue:

    def __init__(self, done):
        self.done = done
        self.steps = []
        self.waited = {}
        self.branch = self.join = None

    def wait(self, *marks):
        for mark in marks:
            if mark is None:
                continue
            if isinstance(mark, list):
                self.wait(*mark)
                continue
            signal, count = mark
            if self.waited.get(id(signal), 0) < count:
                self.waited[id(signal)] = count
                self.steps.append((None, (signal, count), None, None, 0))

    def quiet(self, method, *args, **named):
        self.steps.append((method, args, named, None, 0))

    def op(self, method, *args, **named):
        self.steps.append((method, args, named, self.done, 1))
        self.done.count += 1
        return (self.done, self.done.count)

    def dma(self, signal, method, *args, **named):
        self.steps.append((method, args, named, signal, 16))
        signal.count += 16
        return (signal, signal.count)

    def last(self):
        return (self.done, self.done.count) if self.done.count else None

    def emit(self, engine, steps):
        for method, args, named, signal, by in steps:
            if method is None:
                engine.wait_ge(args[0].sem, args[1])
                continue
            made = method(*args, **named)
            if signal is not None:
                made.then_inc(signal.sem, by)

    def replay(self, engine, load):
        self.emit(engine, self.steps[:self.branch])
        with engine.register("fullest") as fullest:
            engine.reg_load(fullest, load)
            with engine.If_cmp(fullest, SLOTS, "IS_GT"):
                self.emit(engine, self.steps[self.branch:self.join])
        self.emit(engine, self.steps[self.join:])


def perceiver_block(nc, a, out, debug=None):
    with ExitStack() as life:
        def sb(name, shape, dt, stack=life):
            return stack.enter_context(nc.sbuf_tensor(name, shape, dt))

        def signal(name):
            return Signal(life.enter_context(nc.semaphore(name)))

        pe, dve, act, pool, sp = nc.tensor, nc.vector, nc.scalar, nc.gpsimd, nc.sync
        T = Queue(signal("tensor_done"))
        V = Queue(signal("vector_done"))
        A = Queue(signal("scalar_done"))
        G = Queue(signal("gpsimd_done"))
        S = Queue(signal("sync_done"))

        psum = life.enter_context(nc.psum_tensor("psum", [P, 8, BANK], F32))

        ident = sb("ident", [P, P], F32)
        identb = sb("identb", [P, P], BF16)
        region_q = ExitStack()
        qT = sb("qT", [P, DT, B * P], F32, region_q)
        region_q.close()
        x1 = sb("x1", [P, B, D], F32)
        stats = sb("stats", [P, B, 6], F32)
        meanvar = sb("meanvar", [P, B, 2], F32)
        minus_half = sb("minus_half", [P, B], F32)
        ones = sb("ones", [P, P], F32)
        magic = sb("magic", [P, 1], F32)
        col = sb("col", [P, 64, B], F32)
        names = {}

        def scalars(name):
            names.setdefault(name, len(names))
            assert len(names) <= 64
            return col[:, names[name], :]

        m = G.op(pool.memset, ident[:, :], 0.0)
        G.wait(m)
        m = G.op(pool.affine_select, out=ident[:, :], in_=ident[:, :], compare_op=ALU.not_equal, fill=1.0, base=0,
                 pattern=[[-1, P]], channel_multiplier=1)
        G.wait(m)
        m = G.op(pool.tensor_copy, identb[:, :], ident[:, :])
        G.op(pool.memset, ones[:, :], 1.0)
        G.op(pool.memset, magic[:, :], ROUND_MAGIC)
        constants = G.op(pool.memset, minus_half[:, :], -0.5)

        def rsqrt_cols(dst, src, scale, eps, after):
            G.wait(after, constants)
            m = G.op(pool.tensor_scalar, dst, src, scale, eps, ALU.mult, ALU.add)
            G.wait(m)
            return G.op(pool.tensor_tensor, dst, dst, minus_half[:, :], ALU.pow)

        def layernorm(dst, src, key, after):
            rstd = scalars(key)
            m = None
            for b in range(B):
                V.wait(after[b], V.last())
                m = V.op(dve.bn_stats, stats[:, b, :], src[:, b, :])
                V.wait(m)
                m = V.op(dve.bn_aggr, meanvar[:, b, :], stats[:, b, :])
            m = rsqrt_cols(rstd, meanvar[:, :, 1], 1.0, 1e-5, m)
            V.wait(m)
            return [V.op(dve.tensor_scalar, dst[:, b, :], src[:, b, :], meanvar[:, b, 0:1], rstd[:, b:b + 1],
                         ALU.subtract, ALU.mult) for b in range(B)]

        def transpose_tile(dst, src, bank, after, bank_free, copier):
            T.wait(after, bank_free, constants)
            for k in range(DT):
                m = T.op(pe.transpose, psum[:, bank, k * P:(k + 1) * P], src[:, k * P:(k + 1) * P], ident[:, :])
            copied = psum[:, bank, :].rearrange("p (k t) -> p k t", k=DT)
            copier.wait(m)
            if copier is A:
                return A.op(act.copy, dst, copied)
            return V.op(dve.tensor_copy, dst, copied)

        region_f, region_r = ExitStack(), ExitStack()
        region_bytes_f = 72 * 1024
        ctx_raw = sb("ctx_raw", [P, DT, CHUNK], F32, region_f)
        ctx_hi = sb("ctx_hi", [P, 2, DT, CHUNK], F32R, region_f)
        ctx_lo = sb("ctx_lo", [P, 2, DT, CHUNK], F32R, region_f)
        wk_hi = sb("wk_hi", [P, DT, D], F32R, region_f)
        wk_lo = sb("wk_lo", [P, DT, D], F32R, region_f)
        wv_hi = sb("wv_hi", [P, DT, D], F32R, region_f)
        wv_lo = sb("wv_lo", [P, DT, D], F32R, region_f)
        region_f.close()
        region_f2 = ExitStack()
        gate_raw = sb("gate_raw", [P, DT, 2 * INNER], F32, region_f2)
        ifg_raw = sb("ifg_raw", [P, 3, DT, D], F32, region_f2)
        region_f2.close()
        WSLOTS = 4
        wslot = [sb(f"wslot{i}", [P, DT * HID], F32) for i in range(2)]
        sb("rest_f", [P, region_bytes_f // 4 - 2 * DT * HID], F32)

        PS = 6
        kT = sb("kT", [P, DT, KEYS], F32, region_r)
        v = sb("v", [P, KTILES, D], F32, region_r)
        prob = sb("prob", [P, PS, KEYS], F32, region_r)
        biasmap = sb("biasmap", [P, KEYS], F32, region_r)
        oT = sb("oT", [P, DT, B * P], F32, region_r)
        qpad = sb("qpad", [P, 2, QUAD, P], F32, region_r)
        PTS = 3
        probT = sb("probT", [P, PTS, QUAD * P], F32, region_r)
        top = sb("top", [P, HEADS, 4], F32, region_r)
        rinv = sb("rinv", [P, 2, QUAD], F32, region_r)
        rbc = sb("rbc", [P, 2, P], F32, region_r)
        rT = sb("rT", [P, 2, P], F32, region_r)
        region_r.close()

        view = lambda slot: prob[:, slot, :].rearrange("p (k n) -> p k n", k=DT)
        wq_sb, wk_sb, wv_sb, xhT, x_in = (view(s) for s in range(5))
        rows = lambda w: w.rearrange("(k p) n -> p k n", p=P)

        s_x, s_wq, s_wk, s_wv, s_bias, s_ctx = (signal(n) for n in
                                                ("x_in", "wq_in", "wk_in", "wv_in", "bias_in", "ctx_in"))
        wk_loaded = S.dma(s_wk, sp.dma_start, wk_sb, rows(a["wk"]))

        def load_ctx(b, c, free):
            S.wait(free)
            return S.dma(s_ctx, sp.dma_start, ctx_raw[:, :, :],
                         a["ctx_t"][b].rearrange("(k p) n -> p k n", p=P)[:, :, c * CHUNK:(c + 1) * CHUNK])

        ctx_loaded = load_ctx(0, 0, None)
        wv_loaded = S.dma(s_wv, sp.dma_start, wv_sb, rows(a["wv"]))
        wq_loaded = S.dma(s_wq, sp.dma_start, wq_sb, rows(a["wq"]))
        x_loaded = S.dma(s_x, sp.dma_start, x_in, a["x"].rearrange("b s d -> s b d"))
        bias_loaded = S.dma(s_bias, sp.dma_start, biasmap[:, :], a["bias"])

        def split(hi, lo, raw, after):
            V.wait(after)
            m = V.op(dve.tensor_copy, hi, raw)
            V.wait(m)
            return V.op(dve.tensor_tensor, lo, raw, hi.bitcast(F32), ALU.subtract)

        wk_split = split(wk_hi[:, :, :], wk_lo[:, :, :], wk_sb, wk_loaded)
        g_zero = G.op(pool.memset, qpad[:, :, :, :], 0.0)

        WORK = (4, 5, 6)
        OUT_BANK = 7
        work_free = {w: None for w in WORK}
        turn = [0]

        def next_bank():
            w = WORK[turn[0] % len(WORK)]
            turn[0] += 1
            return w

        kT_read = [None] * DT
        v_read = [None] * KTILES
        ctx_read = [None, None]
        kT_ready = {}
        v_ready = {}

        def project_keys(c, half, ready, tiles=range(DT)):
            for m in tiles:
                w = next_bank()
                T.wait(work_free[w], ready, wk_split)
                for k in range(DT):
                    wh, wl = wk_hi[:, k, m * P:(m + 1) * P], wk_lo[:, k, m * P:(m + 1) * P]
                    T.quiet(pe.matmul, psum[:, w, :], wh, ctx_hi[:, half, k, :], start=(k == 0), stop=False)
                    T.quiet(pe.matmul, psum[:, w, :], wh, ctx_lo[:, half, k, :], start=False, stop=False)
                    done = T.op(pe.matmul, psum[:, w, :], wl, ctx_hi[:, half, k, :], start=False, stop=(k == DT - 1))
                A.wait(done, kT_read[m])
                kT_ready[m, c] = work_free[w] = A.op(act.copy, kT[:, m, c * CHUNK:(c + 1) * CHUNK], psum[:, w, :])

        def project_values(c, half):
            for t in range(CHUNK // P):
                w, kt = next_bank(), c * (CHUNK // P) + t
                T.wait(work_free[w], wv_split)
                for k in range(DT):
                    ch, cl = ctx_hi[:, half, k, t * P:(t + 1) * P], ctx_lo[:, half, k, t * P:(t + 1) * P]
                    T.quiet(pe.matmul, psum[:, w, :], ch, wv_hi[:, k, :], start=(k == 0), stop=False)
                    T.quiet(pe.matmul, psum[:, w, :], ch, wv_lo[:, k, :], start=False, stop=False)
                    done = T.op(pe.matmul, psum[:, w, :], cl, wv_hi[:, k, :], start=False, stop=(k == DT - 1))
                V.wait(done, v_read[kt])
                v_ready[kt] = work_free[w] = V.op(dve.tensor_copy, v[:, kt, :], psum[:, w, :])
            return done

        slot_free = [None] * PS
        s_free = [None, None]
        qpad_read = [None, None]
        out_read = [None, None]
        head_count = [0]
        unit = [0]

        def load_queries(n, b, g):
            G.wait(g_zero, q_ready[g], qpad_read[n % 2])
            for j in range(QUAD):
                rows_j = slice(j * DH, (j + 1) * DH)
                m = G.op(pool.tensor_copy, qpad[rows_j, n % 2, j, :], qT[rows_j, g, b * P:(b + 1) * P])
            return m

        def scores(n, b, g, j, queries):
            h, slot = QUAD * g + j, head_count[0] % PS
            head_count[0] += 1
            V.wait(slot_free[slot], bias_loaded)
            m = None
            for half in range(2):
                u = unit[0] % 2
                unit[0] += 1
                T.wait(queries, s_free[u])
                for c in range(2):
                    chunk = 2 * half + c
                    T.wait(kT_ready[g, chunk])
                    done = T.op(pe.matmul, psum[:, 2 * u + c, :], qpad[:, n % 2, j, :],
                                kT[:, g, chunk * CHUNK:(chunk + 1) * CHUNK], start=True, stop=True)
                keys = slice(half * 2 * CHUNK, (half + 1) * 2 * CHUNK)
                V.wait(done, m)
                m = s_free[u] = V.op(
                    dve.tensor_tensor_reduce, prob[:, slot, keys],
                    psum[:, 2 * u:2 * u + 2, :].rearrange("p a n -> p (a n)"), biasmap[:, keys], 1.0,
                    top[:, h, 0:1] if half else LOWEST, ALU.add, ALU.max, top[:, h, half:half + 1])
            kT_read[g] = qpad_read[n % 2] = done
            V.wait(m)
            m = V.op(dve.tensor_scalar, top[:, h, 2:3], top[:, h, 1:2], -1.0, None, ALU.mult)
            A.wait(m, sums_read.get(h))
            m = A.op(act.activation, prob[:, slot, :], prob[:, slot, :], ACT.Exp, bias=top[:, h, 2:3], scale=1.0,
                     accum_out=top[:, h, 3:4])
            return slot, m

        probT_read = [None] * PTS
        sums_read = {}

        def weighted_values(n, b, g, heads):
            half = n % 2
            outp = psum[:, OUT_BANK, half * P:(half + 1) * P]
            moved = {}

            def turn_tile(kt):
                w, r = next_bank(), kt % PTS
                T.wait(work_free[w], [m for _, m in heads])
                for j, (slot, _) in enumerate(heads):
                    done = T.op(pe.transpose, psum[:, w, j * P:(j + 1) * P], prob[:, slot, kt * P:(kt + 1) * P],
                                ident[:, :])
                if kt == KTILES - 1:
                    for slot, _ in heads:
                        slot_free[slot] = done
                q = V if kt % 16 in (1, 3, 5, 8, 10, 12, 14) else A
                q.wait(done, probT_read[r])
                if q is A:
                    work_free[w] = A.op(act.copy, probT[:, r, :], psum[:, w, :])
                else:
                    work_free[w] = V.op(dve.tensor_copy, probT[:, r, :], psum[:, w, :])
                moved[kt] = work_free[w]

            def multiply(kt):
                r = kt % PTS
                T.wait(moved[kt], v_ready[kt], out_read[half] if kt == 0 else None)
                for j in range(QUAD):
                    cols = slice((QUAD * g + j) * DH, (QUAD * g + j + 1) * DH)
                    done = T.op(pe.matmul, outp[j * DH:(j + 1) * DH, :], v[:, kt, cols],
                                probT[:, r, j * P:(j + 1) * P], start=(kt == 0), stop=(kt == KTILES - 1),
                                tile_position=(0, j * DH))
                v_read[kt] = probT_read[r] = done
                return done

            for kt in range(KTILES + 2):
                if kt < KTILES:
                    turn_tile(kt)
                if kt >= 2:
                    product = multiply(kt - 2)
            V.wait(heads[-1][1], rinv_read[half])
            m = V.op(dve.reciprocal, rinv[:, half, :], top[:, QUAD * g:QUAD * (g + 1), 3])
            for h in range(QUAD * g, QUAD * (g + 1)):
                sums_read[h] = m
            V.wait(m, rbc_read[half])
            m = V.op(dve.tensor_copy, rbc[:, half, :].rearrange("p (j d) -> p j d", j=QUAD),
                     rinv[:, half, :].rearrange("p (j d) -> p j d", d=1).broadcast_to([P, QUAD, DH]))
            rinv_read[half] = m
            w = next_bank()
            T.wait(m, work_free[w])
            m = rbc_read[half] = T.op(pe.transpose, psum[:, w, 0:P], rbc[:, half, :], ident[:, :])
            A.wait(m, rT_read[half])
            m = work_free[w] = A.op(act.copy, rT[:, half, :], psum[:, w, 0:P])
            V.wait(m, product)
            m = rT_read[half] = out_read[half] = V.op(dve.tensor_tensor, oT[:, g, b * P:(b + 1) * P], outp,
                                                      rT[:, half, :], ALU.mult)
            oT_ready[g, b] = m

        rinv_read, rbc_read, rT_read = [None] * 2, [None] * 2, [None] * 2
        oT_ready = {}
        q_ready = {}

        def split_chunk(number):
            nonlocal ctx_loaded
            half = number % 2
            V.wait(ctx_read[half])
            ready = split(ctx_hi[:, half, :, :], ctx_lo[:, half, :, :], ctx_raw[:, :, :], ctx_loaded)
            if number + 1 < B * CHUNKS:
                ctx_loaded = load_ctx((number + 1) // CHUNKS, (number + 1) % CHUNKS, ready)
            return ready

        pending = None
        n = 0
        chunk_ready = {0: split_chunk(0)}
        wv_split = split(wv_hi[:, :, :], wv_lo[:, :, :], wv_sb, wv_loaded)
        for b in range(B):
            for c in range(CHUNKS):
                number = b * CHUNKS + c
                half = number % 2
                project_keys(c, half, chunk_ready[number])
                if c == 0 and pending:
                    weighted_values(*pending)
                    pending = None
                if number + 1 < B * CHUNKS:
                    chunk_ready[number + 1] = split_chunk(number + 1)
                ctx_read[half] = project_values(c, half)
                if b == 0 and c == 1:
                    normed = layernorm(x_in, x_in, "rstd0", [x_loaded] * B)
                    for t in range(B):
                        w = next_bank()
                        m = work_free[w] = transpose_tile(xhT[:, :, t * P:(t + 1) * P], x_in[:, t, :], w, normed[t],
                                                          work_free[w], A)
                    for g in range(DT):
                        w = next_bank()
                        T.wait(m, wq_loaded, work_free[w])
                        for k in range(DT):
                            done = T.op(pe.matmul, psum[:, w, :], wq_sb[:, k, g * P:(g + 1) * P], xhT[:, k, :],
                                        start=(k == 0), stop=(k == DT - 1))
                        A.wait(done)
                        q_ready[g] = work_free[w] = A.op(act.activation, qT[:, g, :], psum[:, w, :], ACT.Copy,
                                                         scale=float(DH) ** -0.5)
                    slot_free = [[q_ready[DT - 1], done, normed[-1], wv_split]] * PS
            for g in range(DT):
                queries = load_queries(n, b, g)
                heads = [scores(n, b, g, j, queries) for j in range(2)]
                if pending:
                    weighted_values(*pending)
                heads += [scores(n, b, g, j, queries) for j in range(2, QUAD)]
                pending = (n, b, g, heads)
                n += 1
        s_gate, s_ifg = signal("gate_raw_in"), signal("ifg_raw_in")
        S.wait(ctx_read[0], ctx_read[1])
        for n_, key in enumerate(("w_i_t", "w_f_t", "w_g_t")):
            ifg_loaded = S.dma(s_ifg, sp.dma_start, ifg_raw[:, n_], rows(a[key]))
        gate_loaded = S.dma(s_gate, sp.dma_start, gate_raw[:, :, :], rows(a["w_gate_t"]))
        weighted_values(*pending)

        wo_sb, x_again = view(0), view(1)
        s_wo = signal("wo_in")
        S.wait(slot_free[0], slot_free[1])
        wo_loaded = S.dma(s_wo, sp.dma_start, wo_sb, rows(a["wo"]))
        x_loaded = S.dma(s_x, sp.dma_start, x_again, a["x"].rearrange("b s d -> s b d"))
        x1_ready = []
        for b in range(B):
            w = next_bank()
            T.wait(work_free[w], wo_loaded)
            for g in range(DT):
                T.wait(oT_ready[g, b])
                done = T.op(pe.matmul, psum[:, w, :], oT[:, g, b * P:(b + 1) * P], wo_sb[:, g, :],
                            start=(g == 0), stop=(g == DT - 1))
            V.wait(done, x_loaded, queries)
            m = work_free[w] = V.op(dve.tensor_tensor, x1[:, b, :], psum[:, w, :], x_again[:, b, :], ALU.add)
            x1_ready.append(m)
        attention_over = [q.last() for q in (T, V, A, G)]


        region_2 = ExitStack()
        MATS = ("i", "f", "g", "o", "gate", "down")
        NUMEL = {"i": D * D, "f": D * D, "g": D * D, "o": D * D, "gate": 2 * INNER * D, "down": INNER * D}
        tern = {n: sb("tern_" + n, [P, DT, D], BF16, region_2) for n in ("i", "f", "g", "o")}
        tern["gate"] = sb("tern_gate", [P, DT, 2 * INNER], BF16, region_2)
        tern["down"] = sb("tern_down", [P, IT, D], BF16, region_2)
        region_raw = ExitStack()
        o_raw = sb("o_raw", [P, DT, D], F32, region_raw)
        down_raw = sb("down_raw", [P, IT, D], F32, region_raw)
        region_raw.close()
        z_int = sb("z_int", [P, B, INNER], BF16, region_2)
        z_intT = sb("z_intT", [P, IT, B * P], BF16, region_2)
        sb("pad_raw", [P, 4 * (DT * D + IT * D) - 2 * (B * INNER + IT * B * P)], mybir.dt.uint8, region_2)
        resid = sb("resid", [P, B, D], F32, region_2)
        work = sb("work", [P, B, D], F32, region_2)
        q_int = sb("q_int", [P, B, D], BF16, region_2)
        q_intT = sb("q_intT", [P, DT, B * P], BF16, region_2)
        step_row = sb("step_row", [P, B * P], F32, region_2)
        scan = sb("scan", [P, 3, DT, B * P], F32, region_2)
        swish_g = scan[:, 0]
        junk = sb("junk", [P, INNER], BF16, region_2)
        spread = sb("spread", [P, P], F32, region_2)
        gains = sb("gains", [P, 3, D], F32, region_2)
        lower = sb("lower", [P, 3, DT], F32, region_2)
        wsum = sb("wsum", [P, len(MATS), 4], F32, region_2)
        wmean = sb("wmean", [P, 2, len(MATS)], F32, region_2)
        tok = sb("tok", [P, 6, B], F32, region_2)

        G.wait(*attention_over)
        V.wait(constants, *attention_over)
        A.wait(constants, *attention_over)
        S.wait(*attention_over)
        s_small, s_oraw, s_draw = signal("small_in"), signal("o_raw_in"), signal("down_raw_in")
        o_loaded = S.dma(s_oraw, sp.dma_start, o_raw[:, :, :], rows(a["w_o_t"]))
        down_loaded = S.dma(s_draw, sp.dma_start, down_raw[:, :, :], rows(a["w_down_t"]))
        for n_, key in enumerate(("attn_norm", "g_norm", "mlp_norm")):
            small = S.dma(s_small, sp.dma_start, gains[:, n_, :],
                          a[key].rearrange("(o d) -> o d", o=1).broadcast_to([P, D]))
        small = S.dma(s_small, sp.dma_start, lower[:, 0, :], a["lower"])

        raw = {"i": ifg_raw[:, 0], "f": ifg_raw[:, 1], "g": ifg_raw[:, 2], "o": o_raw[:, :, :],
               "gate": gate_raw[:, :, :], "down": down_raw[:, :, :]}
        raw_loaded = {"i": ifg_loaded, "f": ifg_loaded, "g": ifg_loaded, "gate": gate_loaded, "o": o_loaded,
                      "down": down_loaded}

        bank_free = [attention_over] * 8
        bank_turn = [0]

        def bank():
            bank_turn[0] += 1
            return bank_turn[0] % 8

        def abs_sums(mats):
            for n in mats:
                V.wait(raw_loaded[n])
                m = V.op(dve.tensor_reduce, wsum[:, MATS.index(n), 0:1], raw[n], AX.XY, ALU.add,
                         apply_absolute_value=True)
            return m

        def mean_abs(lo, hi, after):
            w = bank()
            T.wait(after, bank_free[w])
            m = T.op(pe.matmul, psum[:, w, lo:hi], ones[:, :], wsum[:, lo:hi, 0], start=True, stop=True)
            V.wait(m)
            for i in range(lo, hi):
                m = bank_free[w] = V.op(dve.tensor_scalar, wmean[:, 0, i:i + 1], psum[:, w, i:i + 1],
                                        1.0 / NUMEL[MATS[i]], 1e-5, ALU.mult, ALU.max)
            V.wait(m)
            return V.op(dve.reciprocal, wmean[:, 1, lo:hi], wmean[:, 0, lo:hi])

        def ternary(n, after, pieces=1):
            i = MATS.index(n)
            flat = lambda t: t.rearrange("p k n -> p (k n)")
            src, dst = flat(raw[n]), flat(tern[n][:, :, :])
            size = src.shape[1] // pieces
            for c in range(pieces):
                part = slice(c * size, (c + 1) * size)
                A.wait(after)
                m = A.op(act.activation, src[:, part], src[:, part], ACT.Identity, bias=magic[:, 0:1],
                         scale=wmean[:, 1, i:i + 1])
                V.wait(m)
                m = V.op(dve.tensor_scalar, dst[:, part], src[:, part], ROUND_MAGIC, 1.0, ALU.subtract, ALU.min)
                V.wait(m)
                m = V.op(dve.tensor_scalar, dst[:, part], dst[:, part], -1.0, None, ALU.max)
            return m

        def squares(key, src, width, marks):
            for b in range(B):
                A.wait(marks[b], A.last())
                m = A.op(act.activation, junk[:, 0:width], src(b), ACT.Square,
                         accum_out=scalars(key)[:, b:b + 1])
            return rsqrt_cols(scalars(key), scalars(key), 1.0 / width, 1e-6, m), m

        def quantize(key, src, dst, width, marks):
            rn, _ = squares(key + "_rn", src, width, marks)
            peak, quantum, factor = scalars(key + "_peak"), scalars(key + "_quantum"), scalars(key + "_factor")
            for b in range(B):
                V.wait(marks[b])
                m = V.op(dve.tensor_reduce, peak[:, b:b + 1], src(b), AX.X, ALU.max, apply_absolute_value=True)
            V.wait(m, rn)
            m = V.op(dve.tensor_tensor, peak, peak, scalars(key + "_rn"), ALU.mult)
            V.wait(m)
            step = m = V.op(dve.tensor_scalar, quantum, peak, 1e-5, 1.0 / 127.0, ALU.max, ALU.mult)
            V.wait(m)
            m = V.op(dve.reciprocal, factor, quantum)
            V.wait(m)
            m = V.op(dve.tensor_tensor, factor, factor, scalars(key + "_rn"), ALU.mult)
            out_marks = []
            for b in range(B):
                A.wait(m)
                m2 = A.op(act.activation, src(b), src(b), ACT.Identity, bias=magic[:, 0:1], scale=factor[:, b:b + 1])
                V.wait(m2)
                out_marks.append(V.op(dve.tensor_scalar, dst(b), src(b), ROUND_MAGIC, 127.0, ALU.subtract, ALU.min))
            return out_marks, quantum, step

        def turn_integers(dst, src, tiles, marks):
            done = []
            for b in range(B):
                for k0 in range(0, tiles, 4):
                    ks = range(k0, min(k0 + 4, tiles))
                    w = bank()
                    T.wait(marks[b], bank_free[w], constants)
                    half = psum[:, w, :].bitcast(BF16)
                    for k in ks:
                        m = T.op(pe.transpose, half[:, (k - k0) * P:(k - k0 + 1) * P], src(b)[:, k * P:(k + 1) * P],
                                 identb[:, :])
                    q = V if (b + k0 // 4) % 2 else A
                    q.wait(m)
                    args = (dst[:, k0:ks[-1] + 1, b * P:(b + 1) * P],
                            half[:, 0:len(ks) * P].rearrange("p (k t) -> p k t", t=P))
                    m = bank_free[w] = (V.op(dve.tensor_copy, *args) if q is V else A.op(act.copy, *args))
                done.append(m)
            return [[V.last(), A.last()]] * B

        def token_scale(i, quantum, mat, after):
            V.wait(after)
            k = MATS.index(mat)
            return V.op(dve.tensor_scalar, tok[:, i, :], quantum, wmean[:, 0, k:k + 1], None, ALU.mult)

        wsum_ready = mean_abs(0, 3, abs_sums(("i", "f", "g")))
        tern_ready = {n: ternary(n, wsum_ready) for n in ("i", "f")}
        resid_ready = layernorm(resid, x1, "rstd1", x1_ready)
        rr, _ = squares("rr", lambda b: resid[:, b, :], D, resid_ready)
        V.wait(rr, small)
        ready = [V.op(dve.scalar_tensor_tensor, work[:, b, :], resid[:, b, :], scalars("rr")[:, b:b + 1],
                      gains[:, 0, :], ALU.mult, ALU.mult) for b in range(B)]
        ready, quantum, step = quantize("qa", lambda b: work[:, b, :], lambda b: q_int[:, b, :], D, ready)
        turned = turn_integers(q_intT, lambda b: q_int[:, b, :], DT, ready)

        w = bank()
        for b in range(B):
            V.wait(step, V.last(), T.last())
            m = V.op(dve.tensor_copy, spread[:, :], quantum[:, b:b + 1].broadcast_to([P, P]))
            T.wait(m, bank_free[w])
            m = T.op(pe.transpose, psum[:, w, b * P:(b + 1) * P], spread[:, :], ident[:, :])
        A.wait(m)
        row_ready = bank_free[w] = A.op(act.copy, step_row[:, :], psum[:, w, :])
        tern_ready["g"] = ternary("g", wsum_ready)
        m = V.op(dve.tensor_scalar, lower[:, 1, :], lower[:, 0, :], -1.0, 1.0, ALU.mult, ALU.add)
        lower_ready = m

        state_ready = []
        for c in range(DT):
            raws = {}
            for n, place in (("f", 1), ("i", 0)):
                w = bank()
                T.wait(turned[0], tern_ready[n], bank_free[w])
                for k in range(DT):
                    m = T.op(pe.matmul, psum[:, w, :], tern[n][:, k, c * P:(c + 1) * P], q_intT[:, k, :],
                             start=(k == 0), stop=(k == DT - 1))
                V.wait(m, row_ready)
                raws[n] = bank_free[w] = V.op(
                    dve.scalar_tensor_tensor, scan[:, place, c, :], psum[:, w, :],
                    wmean[:, 0, MATS.index(n):MATS.index(n) + 1], step_row[:, :], ALU.mult, ALU.mult)
            A.wait(raws["f"])
            f = A.op(act.activation, scan[:, 1, c, :], scan[:, 1, c, :], ACT.Sigmoid)
            A.wait(raws["i"])
            si = A.op(act.activation, scan[:, 2, c, :], scan[:, 0, c, :], ACT.Sigmoid)
            V.wait(f, lower_ready)
            f = V.op(dve.tensor_scalar, scan[:, 1, c, :], scan[:, 1, c, :], lower[:, 1, c:c + 1],
                     lower[:, 0, c:c + 1], ALU.mult, ALU.add)
            V.wait(si)
            m = V.op(dve.tensor_tensor, scan[:, 0, c, :], scan[:, 0, c, :], scan[:, 2, c, :], ALU.mult)
            V.wait(f, m)
            m = V.op(dve.scalar_tensor_tensor, scan[:, 0, c, :], scan[:, 1, c, :], 1.0, scan[:, 0, c, :],
                     ALU.subtract, ALU.mult, reverse0=True)
            V.wait(m)
            for b in range(B):
                span = slice(b * P, (b + 1) * P)
                m = V.op(dve.tensor_tensor_scan, scan[:, 2, c, span], scan[:, 1, c, span], scan[:, 0, c, span], 0.0,
                         ALU.mult, ALU.add)
            state_ready.append(m)

        g_scaled = token_scale(0, quantum, "g", step)
        for b in range(B):
            w = bank()
            T.wait(turned[b], tern_ready["g"], bank_free[w])
            for k in range(DT):
                m = T.op(pe.matmul, psum[:, w, :], q_intT[:, k, b * P:(b + 1) * P], tern["g"][:, k, :],
                         start=(k == 0), stop=(k == DT - 1))
            A.wait(m, g_scaled, state_ready)
            m = A.op(act.activation, swish_g[:, b, :], psum[:, w, :], ACT.Sigmoid, scale=tok[:, 0, b:b + 1])
            V.wait(m)
            g_ready = bank_free[w] = V.op(dve.scalar_tensor_tensor, swish_g[:, b, :], psum[:, w, :],
                                          tok[:, 0, b:b + 1], swish_g[:, b, :], ALU.mult, ALU.mult)

        state_bank = [bank() for _ in range(B)]
        for b in range(B):
            T.wait(state_ready, bank_free[state_bank[b]])
            for c in range(DT):
                m = T.op(pe.transpose, psum[:, state_bank[b], c * P:(c + 1) * P], scan[:, 2, c, b * P:(b + 1) * P],
                         ident[:, :])
            state_ready[b] = m
        ro, squared = squares("ro", lambda b: psum[:, state_bank[b], :], D, state_ready)
        V.wait(ro, g_ready)
        ready = []
        for b in range(B):
            m = bank_free[state_bank[b]] = V.op(dve.scalar_tensor_tensor, work[:, b, :], psum[:, state_bank[b], :],
                                                scalars("ro")[:, b:b + 1], gains[:, 1, :], ALU.mult, ALU.mult)
            V.wait(m)
            ready.append(V.op(dve.tensor_tensor, work[:, b, :], work[:, b, :], swish_g[:, b, :], ALU.mult))
        wsum_ready = mean_abs(3, 6, abs_sums(("o", "gate", "down")))
        tern_ready["o"] = ternary("o", wsum_ready)
        ready, quantum, step = quantize("qo", lambda b: work[:, b, :], lambda b: q_int[:, b, :], D, ready)
        turned = turn_integers(q_intT, lambda b: q_int[:, b, :], DT, ready)
        o_scaled = token_scale(1, quantum, "o", step)

        def ternary_product(mat, srcT, tiles, scaled, i, marks):
            out_marks = []
            for b in range(B):
                w = bank()
                T.wait(marks[b], tern_ready[mat], bank_free[w])
                for k in range(tiles):
                    m = T.op(pe.matmul, psum[:, w, :], srcT[:, k, b * P:(b + 1) * P], tern[mat][:, k, :],
                             start=(k == 0), stop=(k == tiles - 1))
                V.wait(m, scaled)
                m = bank_free[w] = V.op(dve.scalar_tensor_tensor, resid[:, b, :], psum[:, w, :], tok[:, i, b:b + 1],
                                        resid[:, b, :], ALU.mult, ALU.add)
                out_marks.append(m)
            return out_marks

        resid_ready = ternary_product("o", q_intT, DT, o_scaled, 1, turned)

        rm, _ = squares("rm", lambda b: resid[:, b, :], D, resid_ready)
        V.wait(rm)
        ready = [V.op(dve.scalar_tensor_tensor, work[:, b, :], resid[:, b, :], scalars("rm")[:, b:b + 1],
                      gains[:, 2, :], ALU.mult, ALU.mult) for b in range(B)]
        tern_ready["gate"] = ternary("gate", wsum_ready, 4)
        ready, quantum, step = quantize("qm", lambda b: work[:, b, :], lambda b: q_int[:, b, :], D, ready)
        turned = turn_integers(q_intT, lambda b: q_int[:, b, :], DT, ready)
        gate_scaled = token_scale(2, quantum, "gate", step)
        tern_ready["down"] = ternary("down", wsum_ready, 2)
        raws_done = [V.last(), A.last()]
        z = scan[:, :, :, :].rearrange("p a c t -> p (a c t)")[:, 0:B * INNER].rearrange("p (b n) -> p b n", b=B)
        z_ready = []
        for b in range(B):
            for lo in range(0, INNER, BANK):
                n_ = min(BANK, INNER - lo)
                w_gate, w_up = bank(), bank()
                for w, base in ((w_gate, 0), (w_up, INNER)):
                    T.wait(turned[b], tern_ready["gate"], bank_free[w])
                    for k in range(DT):
                        m = T.op(pe.matmul, psum[:, w, 0:n_], q_intT[:, k, b * P:(b + 1) * P],
                                 tern["gate"][:, k, base + lo:base + lo + n_], start=(k == 0), stop=(k == DT - 1))
                A.wait(m, gate_scaled, state_ready)
                dst = z[:, b, lo:lo + n_]
                m = A.op(act.activation, dst, psum[:, w_gate, 0:n_], ACT.Sigmoid, scale=tok[:, 2, b:b + 1])
                V.wait(m)
                m = bank_free[w_gate] = V.op(dve.scalar_tensor_tensor, dst, psum[:, w_gate, 0:n_],
                                             tok[:, 2, b:b + 1], dst, ALU.mult, ALU.mult)
                V.wait(m)
                m = bank_free[w_up] = V.op(dve.scalar_tensor_tensor, dst, psum[:, w_up, 0:n_], tok[:, 2, b:b + 1],
                                           dst, ALU.mult, ALU.mult)
            z_ready.append(m)
        V.wait(raws_done)
        ready, quantum, step = quantize("qz", lambda b: z[:, b, :], lambda b: z_int[:, b, :], INNER, z_ready)
        turned = turn_integers(z_intT, lambda b: z_int[:, b, :], IT, ready)
        z_scaled = token_scale(3, quantum, "down", step)
        resid_ready = ternary_product("down", z_intT, IT, z_scaled, 3, turned)
        x2_ready = []
        for b in range(B):
            V.wait(resid_ready[b])
            x2_ready.append(V.op(dve.tensor_tensor, x1[:, b, :], x1[:, b, :], resid[:, b, :], ALU.add))
        region_2.close()
        x1_ready = x2_ready


        phase2_over = [q.last() for q in (T, V, A, G)]
        wslot += [sb(f"wslot{i}", [P, DT * HID], F32) for i in range(2, WSLOTS)]
        xm = sb("xm", [P, B, D], F32)
        xm_hi = sb("xm_hi", [P, B, D], F32R)
        xm_lo = sb("xm_lo", [P, B, D], F32R)
        route = ExitStack()
        xmT = sb("xmT", [P, DT, B * P], F32, route)
        route.close()
        hidden = sb("hidden", [P, HT, SLOTS], F32)
        wr = sb("wr", [P, DT, EXPERTS], F32)
        br = sb("br", [P, EXPERTS], F32)
        b1 = sb("b1", [P, EXPERTS, HT], F32)
        b2 = sb("b2", [EXPERTS, D], F32)
        iota_e = sb("iota_e", [P, EXPERTS], F32)
        iota_s = sb("iota_s", [P, SLOTS], F32)
        before = sb("before", [P, P], BF16)
        onesb = sb("onesb", [P, P], BF16)
        logits = sb("logits", [P, B, EXPERTS], F32)
        best = sb("best", [P, B, 8], F32)
        best_at = sb("best_at", [P, B, 8], U32)
        best_atf = sb("best_atf", [P, B, 2], F32)
        gates2 = sb("gates2", [P, B, 4], F32)
        onehot = sb("onehot", [P, B, 2, EXPERTS], F32)
        gate = sb("gate", [P, B, EXPERTS], F32)
        gateT = sb("gateT", [EXPERTS, B * P], F32)
        chosen = sb("chosen", [P, B, EXPERTS], F32)
        chosenb = sb("chosenb", [P, B, EXPERTS], BF16)
        place = sb("place", [P, B, EXPERTS], F32)
        load = sb("load", [P, 1], I32)
        pick = sb("pick", [P, 2, B, 2, SLOTS], F32R)
        picked = sb("picked", [P, 2, DT, SLOTS], F32)
        pickT = sb("pickT", [P, 2, B * P], F32R)
        slot_gate = sb("slot_gate", [P, 2, 2], F32)
        yT = sb("yT", [P, DT, SLOTS], F32)
        y_hi = sb("y_hi", [P, 2, D], F32R)
        y_lo = sb("y_lo", [P, 2, D], F32R)

        STILES = [(st, min(P, SLOTS - st * P)) for st in range(-(-SLOTS // P))]
        s_w = [signal(f"weights{i}_in") for i in range(WSLOTS)]
        w_free = [raws_done, raws_done, phase2_over, phase2_over]
        w_turn = [0]

        def load_weights(source):
            i = w_turn[0] % WSLOTS
            w_turn[0] += 1
            S.wait(w_free[i])
            return i, S.dma(s_w[i], sp.dma_start, wslot[i][:, :].rearrange("p (k n) -> p k n", n=source.shape[1]),
                            source.rearrange("(k p) n -> p k n", p=P))

        def expert_loads(e):
            return load_weights(a["w1"][e]), load_weights(a["w2"][e])

        loads = {(0, 0): expert_loads(0)}
        S.wait(phase2_over)
        s_route = signal("router_in")
        S.dma(s_route, sp.dma_start, wr[:, :, :], a["wr"].rearrange("(k p) e -> p k e", p=P))
        S.dma(s_route, sp.dma_start, br[:, :], a["br"].rearrange("(o e) -> o e", o=1).broadcast_to([P, EXPERTS]))
        S.dma(s_route, sp.dma_start, b1[:, :, :], a["b1_t"])
        route_loaded = S.dma(s_route, sp.dma_start, b2[:, :], a["b2"])
        loads[0, 1] = expert_loads(1)

        G.wait(phase2_over)
        A.wait(phase2_over)
        V.wait(phase2_over)
        G.op(pool.iota, iota_e[:, :], [[1, EXPERTS]], base=0, channel_multiplier=0,
             allow_small_or_imprecise_dtypes=True)
        G.op(pool.iota, iota_s[:, :], [[1, SLOTS]], base=1, channel_multiplier=0,
             allow_small_or_imprecise_dtypes=True)
        m = G.op(pool.memset, onesb[:, :], 1.0)
        G.wait(m)
        route_constants = G.op(pool.affine_select, out=before[:, :], in_=onesb[:, :], compare_op=ALU.is_gt, fill=0.0,
                               base=0, pattern=[[1, P]], channel_multiplier=-1)

        OUT = range(4)
        RING = (4, 5, 6, 7)
        bank_free = {w: phase2_over for w in range(8)}
        ring_turn = [0]

        def ring():
            ring_turn[0] += 1
            return RING[ring_turn[0] % len(RING)]

        normed = layernorm(xm, x1, "rstd2", x2_ready)
        for b in range(B):
            w = ring()
            m = bank_free[w] = transpose_tile(xmT[:, :, b * P:(b + 1) * P], xm[:, b, :], w, normed[b], bank_free[w],
                                              A)
            xmT_ready = m
        w = ring()
        T.wait(xmT_ready, route_loaded, bank_free[w])
        for b in range(B):
            for k in range(DT):
                m = T.op(pe.matmul, psum[:, w, b * EXPERTS:(b + 1) * EXPERTS], xmT[:, k, b * P:(b + 1) * P],
                         wr[:, k, :], start=(k == 0), stop=(k == DT - 1))
        V.wait(m, route_constants)
        for b in range(B):
            m = V.op(dve.tensor_tensor, logits[:, b, :], psum[:, w, b * EXPERTS:(b + 1) * EXPERTS], br[:, :], ALU.add)
        routed = bank_free[w] = m
        V.wait(m)
        for b in range(B):
            m = V.op(dve.max, best[:, b, :], logits[:, b, :])
        V.wait(m)
        diff = V.op(dve.tensor_tensor, gates2[:, :, 0], best[:, :, 1], best[:, :, 0], ALU.subtract)
        for b in range(B):
            m = V.op(dve.max_index, best_at[:, b, :], best[:, b, :], logits[:, b, :])
        A.wait(diff)
        expd = A.op(act.activation, gates2[:, :, 1], gates2[:, :, 0], ACT.Exp)
        V.wait(m)
        m = V.op(dve.tensor_copy, best_atf[:, :, :], best_at[:, :, 0:2])
        V.wait(m)
        for b in range(B):
            for i in range(2):
                m = V.op(dve.tensor_scalar, onehot[:, b, i, :], iota_e[:, :], best_atf[:, b, i:i + 1], None,
                         ALU.is_equal)
        V.wait(m)
        m = V.op(dve.tensor_tensor, chosen[:, :, :], onehot[:, :, 0, :], onehot[:, :, 1, :], ALU.add)
        V.wait(m)
        chosen_ready = V.op(dve.tensor_copy, chosenb[:, :, :], chosen[:, :, :])
        V.wait(expd)
        m = V.op(dve.tensor_scalar, gates2[:, :, 2], gates2[:, :, 1], 1.0, None, ALU.add)
        V.wait(m)
        m = V.op(dve.reciprocal, gates2[:, :, 2], gates2[:, :, 2])
        V.wait(m)
        m = V.op(dve.tensor_tensor, gates2[:, :, 3], gates2[:, :, 1], gates2[:, :, 2], ALU.mult)
        V.wait(m)
        for b in range(B):
            m = V.op(dve.tensor_scalar, gate[:, b, :], onehot[:, b, 0, :], gates2[:, b, 2:3], None, ALU.mult)
        V.wait(m)
        for b in range(B):
            m = V.op(dve.scalar_tensor_tensor, gate[:, b, :], onehot[:, b, 1, :], gates2[:, b, 3:4], gate[:, b, :],
                     ALU.mult, ALU.add)
        gate_ready = m

        w = ring()
        T.wait(chosen_ready, bank_free[w])
        for b in range(B):
            for earlier in range(b):
                T.quiet(pe.matmul, psum[:, w, b * EXPERTS:(b + 1) * EXPERTS], onesb[:, :], chosenb[:, earlier, :],
                        start=(earlier == 0), stop=False)
            T.quiet(pe.matmul, psum[:, w, b * EXPERTS:(b + 1) * EXPERTS], before[:, :], chosenb[:, b, :],
                    start=(b == 0), stop=True)
        for b in range(B):
            m = T.op(pe.matmul, psum[:, w, B * EXPERTS:(B + 1) * EXPERTS], onesb[:, :], chosenb[:, b, :],
                     start=(b == 0), stop=(b == B - 1))
        V.wait(m)
        m = V.op(dve.scalar_tensor_tensor, place[:, :, :].rearrange("p b e -> p (b e)"), psum[:, w, 0:B * EXPERTS],
                 1.0, chosen[:, :, :].rearrange("p b e -> p (b e)"), ALU.add, ALU.mult)
        place_ready = m
        load_ready = bank_free[w] = V.op(dve.tensor_reduce, load[:, :], psum[:, w, B * EXPERTS:(B + 1) * EXPERTS],
                                         AX.X, ALU.max)
        V.wait(normed)
        m = V.op(dve.tensor_copy, xm_hi[:, :, :], xm[:, :, :])
        V.wait(m)
        xm_ready = V.op(dve.tensor_tensor, xm_lo[:, :, :], xm[:, :, :], xm_hi[:, :, :].bitcast(F32), ALU.subtract)
        w = ring()
        T.wait(gate_ready, bank_free[w])
        for b in range(B):
            m = T.op(pe.transpose, psum[0:EXPERTS, w, b * P:(b + 1) * P], gate[:, b, :], ident[:, :])
        A.wait(m)
        gateT_ready = bank_free[w] = A.op(act.copy, gateT[:, :], psum[0:EXPERTS, w, :])

        class Last:
            pick = [None, None]
            picked = [None, None]
            pickT = slot_gate = hidden = yT = y = None

        def gather(pair, r, half):
            for b in range(B):
                for i in range(2):
                    V.wait(place_ready, Last.pick[half])
                    e = 2 * pair + i
                    picks = V.op(dve.tensor_scalar, pick[:, half, b, i, :], iota_s[:, :], float(r * SLOTS),
                                 place[:, b, e:e + 1], ALU.add, ALU.is_equal)
            for k in range(DT):
                w = ring()
                T.wait(picks, xm_ready, bank_free[w])
                for b in range(B):
                    for part in (xm_hi, xm_lo):
                        m = T.op(pe.matmul, psum[:, w, 0:2 * SLOTS], part[:, b, k * P:(k + 1) * P],
                                 pick[:, half, b, :, :].rearrange("p i s -> p (i s)"),
                                 start=(b == 0 and part is xm_hi), stop=(b == B - 1 and part is xm_lo))
                A.wait(m, Last.picked)
                m = bank_free[w] = A.op(act.copy, picked[:, :, k, :],
                                        psum[:, w, 0:2 * SLOTS].rearrange("p (i s) -> p i s", i=2))
            return m

        def hidden_layer(e, i, slot_mark, gathered):
            slot, loaded = slot_mark
            w1 = wslot[slot][:, :].rearrange("p (k n) -> p k n", k=DT)
            marks = []
            for h in range(HT):
                w = ring()
                T.wait(loaded, gathered, bank_free[w])
                for k in range(DT):
                    m = T.op(pe.matmul, psum[:, w, 0:SLOTS], w1[:, k, h * P:(h + 1) * P], picked[:, i, k, :],
                             start=(k == 0), stop=(k == DT - 1))
                if h % 2:
                    A.wait(m, Last.hidden)
                    m2 = A.op(act.activation, hidden[:, h, :], psum[:, w, 0:SLOTS], ACT.Relu, bias=b1[:, e, h:h + 1])
                else:
                    V.wait(m, Last.hidden)
                    m2 = V.op(dve.tensor_scalar, hidden[:, h, :], psum[:, w, 0:SLOTS], b1[:, e, h:h + 1], 0.0,
                              ALU.add, ALU.max)
                bank_free[w] = m2
                marks.append(m2)
            w_free[slot] = Last.picked[i] = m
            return marks

        def output_layer(slot_mark, hidden_ready):
            slot, loaded = slot_mark
            w2 = wslot[slot][:, :].rearrange("p (h n) -> p h n", h=HT)
            for k in range(DT):
                w = ring()
                T.wait(loaded, bank_free[w])
                for h in range(HT):
                    T.wait(hidden_ready[h])
                    m = T.op(pe.matmul, psum[:, w, 0:SLOTS], w2[:, h, k * P:(k + 1) * P], hidden[:, h, :],
                             start=(h == 0), stop=(h == HT - 1))
                q = A if k % 2 else V
                q.wait(m, Last.yT)
                out_mark = bank_free[w] = (A.op(act.copy, yT[:, k, :], psum[:, w, 0:SLOTS]) if q is A else
                                           V.op(dve.tensor_copy, yT[:, k, :], psum[:, w, 0:SLOTS]))
            w_free[slot] = Last.hidden = m
            return [V.last(), A.last()]

        first_scatter = [True]

        def slot_tables(e, i, half):
            for st, rows_ in STILES:
                w = ring()
                T.wait(bank_free[w])
                for b in range(B):
                    m = T.op(pe.transpose, psum[0:rows_, w, b * P:(b + 1) * P],
                             pick[:, half, b, i, st * P:st * P + rows_].bitcast(F32), ident[:, :])
                V.wait(m, Last.pickT)
                bank_free[w] = V.op(dve.tensor_copy, pickT[0:rows_, st, :], psum[0:rows_, w, :])
            w = ring()
            T.wait(gate_ready, bank_free[w])
            for st, rows_ in STILES:
                for b in range(B):
                    m = T.op(pe.matmul, psum[0:rows_, w, st:st + 1],
                             pick[:, half, b, i, st * P:st * P + rows_].bitcast(F32), gate[:, b, e:e + 1],
                             start=(b == 0), stop=(b == B - 1))
            Last.pick[half] = m
            V.wait(m, Last.slot_gate)
            for st, rows_ in STILES:
                m = bank_free[w] = V.op(dve.tensor_copy, slot_gate[0:rows_, st, i:i + 1], psum[0:rows_, w, st:st + 1])
            return m

        def scatter(i, yT_ready, tables):
            for st, rows_ in STILES:
                w = ring()
                T.wait(yT_ready, bank_free[w])
                for k in range(DT):
                    m = Last.yT = T.op(pe.transpose, psum[0:rows_, w, k * P:(k + 1) * P],
                                       yT[:, k, st * P:st * P + rows_], ident[:, :])
                A.wait(m, tables, Last.y)
                m = A.op(act.activation, y_hi[0:rows_, st, :], psum[0:rows_, w, :], ACT.Copy,
                         scale=slot_gate[0:rows_, st, i:i + 1])
                V.wait(m, Last.y)
                m = bank_free[w] = V.op(dve.scalar_tensor_tensor, y_lo[0:rows_, st, :], psum[0:rows_, w, :],
                                        slot_gate[0:rows_, st, i:i + 1], y_hi[0:rows_, st, :].bitcast(F32),
                                        ALU.mult, ALU.subtract)
            Last.slot_gate = m
            T.wait(m)
            for b in OUT:
                T.wait(bank_free[b])
                for st, rows_ in STILES:
                    for part in (y_hi, y_lo):
                        m = T.op(pe.matmul, psum[:, b, :], pickT[0:rows_, st, b * P:(b + 1) * P],
                                 part[0:rows_, st, :], start=(first_scatter[0] and st == 0 and part is y_hi),
                                 stop=False, skip_group_check=True)
            first_scatter[0] = False
            Last.y = Last.pickT = m

        def experts_round(r, preloaded):
            waiting = None
            for pair in range(EXPERTS // 2):
                half = pair % 2
                gathered = gather(pair, r, half)
                for i in range(2):
                    e = 2 * pair + i
                    w1_mark, w2_mark = preloaded.pop((r, e)) if (r, e) in preloaded else expert_loads(e)
                    hidden_ready = hidden_layer(e, i, w1_mark, gathered)
                    if waiting:
                        scatter(*waiting)
                    tables = slot_tables(e, i, half)
                    yT_ready = output_layer(w2_mark, hidden_ready)
                    if e + 2 < EXPERTS:
                        preloaded[r, e + 2] = expert_loads(e + 2)
                    waiting = (i, yT_ready, tables)
            scatter(*waiting)

        experts_round(0, loads)

        everyone = (T, V, A, G, S)
        state = [q.last() for q in (T, V, A, G)]
        known = {q: dict(q.waited) for q in everyone}
        for q, name in zip(everyone, ("tensor", "vector", "scalar", "gpsimd", "sync")):
            q.wait(load_ready)
            q.branch = len(q.steps)
            known[q] = dict(q.waited)
            q.done = signal(name + "_extra_done")
        s_w = [signal(f"extra_weights{i}_in") for i in range(WSLOTS)]
        saved_bank_free = dict(bank_free)
        for r in range(1, ROUNDS):
            loads = {(r, 0): expert_loads(0), (r, 1): expert_loads(1)}
            experts_round(r, loads)
        for q, name in zip(everyone, ("tensor", "vector", "scalar", "gpsimd", "sync")):
            q.join = len(q.steps)
            q.waited = known[q]
            q.done = signal(name + "_end_done")

        T.wait(gateT_ready, route_loaded)
        out_ready = []
        for b in OUT:
            m = T.op(pe.matmul, psum[:, b, :], gateT[:, b * P:(b + 1) * P], b2[:, :], start=False, stop=True,
                     skip_group_check=True)
            V.wait(m)
            out_ready.append(V.op(dve.tensor_tensor, x1[:, b, :], psum[:, b, :], x1[:, b, :], ALU.add))
        s_out = signal("out_stored")
        for b in range(B):
            S.wait(out_ready[b])
            stored = S.dma(s_out, sp.dma_start, out[b], x1[:, b, :])
        S.wait(stored)

        block = life.enter_context(nc.Block())

        @block.tensor
        def _(engine):
            T.replay(engine, load[0:1, 0:1])

        @block.vector
        def _(engine):
            V.replay(engine, load[0:1, 0:1])

        @block.scalar
        def _(engine):
            A.replay(engine, load[0:1, 0:1])

        @block.gpsimd
        def _(engine):
            G.replay(engine, load[0:1, 0:1])

        @block.sync
        def _(engine):
            S.replay(engine, load[0:1, 0:1])


def lay_out(i):
    import numpy as np
    c = lambda t: np.ascontiguousarray(np.asarray(t))
    return {
        "x": c(i["x"]), "ctx_t": c(np.asarray(i["ctx_1024"]).transpose(0, 2, 1)),
        "bias": c(np.asarray(i["fside_1x1xSxS2_0"]).reshape(P, KEYS)),
        "wq": c(i["L0_xattn_Wq"]), "wk": c(i["L0_xattn_Wk"]), "wv": c(i["L0_xattn_Wv"]), "wo": c(i["L0_xattn_Wo"]),
        "attn_norm": c(i["L0_attn_attn_norm_w"]), "g_norm": c(i["L0_attn_g_norm_w"]),
        "mlp_norm": c(i["L0_attn_mlp_norm_w"]), "lower": c(np.asarray(i["L0_attn_lower_bound"]).reshape(DT, P).T),
        "wr": c(i["L0_ffn_Wr"]), "br": c(i["L0_ffn_br"]), "w1": c(i["L0_ffn_W1"]), "w2": c(i["L0_ffn_W2"]),
        "b1_t": c(np.asarray(i["L0_ffn_b1"]).reshape(EXPERTS, HT, P).transpose(2, 0, 1)), "b2": c(i["L0_ffn_b2"]),
        "w_i_t": c(np.asarray(i["L0_attn_w_i"]).T), "w_f_t": c(np.asarray(i["L0_attn_w_f"]).T),
        "w_g_t": c(np.asarray(i["L0_attn_w_g"]).T), "w_o_t": c(np.asarray(i["L0_attn_w_o"]).T),
        "w_gate_t": c(np.asarray(i["L0_attn_w_gate"]).T), "w_down_t": c(np.asarray(i["L0_attn_w_down"]).T),
    }


def kernel(**inputs):
    import concourse.bacc as bacc
    from concourse.bass_utils import run_bass_kernel_spmd

    nc = bacc.Bacc("TRN2", target_bir_lowering=False, num_devices=1, dynamic_dma_scratch_size=1024)
    arrays = {f"in_{name}": t for name, t in lay_out(inputs).items()}
    args = {name[3:]: nc.dram_tensor(name, t.shape, mybir.dt.from_np(t.dtype), kind="ExternalInput").ap()
            for name, t in arrays.items()}
    out = nc.dram_tensor("out_x", (B, P, D), F32, kind="ExternalOutput").ap()
    perceiver_block(nc, args, out)
    return run_bass_kernel_spmd(nc, [arrays], core_ids=[0]).results[0]["out_x"]
```

```python
from contextlib import ExitStack

import concourse.bass as bass
from concourse import mybir

F32 = mybir.dt.float32
F32R = mybir.dt.float32r
BF16 = mybir.dt.bfloat16
I32 = mybir.dt.int32
U32 = mybir.dt.uint32
ALU = mybir.AluOpType
ACT = mybir.ActivationFunctionType
AX = mybir.AxisListType

P = 128
B = 4
D = 512
DT = D // P
KEYS = 2048
HEADS = 16
DH = D // HEADS
QUAD = P // DH
CHUNK = 512
KTILES = KEYS // P
INNER = 1408
IT = INNER // P
CHUNKS = KEYS // CHUNK
BANK = 512
EXPERTS = 8
HID = 2048
HT = HID // P
STACKS = 3
PARTS = 3
SLOTS = 192
ROUNDS = -(-B * P // SLOTS)
ROUND_MAGIC = 1.5 * 2.0 ** 23
LOWEST = -3.0e38


class Signal:

    def __init__(self, sem):
        self.sem = sem
        self.count = 0


class Queue:

    def __init__(self, done):
        self.done = done
        self.steps = []
        self.waited = {}
        self.branch = self.join = None

    def wait(self, *marks):
        for mark in marks:
            if mark is None:
                continue
            if isinstance(mark, list):
                self.wait(*mark)
                continue
            signal, count = mark
            if self.waited.get(id(signal), 0) < count:
                self.waited[id(signal)] = count
                self.steps.append((None, (signal, count), None, None, 0))

    def quiet(self, method, *args, **named):
        self.steps.append((method, args, named, None, 0))

    def op(self, method, *args, **named):
        self.steps.append((method, args, named, self.done, 1))
        self.done.count += 1
        return (self.done, self.done.count)

    def dma(self, signal, method, *args, **named):
        self.steps.append((method, args, named, signal, 16))
        signal.count += 16
        return (signal, signal.count)

    def last(self):
        return (self.done, self.done.count) if self.done.count else None

    def emit(self, engine, steps):
        for method, args, named, signal, by in steps:
            if method is None:
                engine.wait_ge(args[0].sem, args[1])
                continue
            made = method(*args, **named)
            if signal is not None:
                made.then_inc(signal.sem, by)

    def replay(self, engine, load):
        self.emit(engine, self.steps[:self.branch])
        with engine.register("fullest") as fullest:
            engine.reg_load(fullest, load)
            with engine.If_cmp(fullest, SLOTS, "IS_GT"):
                self.emit(engine, self.steps[self.branch:self.join])
        self.emit(engine, self.steps[self.join:])


def perceiver_block(nc, a, out, debug=None):
    with ExitStack() as life:
        def sb(name, shape, dt, stack=life):
            return stack.enter_context(nc.sbuf_tensor(name, shape, dt))

        def signal(name):
            return Signal(life.enter_context(nc.semaphore(name)))

        pe, dve, act, pool, sp = nc.tensor, nc.vector, nc.scalar, nc.gpsimd, nc.sync
        T = Queue(signal("tensor_done"))
        V = Queue(signal("vector_done"))
        A = Queue(signal("scalar_done"))
        G = Queue(signal("gpsimd_done"))
        S = Queue(signal("sync_done"))

        psum = life.enter_context(nc.psum_tensor("psum", [P, 8, BANK], F32))

        ident = sb("ident", [P, P], F32)
        identb = sb("identb", [P, P], BF16)
        region_bias = ExitStack()
        biasmap = sb("biasmap", [P, KEYS], F32, region_bias)
        region_bias.close()
        x1 = sb("x1", [P, B, D], F32)
        stats = sb("stats", [P, B, 6], F32)
        meanvar = sb("meanvar", [P, B, 2], F32)
        minus_half = sb("minus_half", [P, B], F32)
        ones = sb("ones", [P, P], F32)
        magic = sb("magic", [P, 1], F32)
        col = sb("col", [P, 64, B], F32)
        names = {}

        def scalars(name):
            names.setdefault(name, len(names))
            assert len(names) <= 64
            return col[:, names[name], :]

        m = G.op(pool.memset, ident[:, :], 0.0)
        G.wait(m)
        m = G.op(pool.affine_select, out=ident[:, :], in_=ident[:, :], compare_op=ALU.not_equal, fill=1.0, base=0,
                 pattern=[[-1, P]], channel_multiplier=1)
        G.wait(m)
        m = G.op(pool.tensor_copy, identb[:, :], ident[:, :])
        G.op(pool.memset, ones[:, :], 1.0)
        G.op(pool.memset, magic[:, :], ROUND_MAGIC)
        constants = G.op(pool.memset, minus_half[:, :], -0.5)

        def rsqrt_cols(dst, src, scale, eps, after):
            G.wait(after, constants)
            m = G.op(pool.tensor_scalar, dst, src, scale, eps, ALU.mult, ALU.add)
            G.wait(m)
            return G.op(pool.tensor_tensor, dst, dst, minus_half[:, :], ALU.pow)

        def layernorm(dst, src, key, after):
            rstd = scalars(key)
            m = None
            for b in range(B):
                V.wait(after[b], V.last())
                m = V.op(dve.bn_stats, stats[:, b, :], src[:, b, :])
                V.wait(m)
                m = V.op(dve.bn_aggr, meanvar[:, b, :], stats[:, b, :])
            m = rsqrt_cols(rstd, meanvar[:, :, 1], 1.0, 1e-5, m)
            V.wait(m)
            return [V.op(dve.tensor_scalar, dst[:, b, :], src[:, b, :], meanvar[:, b, 0:1], rstd[:, b:b + 1],
                         ALU.subtract, ALU.mult) for b in range(B)]

        def transpose_tile(dst, src, bank, after, bank_free, copier):
            T.wait(after, bank_free, constants)
            for k in range(DT):
                m = T.op(pe.transpose, psum[:, bank, k * P:(k + 1) * P], src[:, k * P:(k + 1) * P], ident[:, :])
            copied = psum[:, bank, :].rearrange("p (k t) -> p k t", k=DT)
            copier.wait(m)
            if copier is A:
                return A.op(act.copy, dst, copied)
            return V.op(dve.tensor_copy, dst, copied)

        region_f, region_r = ExitStack(), ExitStack()
        region_bytes_f = 72 * 1024
        wk_hi = sb("wk_hi", [P, DT, D], F32R, region_f)
        wk_lo = sb("wk_lo", [P, DT, D], F32R, region_f)
        wv_hi = sb("wv_hi", [P, DT, D], F32R, region_f)
        wv_lo = sb("wv_lo", [P, DT, D], F32R, region_f)
        region_c, region_s = ExitStack(), ExitStack()
        ctx_raw = sb("ctx_raw", [P, DT, CHUNK], F32, region_c)
        ctx_part = sb("ctx_part", [P, 2, 2, DT, CHUNK], F32R, region_c)
        region_c.close()
        keys_hi = sb("keys_hi", [P, KEYS], F32R, region_s)
        keys_lo = sb("keys_lo", [P, KEYS], F32R, region_s)
        stack = sb("stack", [P, STACKS, KEYS], F32R, region_s)
        region_s.close()
        region_f.close()
        region_f2 = ExitStack()
        gate_raw = sb("gate_raw", [P, DT, 2 * INNER], F32, region_f2)
        ifg_raw = sb("ifg_raw", [P, 3, DT, D], F32, region_f2)
        region_f2.close()
        WSLOTS = 4
        wslot = [sb(f"wslot{i}", [P, DT * HID], F32) for i in range(2)]
        sb("rest_f", [P, region_bytes_f // 4 - 2 * DT * HID], F32)

        PS = 2 * QUAD
        kT = sb("kT", [P, DT, KEYS], F32, region_r)
        v = sb("v", [P, KTILES, D], F32, region_r)
        region_p = ExitStack()
        early_stack = sb("early_stack", [P, PS, KEYS], F32R, region_p)
        region_p.close()
        prob = sb("prob", [P, PS, KEYS], F32, region_r)
        qstack = sb("qstack", [P, 2, QUAD, P], F32R, region_r)
        oT = sb("oT", [P, 2, P], F32, region_r)
        PTS = 3
        probT = sb("probT", [P, PTS, QUAD * P], F32, region_r)
        top = sb("top", [P, HEADS, 4], F32, region_r)
        rinv = sb("rinv", [P, 2, QUAD], F32, region_r)
        rbc = sb("rbc", [P, P], F32, region_r)
        rT = sb("rT", [P, P], F32, region_r)
        region_r.close()

        view = lambda slot: prob[:, slot, :].rearrange("p (k n) -> p k n", k=DT)
        wq_sb, wk_sb, wv_sb, xhT, x_in, q_all, q_hi, q_lo = (view(s) for s in range(8))
        q_parts = nc.dram_tensor("q_parts", (2, D, B * P), F32, kind="Internal").ap()
        attended = nc.dram_tensor("attended", (D, B * P), F32, kind="Internal").ap()
        rows = lambda w: w.rearrange("(k p) n -> p k n", p=P)

        s_x, s_wq, s_wk, s_wv, s_bias, s_ctx = (signal(n) for n in
                                                ("x_in", "wq_in", "wk_in", "wv_in", "bias_in", "ctx_in"))
        wk_loaded = S.dma(s_wk, sp.dma_start, wk_sb, rows(a["wk"]))

        def load_ctx(b, c, free):
            S.wait(free)
            return S.dma(s_ctx, sp.dma_start, ctx_raw[:, :, :],
                         a["ctx_t"][b].rearrange("(k p) n -> p k n", p=P)[:, :, c * CHUNK:(c + 1) * CHUNK])

        ctx_loaded = load_ctx(0, 0, None)
        wv_loaded = S.dma(s_wv, sp.dma_start, wv_sb, rows(a["wv"]))
        wq_loaded = S.dma(s_wq, sp.dma_start, wq_sb, rows(a["wq"]))
        x_loaded = S.dma(s_x, sp.dma_start, x_in, a["x"].rearrange("b s d -> s b d"))
        bias_loaded = S.dma(s_bias, sp.dma_start, biasmap[:, :], a["bias"])

        def split(hi, lo, raw, after):
            V.wait(after)
            m = V.op(dve.tensor_copy, hi, raw)
            V.wait(m)
            return V.op(dve.tensor_tensor, lo, raw, hi.bitcast(F32), ALU.subtract)

        wk_split = split(wk_hi[:, :, :], wk_lo[:, :, :], wk_sb, wk_loaded)
        WORK = (4, 5, 6)
        OUT_BANK = 7
        work_free = {w: None for w in WORK}
        turn = [0]

        def next_bank():
            w = WORK[turn[0] % len(WORK)]
            turn[0] += 1
            return w

        kT_read = [None] * DT
        v_read = [None] * KTILES
        ctx_read = [None, None]
        kT_ready = {}
        v_ready = {}

        def project_keys(c, half, ready, tiles=range(DT)):
            for m in tiles:
                w = next_bank()
                T.wait(work_free[w], ready, wk_split)
                for k in range(DT):
                    wh, wl = wk_hi[:, k, m * P:(m + 1) * P], wk_lo[:, k, m * P:(m + 1) * P]
                    T.quiet(pe.matmul, psum[:, w, :], wh, ctx_part[:, half, 0, k, :], start=(k == 0), stop=False)
                    T.quiet(pe.matmul, psum[:, w, :], wh, ctx_part[:, half, 1, k, :], start=False, stop=False)
                    done = T.op(pe.matmul, psum[:, w, :], wl, ctx_part[:, half, 0, k, :], start=False, stop=(k == DT - 1))
                A.wait(done, kT_read[m])
                kT_ready[m, c] = work_free[w] = A.op(act.copy, kT[:, m, c * CHUNK:(c + 1) * CHUNK], psum[:, w, :])

        def project_values(c, half, tiles=range(CHUNK // P)):
            for t in tiles:
                w, kt = next_bank(), c * (CHUNK // P) + t
                T.wait(work_free[w], wv_split)
                for k in range(DT):
                    ch, cl = ctx_part[:, half, 0, k, t * P:(t + 1) * P], ctx_part[:, half, 1, k, t * P:(t + 1) * P]
                    T.quiet(pe.matmul, psum[:, w, :], ch, wv_hi[:, k, :], start=(k == 0), stop=False)
                    T.quiet(pe.matmul, psum[:, w, :], ch, wv_lo[:, k, :], start=False, stop=False)
                    done = T.op(pe.matmul, psum[:, w, :], cl, wv_hi[:, k, :], start=False, stop=(k == DT - 1))
                if c < CHUNKS - 1:
                    V.wait(done, v_read[kt])
                    v_ready[kt] = work_free[w] = V.op(dve.tensor_copy, v[:, kt, :], psum[:, w, :])
                else:
                    A.wait(done, v_read[kt])
                    v_ready[kt] = work_free[w] = A.op(act.copy, v[:, kt, :], psum[:, w, :])
            return done

        slot_free = [None] * PS
        s_free = [None, None]
        stack_read = [None] * (STACKS + QUAD)
        stack_loaded = [None] * (STACKS + QUAD)
        queries_read = [None, None]
        queries_loaded = [None, None]
        out_read = [None, None]
        keys_moved = []
        s_stack = [signal(f"stack{i}_in") for i in range(STACKS + QUAD)]
        s_queries = [signal(f"queries{i}_in") for i in range(2)]

        def load_queries(n, b, g):
            S.wait(q_stored, queries_read[n % 2])
            for block, part in enumerate((0, 0, 1)):
                queries_loaded[n % 2] = S.dma(
                    s_queries[n % 2], sp.dma_start,
                    qstack[block * DH:(block + 1) * DH, n % 2, :, :].bitcast(F32),
                    q_parts[part, g * P:(g + 1) * P, b * P:(b + 1) * P].rearrange("(j d) t -> d j t", d=DH))

        def split_keys(g, free):
            V.wait(free, keys_moved, [kT_ready[g, c] for c in range(CHUNKS)])
            high = V.op(dve.tensor_copy, keys_hi[:, :], kT[:, g, :])
            G.wait(free, keys_moved, high)
            low = G.op(pool.tensor_tensor, keys_lo[:, :], kT[:, g, :], keys_hi[:, :].bitcast(F32), ALU.subtract)
            kT_read[g] = low
            keys_moved.clear()
            return high, low

        def stack_of(g, j):
            return STACKS + j if g == 0 else (QUAD * (g - 1) + j) % STACKS

        def stack_place(n, g, j):
            return early_stack[:, (QUAD * (n + 1) + j) % PS, :] if g == 0 else stack[:, stack_of(g, j), :]

        def load_stack(n, g, j, split_done, free=None):
            i = stack_of(g, j)
            high, low = split_done
            place = stack_place(n, g, j)
            S.wait(slot_free[(QUAD * (n + 1) + j) % PS] if g == 0 else [stack_read[i], free])
            for block, part, ready in ((0, keys_hi, high), (2, keys_hi, high), (1, keys_lo, low)):
                S.wait(ready)
                stack_loaded[i] = S.dma(s_stack[i], sp.dma_start,
                                        place[block * DH:(block + 1) * DH, :].bitcast(F32),
                                        part[j * DH:(j + 1) * DH, :].bitcast(F32))
            keys_moved.append(stack_loaded[i])

        def scores(n, g, j):
            h, slot, i = QUAD * g + j, (QUAD * n + j) % PS, stack_of(g, j)
            place = stack_place(n, g, j)
            T.wait(queries_loaded[n % 2], stack_loaded[i])
            V.wait(slot_free[slot], bias_loaded)
            done = [None] * 2
            for half in range(2):
                T.wait(s_free[half])
                for c in range(2 * half, 2 * half + 2):
                    done[half] = T.op(pe.matmul, psum[:, c, :], qstack[0:PARTS * DH, n % 2, j, :],
                                      place[0:PARTS * DH, c * CHUNK:(c + 1) * CHUNK], start=True, stop=True)
            stack_read[i] = queries_read[n % 2] = done[1]
            if g == 0:
                slot_free[(QUAD * (n + 1) + j) % PS] = done[1]

            def add_bias(half, lowest):
                keys = slice(half * 2 * CHUNK, (half + 1) * 2 * CHUNK)
                V.wait(done[half])
                s_free[half] = V.op(
                    dve.tensor_tensor_reduce, prob[:, slot, keys],
                    psum[:, 2 * half:2 * half + 2, :].rearrange("p a n -> p (a n)"), biasmap[:, keys], 1.0,
                    lowest, ALU.add, ALU.max, top[:, h, half:half + 1])
                return s_free[half]

            first = add_bias(0, LOWEST)

            def second_half():
                V.wait(first)
                V.wait(add_bias(1, top[:, h, 0:1]))
                return V.op(dve.tensor_scalar, top[:, h, 2:3], top[:, h, 1:2], -1.0, None, ALU.mult)

            return second_half

        def exponentials(n, g, j, negated):
            h, slot = QUAD * g + j, (QUAD * n + j) % PS
            A.wait(negated, sums_read.get(h))
            m = A.op(act.activation, prob[:, slot, :], prob[:, slot, :], ACT.Exp, bias=top[:, h, 2:3], scale=1.0,
                     accum_out=top[:, h, 3:4])
            return slot, m

        probT_read = [None] * PTS
        sums_read = {}

        def weighted_values(n, b, g, heads, quarter=None, meanwhile=None, exponentiate=None):
            half = n % 2
            outp = psum[:, OUT_BANK, half * P:(half + 1) * P]

            def turn_tile(kt):
                w, r = next_bank(), kt % PTS
                T.wait(work_free[w], [m for _, m in heads])
                for j, (slot, _) in enumerate(heads):
                    done = T.op(pe.transpose, psum[:, w, j * P:(j + 1) * P], prob[:, slot, kt * P:(kt + 1) * P],
                                ident[:, :])
                if kt == KTILES - 1:
                    for slot, _ in heads:
                        slot_free[slot] = done
                q = V if kt in STARTS else A
                q.wait(done, probT_read[r])
                if q is A:
                    work_free[w] = A.op(act.copy, probT[:, r, :], psum[:, w, :])
                else:
                    work_free[w] = V.op(dve.tensor_copy, probT[:, r, :], psum[:, w, :])
                moved[kt] = work_free[w]

            def multiply(kt):
                r = kt % PTS
                T.wait(moved[kt], v_ready[kt], out_read if kt == 0 else None)
                for j in range(QUAD):
                    cols = slice((QUAD * g + j) * DH, (QUAD * g + j + 1) * DH)
                    done = T.op(pe.matmul, outp[j * DH:(j + 1) * DH, :], v[:, kt, cols],
                                probT[:, r, j * P:(j + 1) * P], start=(kt == 0), stop=(kt == KTILES - 1),
                                tile_position=(0, j * DH))
                v_read[kt] = probT_read[r] = done
                return done

            result = None

            def spread_reciprocals():
                V.wait(heads[-1][1], rinv_read[half])
                m = V.op(dve.reciprocal, rinv[:, half, :], top[:, QUAD * g:QUAD * (g + 1), 3])
                for h in range(QUAD * g, QUAD * (g + 1)):
                    sums_read[h] = m
                V.wait(m, rbc_read[0])
                m = V.op(dve.tensor_copy, rbc[:, :].rearrange("p (j d) -> p j d", j=QUAD),
                         rinv[:, half, :].rearrange("p (j d) -> p j d", d=1).broadcast_to([P, QUAD, DH]))
                rinv_read[half] = m
                spread_ready[0] = m

            def turn_reciprocals():
                w = next_bank()
                T.wait(spread_ready[0], work_free[w])
                m = rbc_read[0] = T.op(pe.transpose, psum[:, w, 0:P], rbc[:, :], ident[:, :])
                A.wait(m, rT_read[0])
                rT_ready[0] = work_free[w] = A.op(act.copy, rT[:, :], psum[:, w, 0:P])

            def finish():
                multiply(KTILES - 2)
                product = multiply(KTILES - 1)
                V.wait(rT_ready[0], product, attended_stored[half])
                m = rT_read[0] = out_read[half] = V.op(dve.tensor_tensor, oT[:, half, :], outp, rT[:, :], ALU.mult)
                S.wait(m)
                attended_stored[half] = S.dma(s_attended[half], sp.dma_start,
                                              attended[g * P:(g + 1) * P, b * P:(b + 1) * P], oT[:, half, :])

            for kt in range(KTILES) if quarter is None else range(STARTS[quarter], STARTS[quarter + 1]):
                if kt == KTILES - 2 and exponentiate:
                    result = exponentiate(negated)
                turn_tile(kt)
                if kt in STARTS and meanwhile:
                    negated = meanwhile()
                if kt >= 2:
                    multiply(kt - 2)
                if kt == 1:
                    spread_reciprocals()
                if kt == QUAD + 2:
                    turn_reciprocals()
            if kt == KTILES - 1:
                unfinished.append(finish)
            elif exponentiate:
                result = exponentiate(negated)
            return result

        rinv_read, rbc_read, rT_read = [None] * 2, [None] * 2, [None] * 2
        moved = {}
        unfinished = []

        def finish_quad():
            if unfinished:
                unfinished.pop()()

        STARTS = (0, 3, 7, 11, KTILES)
        rT_ready, spread_ready = [None], [None]
        attended_stored = [None] * 2
        s_attended = [signal(f"attended{i}_stored") for i in range(2)]

        def split_chunk(number):
            nonlocal ctx_loaded
            half = number % 2
            V.wait(ctx_read[half])
            ready = split(ctx_part[:, half, 0, :, :], ctx_part[:, half, 1, :, :], ctx_raw[:, :, :], ctx_loaded)
            if (number + 1) % CHUNKS:
                ctx_loaded = load_ctx(number // CHUNKS, (number + 1) % CHUNKS, ready)
            return ready

        pending = None
        n = 0
        chunk_ready = {0: split_chunk(0)}
        wv_split = split(wv_hi[:, :, :], wv_lo[:, :, :], wv_sb, wv_loaded)
        for b in range(B):
            for c in range(CHUNKS):
                number = b * CHUNKS + c
                half = number % 2
                if c == 0 and pending:
                    finish_quad()
                    weighted_values(*pending)
                    finish_quad()
                    pending = None
                project_keys(c, half, chunk_ready[number], range(DT if c < CHUNKS - 1 else DT - 1))
                if c + 1 < CHUNKS:
                    chunk_ready[number + 1] = split_chunk(number + 1)
                else:
                    split_done = split_keys(0, [chunk_ready[number], ctx_read[0]])
                    load_queries(n, b, 0)
                    for j in range(QUAD):
                        load_stack(n, 0, j, split_done)
                if c < CHUNKS - 1:
                    ctx_read[half] = project_values(c, half)
                if b == 0 and c == 1:
                    normed = layernorm(x_in, x_in, "rstd0", [x_loaded] * B)
                    for t in range(B):
                        w = next_bank()
                        m = work_free[w] = transpose_tile(xhT[:, :, t * P:(t + 1) * P], x_in[:, t, :], w, normed[t],
                                                          work_free[w], A)
                    for g in range(DT):
                        w = next_bank()
                        T.wait(m, wq_loaded, work_free[w])
                        for k in range(DT):
                            done = T.op(pe.matmul, psum[:, w, :], wq_sb[:, k, g * P:(g + 1) * P], xhT[:, k, :],
                                        start=(k == 0), stop=(k == DT - 1))
                        A.wait(done)
                        m2 = work_free[w] = A.op(act.activation, q_all[:, g, :], psum[:, w, :], ACT.Copy,
                                                 scale=float(DH) ** -0.5)
                    m2 = split(q_hi.bitcast(F32R), q_lo.bitcast(F32R), q_all, m2)
                    S.wait(m2)
                    s_parts = signal("query_parts_stored")
                    for i, part in enumerate((q_hi, q_lo)):
                        q_stored = S.dma(s_parts, sp.dma_start,
                                         q_parts[i].rearrange("(k p) t -> p k t", p=P), part)
                    slot_free = [[q_stored, done, normed[-1], wv_split]] * PS
            for g in range(DT):
                heads = []
                for j in range(QUAD):
                    if g == 0:
                        done = project_values(CHUNKS - 1, 1, (j,))
                    second_half = scores(n, g, j)
                    if j == 0 and g + 1 < DT:
                        load_queries(n + 1, b, g + 1)
                    if g == 0 and j == QUAD - 1:
                        project_keys(CHUNKS - 1, 1, chunk_ready[number], (DT - 1,))
                        ctx_read[1] = T.last()
                    h = QUAD * g + j + STACKS - 1
                    if QUAD <= h < HEADS:
                        load_stack(n, h // QUAD, h % QUAD, split_done, None if h == QUAD else ctx_read[1])
                    finish_quad()
                    if pending:
                        heads.append(weighted_values(
                            *pending, quarter=j, meanwhile=second_half,
                            exponentiate=lambda negated, where=(n, g, j): exponentials(*where, negated)))
                    else:
                        heads.append(exponentials(n, g, j, second_half()))
                    if j == 1 and g + 1 < DT:
                        split_done = split_keys(g + 1, None)
                    if g == DT - 1 and b + 1 < B:
                        if j == 1:
                            ctx_loaded = load_ctx(b + 1, 0, list(keys_moved))
                        if j == QUAD - 1:
                            ctx_read[0] = [list(keys_moved), stack_read[0]]
                            ctx_read[1] = [stack_read[1], stack_read[2]]
                            chunk_ready[(b + 1) * CHUNKS] = split_chunk((b + 1) * CHUNKS)
                pending = (n, b, g, heads)
                n += 1
        s_gate, s_ifg = signal("gate_raw_in"), signal("ifg_raw_in")
        S.wait(ctx_read[0], ctx_read[1], stack_read, T.last())
        for n_, key in enumerate(("w_i_t", "w_f_t", "w_g_t")):
            ifg_loaded = S.dma(s_ifg, sp.dma_start, ifg_raw[:, n_], rows(a[key]))
        gate_loaded = S.dma(s_gate, sp.dma_start, gate_raw[:, :, :], rows(a["w_gate_t"]))
        finish_quad()
        weighted_values(*pending)
        finish_quad()

        wo_sb, x_again, attended_sb = view(0), view(1), view(2)
        s_wo = signal("wo_in")
        S.wait(slot_free[0], slot_free[1])
        wo_loaded = S.dma(s_wo, sp.dma_start, wo_sb, rows(a["wo"]))
        x_loaded = S.dma(s_x, sp.dma_start, x_again, a["x"].rearrange("b s d -> s b d"))
        s_again = signal("attended_in")
        S.wait(slot_free[2], attended_stored)
        attended_loaded = S.dma(s_again, sp.dma_start, attended_sb, attended.rearrange("(k p) t -> p k t", p=P))
        x1_ready = []
        for b in range(B):
            w = next_bank()
            T.wait(work_free[w], wo_loaded, attended_loaded)
            for g in range(DT):
                done = T.op(pe.matmul, psum[:, w, :], attended_sb[:, g, b * P:(b + 1) * P], wo_sb[:, g, :],
                            start=(g == 0), stop=(g == DT - 1))
            V.wait(done, x_loaded)
            m = work_free[w] = V.op(dve.tensor_tensor, x1[:, b, :], psum[:, w, :], x_again[:, b, :], ALU.add)
            x1_ready.append(m)
        attention_over = [q.last() for q in (T, V, A, G)]


        region_2 = ExitStack()
        MATS = ("i", "f", "g", "o", "gate", "down")
        NUMEL = {"i": D * D, "f": D * D, "g": D * D, "o": D * D, "gate": 2 * INNER * D, "down": INNER * D}
        tern = {n: sb("tern_" + n, [P, DT, D], BF16, region_2) for n in ("i", "f", "g", "o")}
        tern["gate"] = sb("tern_gate", [P, DT, 2 * INNER], BF16, region_2)
        tern["down"] = sb("tern_down", [P, IT, D], BF16, region_2)
        region_raw = ExitStack()
        o_raw = sb("o_raw", [P, DT, D], F32, region_raw)
        down_raw = sb("down_raw", [P, IT, D], F32, region_raw)
        region_raw.close()
        z_int = sb("z_int", [P, B, INNER], BF16, region_2)
        z_intT = sb("z_intT", [P, IT, B * P], BF16, region_2)
        sb("pad_raw", [P, 4 * (DT * D + IT * D) - 2 * (B * INNER + IT * B * P)], mybir.dt.uint8, region_2)
        resid = sb("resid", [P, B, D], F32, region_2)
        work = sb("work", [P, B, D], F32, region_2)
        q_int = sb("q_int", [P, B, D], BF16, region_2)
        q_intT = sb("q_intT", [P, DT, B * P], BF16, region_2)
        step_row = sb("step_row", [P, B * P], F32, region_2)
        scan = sb("scan", [P, 3, DT, B * P], F32, region_2)
        swish_g = scan[:, 0]
        junk = sb("junk", [P, INNER], BF16, region_2)
        spread = sb("spread", [P, P], F32, region_2)
        gains = sb("gains", [P, 3, D], F32, region_2)
        lower = sb("lower", [P, 3, DT], F32, region_2)
        wsum = sb("wsum", [P, len(MATS), 4], F32, region_2)
        wmean = sb("wmean", [P, 2, len(MATS)], F32, region_2)
        tok = sb("tok", [P, 6, B], F32, region_2)

        G.wait(*attention_over)
        V.wait(constants, *attention_over)
        A.wait(constants, *attention_over)
        S.wait(*attention_over)
        s_small, s_oraw, s_draw = signal("small_in"), signal("o_raw_in"), signal("down_raw_in")
        o_loaded = S.dma(s_oraw, sp.dma_start, o_raw[:, :, :], rows(a["w_o_t"]))
        down_loaded = S.dma(s_draw, sp.dma_start, down_raw[:, :, :], rows(a["w_down_t"]))
        for n_, key in enumerate(("attn_norm", "g_norm", "mlp_norm")):
            small = S.dma(s_small, sp.dma_start, gains[:, n_, :],
                          a[key].rearrange("(o d) -> o d", o=1).broadcast_to([P, D]))
        small = S.dma(s_small, sp.dma_start, lower[:, 0, :], a["lower"])

        raw = {"i": ifg_raw[:, 0], "f": ifg_raw[:, 1], "g": ifg_raw[:, 2], "o": o_raw[:, :, :],
               "gate": gate_raw[:, :, :], "down": down_raw[:, :, :]}
        raw_loaded = {"i": ifg_loaded, "f": ifg_loaded, "g": ifg_loaded, "gate": gate_loaded, "o": o_loaded,
                      "down": down_loaded}

        bank_free = [attention_over] * 8
        bank_turn = [0]

        def bank():
            bank_turn[0] += 1
            return bank_turn[0] % 8

        def abs_sums(mats):
            for n in mats:
                V.wait(raw_loaded[n])
                m = V.op(dve.tensor_reduce, wsum[:, MATS.index(n), 0:1], raw[n], AX.XY, ALU.add,
                         apply_absolute_value=True)
            return m

        def mean_abs(lo, hi, after):
            w = bank()
            T.wait(after, bank_free[w])
            m = T.op(pe.matmul, psum[:, w, lo:hi], ones[:, :], wsum[:, lo:hi, 0], start=True, stop=True)
            V.wait(m)
            for i in range(lo, hi):
                m = bank_free[w] = V.op(dve.tensor_scalar, wmean[:, 0, i:i + 1], psum[:, w, i:i + 1],
                                        1.0 / NUMEL[MATS[i]], 1e-5, ALU.mult, ALU.max)
            V.wait(m)
            return V.op(dve.reciprocal, wmean[:, 1, lo:hi], wmean[:, 0, lo:hi])

        def ternary(n, after, pieces=1):
            i = MATS.index(n)
            flat = lambda t: t.rearrange("p k n -> p (k n)")
            src, dst = flat(raw[n]), flat(tern[n][:, :, :])
            size = src.shape[1] // pieces
            for c in range(pieces):
                part = slice(c * size, (c + 1) * size)
                A.wait(after)
                m = A.op(act.activation, src[:, part], src[:, part], ACT.Identity, bias=magic[:, 0:1],
                         scale=wmean[:, 1, i:i + 1])
                V.wait(m)
                m = V.op(dve.tensor_scalar, dst[:, part], src[:, part], ROUND_MAGIC, 1.0, ALU.subtract, ALU.min)
                V.wait(m)
                m = V.op(dve.tensor_scalar, dst[:, part], dst[:, part], -1.0, None, ALU.max)
            return m

        def squares(key, src, width, marks):
            for b in range(B):
                A.wait(marks[b], A.last())
                m = A.op(act.activation, junk[:, 0:width], src(b), ACT.Square,
                         accum_out=scalars(key)[:, b:b + 1])
            return rsqrt_cols(scalars(key), scalars(key), 1.0 / width, 1e-6, m), m

        def quantize(key, src, dst, width, marks):
            rn, _ = squares(key + "_rn", src, width, marks)
            peak, quantum, factor = scalars(key + "_peak"), scalars(key + "_quantum"), scalars(key + "_factor")
            for b in range(B):
                V.wait(marks[b])
                m = V.op(dve.tensor_reduce, peak[:, b:b + 1], src(b), AX.X, ALU.max, apply_absolute_value=True)
            V.wait(m, rn)
            m = V.op(dve.tensor_tensor, peak, peak, scalars(key + "_rn"), ALU.mult)
            V.wait(m)
            step = m = V.op(dve.tensor_scalar, quantum, peak, 1e-5, 1.0 / 127.0, ALU.max, ALU.mult)
            V.wait(m)
            m = V.op(dve.reciprocal, factor, quantum)
            V.wait(m)
            m = V.op(dve.tensor_tensor, factor, factor, scalars(key + "_rn"), ALU.mult)
            out_marks = []
            for b in range(B):
                A.wait(m)
                m2 = A.op(act.activation, src(b), src(b), ACT.Identity, bias=magic[:, 0:1], scale=factor[:, b:b + 1])
                V.wait(m2)
                out_marks.append(V.op(dve.tensor_scalar, dst(b), src(b), ROUND_MAGIC, 127.0, ALU.subtract, ALU.min))
            return out_marks, quantum, step

        def turn_integers(dst, src, tiles, marks):
            done = []
            for b in range(B):
                for k0 in range(0, tiles, 4):
                    ks = range(k0, min(k0 + 4, tiles))
                    w = bank()
                    T.wait(marks[b], bank_free[w], constants)
                    half = psum[:, w, :].bitcast(BF16)
                    for k in ks:
                        m = T.op(pe.transpose, half[:, (k - k0) * P:(k - k0 + 1) * P], src(b)[:, k * P:(k + 1) * P],
                                 identb[:, :])
                    q = V if (b + k0 // 4) % 2 else A
                    q.wait(m)
                    args = (dst[:, k0:ks[-1] + 1, b * P:(b + 1) * P],
                            half[:, 0:len(ks) * P].rearrange("p (k t) -> p k t", t=P))
                    m = bank_free[w] = (V.op(dve.tensor_copy, *args) if q is V else A.op(act.copy, *args))
                done.append(m)
            return [[V.last(), A.last()]] * B

        def token_scale(i, quantum, mat, after):
            V.wait(after)
            k = MATS.index(mat)
            return V.op(dve.tensor_scalar, tok[:, i, :], quantum, wmean[:, 0, k:k + 1], None, ALU.mult)

        wsum_ready = mean_abs(0, 3, abs_sums(("i", "f", "g")))
        tern_ready = {n: ternary(n, wsum_ready) for n in ("i", "f")}
        resid_ready = layernorm(resid, x1, "rstd1", x1_ready)
        rr, _ = squares("rr", lambda b: resid[:, b, :], D, resid_ready)
        V.wait(rr, small)
        ready = [V.op(dve.scalar_tensor_tensor, work[:, b, :], resid[:, b, :], scalars("rr")[:, b:b + 1],
                      gains[:, 0, :], ALU.mult, ALU.mult) for b in range(B)]
        ready, quantum, step = quantize("qa", lambda b: work[:, b, :], lambda b: q_int[:, b, :], D, ready)
        turned = turn_integers(q_intT, lambda b: q_int[:, b, :], DT, ready)

        w = bank()
        for b in range(B):
            V.wait(step, V.last(), T.last())
            m = V.op(dve.tensor_copy, spread[:, :], quantum[:, b:b + 1].broadcast_to([P, P]))
            T.wait(m, bank_free[w])
            m = T.op(pe.transpose, psum[:, w, b * P:(b + 1) * P], spread[:, :], ident[:, :])
        A.wait(m)
        row_ready = bank_free[w] = A.op(act.copy, step_row[:, :], psum[:, w, :])
        tern_ready["g"] = ternary("g", wsum_ready)
        m = V.op(dve.tensor_scalar, lower[:, 1, :], lower[:, 0, :], -1.0, 1.0, ALU.mult, ALU.add)
        lower_ready = m

        state_ready = []
        for c in range(DT):
            raws = {}
            for n, place in (("f", 1), ("i", 0)):
                w = bank()
                T.wait(turned[0], tern_ready[n], bank_free[w])
                for k in range(DT):
                    m = T.op(pe.matmul, psum[:, w, :], tern[n][:, k, c * P:(c + 1) * P], q_intT[:, k, :],
                             start=(k == 0), stop=(k == DT - 1))
                V.wait(m, row_ready)
                raws[n] = bank_free[w] = V.op(
                    dve.scalar_tensor_tensor, scan[:, place, c, :], psum[:, w, :],
                    wmean[:, 0, MATS.index(n):MATS.index(n) + 1], step_row[:, :], ALU.mult, ALU.mult)
            A.wait(raws["f"])
            f = A.op(act.activation, scan[:, 1, c, :], scan[:, 1, c, :], ACT.Sigmoid)
            A.wait(raws["i"])
            si = A.op(act.activation, scan[:, 2, c, :], scan[:, 0, c, :], ACT.Sigmoid)
            V.wait(f, lower_ready)
            f = V.op(dve.tensor_scalar, scan[:, 1, c, :], scan[:, 1, c, :], lower[:, 1, c:c + 1],
                     lower[:, 0, c:c + 1], ALU.mult, ALU.add)
            V.wait(si)
            m = V.op(dve.tensor_tensor, scan[:, 0, c, :], scan[:, 0, c, :], scan[:, 2, c, :], ALU.mult)
            V.wait(f, m)
            m = V.op(dve.scalar_tensor_tensor, scan[:, 0, c, :], scan[:, 1, c, :], 1.0, scan[:, 0, c, :],
                     ALU.subtract, ALU.mult, reverse0=True)
            V.wait(m)
            for b in range(B):
                span = slice(b * P, (b + 1) * P)
                m = V.op(dve.tensor_tensor_scan, scan[:, 2, c, span], scan[:, 1, c, span], scan[:, 0, c, span], 0.0,
                         ALU.mult, ALU.add)
            state_ready.append(m)

        g_scaled = token_scale(0, quantum, "g", step)
        for b in range(B):
            w = bank()
            T.wait(turned[b], tern_ready["g"], bank_free[w])
            for k in range(DT):
                m = T.op(pe.matmul, psum[:, w, :], q_intT[:, k, b * P:(b + 1) * P], tern["g"][:, k, :],
                         start=(k == 0), stop=(k == DT - 1))
            A.wait(m, g_scaled, state_ready)
            m = A.op(act.activation, swish_g[:, b, :], psum[:, w, :], ACT.Sigmoid, scale=tok[:, 0, b:b + 1])
            V.wait(m)
            g_ready = bank_free[w] = V.op(dve.scalar_tensor_tensor, swish_g[:, b, :], psum[:, w, :],
                                          tok[:, 0, b:b + 1], swish_g[:, b, :], ALU.mult, ALU.mult)

        state_bank = [bank() for _ in range(B)]
        for b in range(B):
            T.wait(state_ready, bank_free[state_bank[b]])
            for c in range(DT):
                m = T.op(pe.transpose, psum[:, state_bank[b], c * P:(c + 1) * P], scan[:, 2, c, b * P:(b + 1) * P],
                         ident[:, :])
            state_ready[b] = m
        ro, squared = squares("ro", lambda b: psum[:, state_bank[b], :], D, state_ready)
        V.wait(ro, g_ready)
        ready = []
        for b in range(B):
            m = bank_free[state_bank[b]] = V.op(dve.scalar_tensor_tensor, work[:, b, :], psum[:, state_bank[b], :],
                                                scalars("ro")[:, b:b + 1], gains[:, 1, :], ALU.mult, ALU.mult)
            V.wait(m)
            ready.append(V.op(dve.tensor_tensor, work[:, b, :], work[:, b, :], swish_g[:, b, :], ALU.mult))
        wsum_ready = mean_abs(3, 6, abs_sums(("o", "gate", "down")))
        tern_ready["o"] = ternary("o", wsum_ready)
        ready, quantum, step = quantize("qo", lambda b: work[:, b, :], lambda b: q_int[:, b, :], D, ready)
        turned = turn_integers(q_intT, lambda b: q_int[:, b, :], DT, ready)
        o_scaled = token_scale(1, quantum, "o", step)

        def ternary_product(mat, srcT, tiles, scaled, i, marks):
            out_marks = []
            for b in range(B):
                w = bank()
                T.wait(marks[b], tern_ready[mat], bank_free[w])
                for k in range(tiles):
                    m = T.op(pe.matmul, psum[:, w, :], srcT[:, k, b * P:(b + 1) * P], tern[mat][:, k, :],
                             start=(k == 0), stop=(k == tiles - 1))
                V.wait(m, scaled)
                m = bank_free[w] = V.op(dve.scalar_tensor_tensor, resid[:, b, :], psum[:, w, :], tok[:, i, b:b + 1],
                                        resid[:, b, :], ALU.mult, ALU.add)
                out_marks.append(m)
            return out_marks

        resid_ready = ternary_product("o", q_intT, DT, o_scaled, 1, turned)

        rm, _ = squares("rm", lambda b: resid[:, b, :], D, resid_ready)
        V.wait(rm)
        ready = [V.op(dve.scalar_tensor_tensor, work[:, b, :], resid[:, b, :], scalars("rm")[:, b:b + 1],
                      gains[:, 2, :], ALU.mult, ALU.mult) for b in range(B)]
        tern_ready["gate"] = ternary("gate", wsum_ready, 4)
        ready, quantum, step = quantize("qm", lambda b: work[:, b, :], lambda b: q_int[:, b, :], D, ready)
        turned = turn_integers(q_intT, lambda b: q_int[:, b, :], DT, ready)
        gate_scaled = token_scale(2, quantum, "gate", step)
        tern_ready["down"] = ternary("down", wsum_ready, 2)
        raws_done = [V.last(), A.last()]
        z = scan[:, :, :, :].rearrange("p a c t -> p (a c t)")[:, 0:B * INNER].rearrange("p (b n) -> p b n", b=B)
        z_ready = []
        for b in range(B):
            for lo in range(0, INNER, BANK):
                n_ = min(BANK, INNER - lo)
                w_gate, w_up = bank(), bank()
                for w, base in ((w_gate, 0), (w_up, INNER)):
                    T.wait(turned[b], tern_ready["gate"], bank_free[w])
                    for k in range(DT):
                        m = T.op(pe.matmul, psum[:, w, 0:n_], q_intT[:, k, b * P:(b + 1) * P],
                                 tern["gate"][:, k, base + lo:base + lo + n_], start=(k == 0), stop=(k == DT - 1))
                A.wait(m, gate_scaled, state_ready)
                dst = z[:, b, lo:lo + n_]
                m = A.op(act.activation, dst, psum[:, w_gate, 0:n_], ACT.Sigmoid, scale=tok[:, 2, b:b + 1])
                V.wait(m)
                m = bank_free[w_gate] = V.op(dve.scalar_tensor_tensor, dst, psum[:, w_gate, 0:n_],
                                             tok[:, 2, b:b + 1], dst, ALU.mult, ALU.mult)
                V.wait(m)
                m = bank_free[w_up] = V.op(dve.scalar_tensor_tensor, dst, psum[:, w_up, 0:n_], tok[:, 2, b:b + 1],
                                           dst, ALU.mult, ALU.mult)
            z_ready.append(m)
        V.wait(raws_done)
        ready, quantum, step = quantize("qz", lambda b: z[:, b, :], lambda b: z_int[:, b, :], INNER, z_ready)
        turned = turn_integers(z_intT, lambda b: z_int[:, b, :], IT, ready)
        z_scaled = token_scale(3, quantum, "down", step)
        resid_ready = ternary_product("down", z_intT, IT, z_scaled, 3, turned)
        x2_ready = []
        for b in range(B):
            V.wait(resid_ready[b])
            x2_ready.append(V.op(dve.tensor_tensor, x1[:, b, :], x1[:, b, :], resid[:, b, :], ALU.add))
        region_2.close()
        x1_ready = x2_ready


        phase2_over = [q.last() for q in (T, V, A, G)]
        wslot += [sb(f"wslot{i}", [P, DT * HID], F32) for i in range(2, WSLOTS)]
        xm = sb("xm", [P, B, D], F32)
        xm_hi = sb("xm_hi", [P, B, D], F32R)
        xm_lo = sb("xm_lo", [P, B, D], F32R)
        route = ExitStack()
        xmT = sb("xmT", [P, DT, B * P], F32, route)
        route.close()
        hidden = sb("hidden", [P, HT, SLOTS], F32)
        wr = sb("wr", [P, DT, EXPERTS], F32)
        br = sb("br", [P, EXPERTS], F32)
        b1 = sb("b1", [P, EXPERTS, HT], F32)
        b2 = sb("b2", [EXPERTS, D], F32)
        iota_e = sb("iota_e", [P, EXPERTS], F32)
        iota_s = sb("iota_s", [P, SLOTS], F32)
        before = sb("before", [P, P], BF16)
        onesb = sb("onesb", [P, P], BF16)
        logits = sb("logits", [P, B, EXPERTS], F32)
        best = sb("best", [P, B, 8], F32)
        best_at = sb("best_at", [P, B, 8], U32)
        best_atf = sb("best_atf", [P, B, 2], F32)
        gates2 = sb("gates2", [P, B, 4], F32)
        onehot = sb("onehot", [P, B, 2, EXPERTS], F32)
        gate = sb("gate", [P, B, EXPERTS], F32)
        gateT = sb("gateT", [EXPERTS, B * P], F32)
        chosen = sb("chosen", [P, B, EXPERTS], F32)
        chosenb = sb("chosenb", [P, B, EXPERTS], BF16)
        place = sb("place", [P, B, EXPERTS], F32)
        load = sb("load", [P, 1], I32)
        pick = sb("pick", [P, 2, B, 2, SLOTS], F32R)
        picked = sb("picked", [P, 2, DT, SLOTS], F32)
        pickT = sb("pickT", [P, 2, B * P], F32R)
        slot_gate = sb("slot_gate", [P, 2, 2], F32)
        yT = sb("yT", [P, DT, SLOTS], F32)
        y_hi = sb("y_hi", [P, 2, D], F32R)
        y_lo = sb("y_lo", [P, 2, D], F32R)

        STILES = [(st, min(P, SLOTS - st * P)) for st in range(-(-SLOTS // P))]
        s_w = [signal(f"weights{i}_in") for i in range(WSLOTS)]
        w_free = [raws_done, raws_done, phase2_over, phase2_over]
        w_turn = [0]

        def load_weights(source):
            i = w_turn[0] % WSLOTS
            w_turn[0] += 1
            S.wait(w_free[i])
            return i, S.dma(s_w[i], sp.dma_start, wslot[i][:, :].rearrange("p (k n) -> p k n", n=source.shape[1]),
                            source.rearrange("(k p) n -> p k n", p=P))

        def expert_loads(e):
            return load_weights(a["w1"][e]), load_weights(a["w2"][e])

        loads = {(0, 0): expert_loads(0)}
        S.wait(phase2_over)
        s_route = signal("router_in")
        S.dma(s_route, sp.dma_start, wr[:, :, :], a["wr"].rearrange("(k p) e -> p k e", p=P))
        S.dma(s_route, sp.dma_start, br[:, :], a["br"].rearrange("(o e) -> o e", o=1).broadcast_to([P, EXPERTS]))
        S.dma(s_route, sp.dma_start, b1[:, :, :], a["b1_t"])
        route_loaded = S.dma(s_route, sp.dma_start, b2[:, :], a["b2"])
        loads[0, 1] = expert_loads(1)

        G.wait(phase2_over)
        A.wait(phase2_over)
        V.wait(phase2_over)
        G.op(pool.iota, iota_e[:, :], [[1, EXPERTS]], base=0, channel_multiplier=0,
             allow_small_or_imprecise_dtypes=True)
        G.op(pool.iota, iota_s[:, :], [[1, SLOTS]], base=1, channel_multiplier=0,
             allow_small_or_imprecise_dtypes=True)
        m = G.op(pool.memset, onesb[:, :], 1.0)
        G.wait(m)
        route_constants = G.op(pool.affine_select, out=before[:, :], in_=onesb[:, :], compare_op=ALU.is_gt, fill=0.0,
                               base=0, pattern=[[1, P]], channel_multiplier=-1)

        OUT = range(4)
        RING = (4, 5, 6, 7)
        bank_free = {w: phase2_over for w in range(8)}
        ring_turn = [0]

        def ring():
            ring_turn[0] += 1
            return RING[ring_turn[0] % len(RING)]

        normed = layernorm(xm, x1, "rstd2", x2_ready)
        for b in range(B):
            w = ring()
            m = bank_free[w] = transpose_tile(xmT[:, :, b * P:(b + 1) * P], xm[:, b, :], w, normed[b], bank_free[w],
                                              A)
            xmT_ready = m
        w = ring()
        T.wait(xmT_ready, route_loaded, bank_free[w])
        for b in range(B):
            for k in range(DT):
                m = T.op(pe.matmul, psum[:, w, b * EXPERTS:(b + 1) * EXPERTS], xmT[:, k, b * P:(b + 1) * P],
                         wr[:, k, :], start=(k == 0), stop=(k == DT - 1))
        V.wait(m, route_constants)
        for b in range(B):
            m = V.op(dve.tensor_tensor, logits[:, b, :], psum[:, w, b * EXPERTS:(b + 1) * EXPERTS], br[:, :], ALU.add)
        routed = bank_free[w] = m
        V.wait(m)
        for b in range(B):
            m = V.op(dve.max, best[:, b, :], logits[:, b, :])
        V.wait(m)
        diff = V.op(dve.tensor_tensor, gates2[:, :, 0], best[:, :, 1], best[:, :, 0], ALU.subtract)
        for b in range(B):
            m = V.op(dve.max_index, best_at[:, b, :], best[:, b, :], logits[:, b, :])
        A.wait(diff)
        expd = A.op(act.activation, gates2[:, :, 1], gates2[:, :, 0], ACT.Exp)
        V.wait(m)
        m = V.op(dve.tensor_copy, best_atf[:, :, :], best_at[:, :, 0:2])
        V.wait(m)
        for b in range(B):
            for i in range(2):
                m = V.op(dve.tensor_scalar, onehot[:, b, i, :], iota_e[:, :], best_atf[:, b, i:i + 1], None,
                         ALU.is_equal)
        V.wait(m)
        m = V.op(dve.tensor_tensor, chosen[:, :, :], onehot[:, :, 0, :], onehot[:, :, 1, :], ALU.add)
        V.wait(m)
        chosen_ready = V.op(dve.tensor_copy, chosenb[:, :, :], chosen[:, :, :])
        V.wait(expd)
        m = V.op(dve.tensor_scalar, gates2[:, :, 2], gates2[:, :, 1], 1.0, None, ALU.add)
        V.wait(m)
        m = V.op(dve.reciprocal, gates2[:, :, 2], gates2[:, :, 2])
        V.wait(m)
        m = V.op(dve.tensor_tensor, gates2[:, :, 3], gates2[:, :, 1], gates2[:, :, 2], ALU.mult)
        V.wait(m)
        for b in range(B):
            m = V.op(dve.tensor_scalar, gate[:, b, :], onehot[:, b, 0, :], gates2[:, b, 2:3], None, ALU.mult)
        V.wait(m)
        for b in range(B):
            m = V.op(dve.scalar_tensor_tensor, gate[:, b, :], onehot[:, b, 1, :], gates2[:, b, 3:4], gate[:, b, :],
                     ALU.mult, ALU.add)
        gate_ready = m

        w = ring()
        T.wait(chosen_ready, bank_free[w])
        for b in range(B):
            for earlier in range(b):
                T.quiet(pe.matmul, psum[:, w, b * EXPERTS:(b + 1) * EXPERTS], onesb[:, :], chosenb[:, earlier, :],
                        start=(earlier == 0), stop=False)
            T.quiet(pe.matmul, psum[:, w, b * EXPERTS:(b + 1) * EXPERTS], before[:, :], chosenb[:, b, :],
                    start=(b == 0), stop=True)
        for b in range(B):
            m = T.op(pe.matmul, psum[:, w, B * EXPERTS:(B + 1) * EXPERTS], onesb[:, :], chosenb[:, b, :],
                     start=(b == 0), stop=(b == B - 1))
        V.wait(m)
        m = V.op(dve.scalar_tensor_tensor, place[:, :, :].rearrange("p b e -> p (b e)"), psum[:, w, 0:B * EXPERTS],
                 1.0, chosen[:, :, :].rearrange("p b e -> p (b e)"), ALU.add, ALU.mult)
        place_ready = m
        load_ready = bank_free[w] = V.op(dve.tensor_reduce, load[:, :], psum[:, w, B * EXPERTS:(B + 1) * EXPERTS],
                                         AX.X, ALU.max)
        V.wait(normed)
        m = V.op(dve.tensor_copy, xm_hi[:, :, :], xm[:, :, :])
        V.wait(m)
        xm_ready = V.op(dve.tensor_tensor, xm_lo[:, :, :], xm[:, :, :], xm_hi[:, :, :].bitcast(F32), ALU.subtract)
        w = ring()
        T.wait(gate_ready, bank_free[w])
        for b in range(B):
            m = T.op(pe.transpose, psum[0:EXPERTS, w, b * P:(b + 1) * P], gate[:, b, :], ident[:, :])
        A.wait(m)
        gateT_ready = bank_free[w] = A.op(act.copy, gateT[:, :], psum[0:EXPERTS, w, :])

        class Last:
            pick = [None, None]
            picked = [None, None]
            pickT = slot_gate = hidden = yT = y = None

        def gather(pair, r, half):
            for b in range(B):
                for i in range(2):
                    V.wait(place_ready, Last.pick[half])
                    e = 2 * pair + i
                    picks = V.op(dve.tensor_scalar, pick[:, half, b, i, :], iota_s[:, :], float(r * SLOTS),
                                 place[:, b, e:e + 1], ALU.add, ALU.is_equal)
            for k in range(DT):
                w = ring()
                T.wait(picks, xm_ready, bank_free[w])
                for b in range(B):
                    for part in (xm_hi, xm_lo):
                        m = T.op(pe.matmul, psum[:, w, 0:2 * SLOTS], part[:, b, k * P:(k + 1) * P],
                                 pick[:, half, b, :, :].rearrange("p i s -> p (i s)"),
                                 start=(b == 0 and part is xm_hi), stop=(b == B - 1 and part is xm_lo))
                A.wait(m, Last.picked)
                m = bank_free[w] = A.op(act.copy, picked[:, :, k, :],
                                        psum[:, w, 0:2 * SLOTS].rearrange("p (i s) -> p i s", i=2))
            return m

        def hidden_layer(e, i, slot_mark, gathered):
            slot, loaded = slot_mark
            w1 = wslot[slot][:, :].rearrange("p (k n) -> p k n", k=DT)
            marks = []
            for h in range(HT):
                w = ring()
                T.wait(loaded, gathered, bank_free[w])
                for k in range(DT):
                    m = T.op(pe.matmul, psum[:, w, 0:SLOTS], w1[:, k, h * P:(h + 1) * P], picked[:, i, k, :],
                             start=(k == 0), stop=(k == DT - 1))
                if h % 2:
                    A.wait(m, Last.hidden)
                    m2 = A.op(act.activation, hidden[:, h, :], psum[:, w, 0:SLOTS], ACT.Relu, bias=b1[:, e, h:h + 1])
                else:
                    V.wait(m, Last.hidden)
                    m2 = V.op(dve.tensor_scalar, hidden[:, h, :], psum[:, w, 0:SLOTS], b1[:, e, h:h + 1], 0.0,
                              ALU.add, ALU.max)
                bank_free[w] = m2
                marks.append(m2)
            w_free[slot] = Last.picked[i] = m
            return marks

        def output_layer(slot_mark, hidden_ready):
            slot, loaded = slot_mark
            w2 = wslot[slot][:, :].rearrange("p (h n) -> p h n", h=HT)
            for k in range(DT):
                w = ring()
                T.wait(loaded, bank_free[w])
                for h in range(HT):
                    T.wait(hidden_ready[h])
                    m = T.op(pe.matmul, psum[:, w, 0:SLOTS], w2[:, h, k * P:(k + 1) * P], hidden[:, h, :],
                             start=(h == 0), stop=(h == HT - 1))
                q = A if k % 2 else V
                q.wait(m, Last.yT)
                out_mark = bank_free[w] = (A.op(act.copy, yT[:, k, :], psum[:, w, 0:SLOTS]) if q is A else
                                           V.op(dve.tensor_copy, yT[:, k, :], psum[:, w, 0:SLOTS]))
            w_free[slot] = Last.hidden = m
            return [V.last(), A.last()]

        first_scatter = [True]

        def slot_tables(e, i, half):
            for st, rows_ in STILES:
                w = ring()
                T.wait(bank_free[w])
                for b in range(B):
                    m = T.op(pe.transpose, psum[0:rows_, w, b * P:(b + 1) * P],
                             pick[:, half, b, i, st * P:st * P + rows_].bitcast(F32), ident[:, :])
                V.wait(m, Last.pickT)
                bank_free[w] = V.op(dve.tensor_copy, pickT[0:rows_, st, :], psum[0:rows_, w, :])
            w = ring()
            T.wait(gate_ready, bank_free[w])
            for st, rows_ in STILES:
                for b in range(B):
                    m = T.op(pe.matmul, psum[0:rows_, w, st:st + 1],
                             pick[:, half, b, i, st * P:st * P + rows_].bitcast(F32), gate[:, b, e:e + 1],
                             start=(b == 0), stop=(b == B - 1))
            Last.pick[half] = m
            V.wait(m, Last.slot_gate)
            for st, rows_ in STILES:
                m = bank_free[w] = V.op(dve.tensor_copy, slot_gate[0:rows_, st, i:i + 1], psum[0:rows_, w, st:st + 1])
            return m

        def scatter(i, yT_ready, tables):
            for st, rows_ in STILES:
                w = ring()
                T.wait(yT_ready, bank_free[w])
                for k in range(DT):
                    m = Last.yT = T.op(pe.transpose, psum[0:rows_, w, k * P:(k + 1) * P],
                                       yT[:, k, st * P:st * P + rows_], ident[:, :])
                A.wait(m, tables, Last.y)
                m = A.op(act.activation, y_hi[0:rows_, st, :], psum[0:rows_, w, :], ACT.Copy,
                         scale=slot_gate[0:rows_, st, i:i + 1])
                V.wait(m, Last.y)
                m = bank_free[w] = V.op(dve.scalar_tensor_tensor, y_lo[0:rows_, st, :], psum[0:rows_, w, :],
                                        slot_gate[0:rows_, st, i:i + 1], y_hi[0:rows_, st, :].bitcast(F32),
                                        ALU.mult, ALU.subtract)
            Last.slot_gate = m
            T.wait(m)
            for b in OUT:
                T.wait(bank_free[b])
                for st, rows_ in STILES:
                    for part in (y_hi, y_lo):
                        m = T.op(pe.matmul, psum[:, b, :], pickT[0:rows_, st, b * P:(b + 1) * P],
                                 part[0:rows_, st, :], start=(first_scatter[0] and st == 0 and part is y_hi),
                                 stop=False, skip_group_check=True)
            first_scatter[0] = False
            Last.y = Last.pickT = m

        def experts_round(r, preloaded):
            waiting = None
            for pair in range(EXPERTS // 2):
                half = pair % 2
                gathered = gather(pair, r, half)
                for i in range(2):
                    e = 2 * pair + i
                    w1_mark, w2_mark = preloaded.pop((r, e)) if (r, e) in preloaded else expert_loads(e)
                    hidden_ready = hidden_layer(e, i, w1_mark, gathered)
                    if waiting:
                        scatter(*waiting)
                    tables = slot_tables(e, i, half)
                    yT_ready = output_layer(w2_mark, hidden_ready)
                    if e + 2 < EXPERTS:
                        preloaded[r, e + 2] = expert_loads(e + 2)
                    waiting = (i, yT_ready, tables)
            scatter(*waiting)

        experts_round(0, loads)

        everyone = (T, V, A, G, S)
        state = [q.last() for q in (T, V, A, G)]
        known = {q: dict(q.waited) for q in everyone}
        for q, name in zip(everyone, ("tensor", "vector", "scalar", "gpsimd", "sync")):
            q.wait(load_ready)
            q.branch = len(q.steps)
            known[q] = dict(q.waited)
            q.done = signal(name + "_extra_done")
        s_w = [signal(f"extra_weights{i}_in") for i in range(WSLOTS)]
        saved_bank_free = dict(bank_free)
        for r in range(1, ROUNDS):
            loads = {(r, 0): expert_loads(0), (r, 1): expert_loads(1)}
            experts_round(r, loads)
        for q, name in zip(everyone, ("tensor", "vector", "scalar", "gpsimd", "sync")):
            q.join = len(q.steps)
            q.waited = known[q]
            q.done = signal(name + "_end_done")

        T.wait(gateT_ready, route_loaded)
        out_ready = []
        for b in OUT:
            m = T.op(pe.matmul, psum[:, b, :], gateT[:, b * P:(b + 1) * P], b2[:, :], start=False, stop=True,
                     skip_group_check=True)
            V.wait(m)
            out_ready.append(V.op(dve.tensor_tensor, x1[:, b, :], psum[:, b, :], x1[:, b, :], ALU.add))
        s_out = signal("out_stored")
        for b in range(B):
            S.wait(out_ready[b])
            stored = S.dma(s_out, sp.dma_start, out[b], x1[:, b, :])
        S.wait(stored)

        block = life.enter_context(nc.Block())

        @block.tensor
        def _(engine):
            T.replay(engine, load[0:1, 0:1])

        @block.vector
        def _(engine):
            V.replay(engine, load[0:1, 0:1])

        @block.scalar
        def _(engine):
            A.replay(engine, load[0:1, 0:1])

        @block.gpsimd
        def _(engine):
            G.replay(engine, load[0:1, 0:1])

        @block.sync
        def _(engine):
            S.replay(engine, load[0:1, 0:1])


def lay_out(i):
    import numpy as np
    c = lambda t: np.ascontiguousarray(np.asarray(t))
    return {
        "x": c(i["x"]), "ctx_t": c(np.asarray(i["ctx_1024"]).transpose(0, 2, 1)),
        "bias": c(np.asarray(i["fside_1x1xSxS2_0"]).reshape(P, KEYS)),
        "wq": c(i["L0_xattn_Wq"]), "wk": c(i["L0_xattn_Wk"]), "wv": c(i["L0_xattn_Wv"]), "wo": c(i["L0_xattn_Wo"]),
        "attn_norm": c(i["L0_attn_attn_norm_w"]), "g_norm": c(i["L0_attn_g_norm_w"]),
        "mlp_norm": c(i["L0_attn_mlp_norm_w"]), "lower": c(np.asarray(i["L0_attn_lower_bound"]).reshape(DT, P).T),
        "wr": c(i["L0_ffn_Wr"]), "br": c(i["L0_ffn_br"]), "w1": c(i["L0_ffn_W1"]), "w2": c(i["L0_ffn_W2"]),
        "b1_t": c(np.asarray(i["L0_ffn_b1"]).reshape(EXPERTS, HT, P).transpose(2, 0, 1)), "b2": c(i["L0_ffn_b2"]),
        "w_i_t": c(np.asarray(i["L0_attn_w_i"]).T), "w_f_t": c(np.asarray(i["L0_attn_w_f"]).T),
        "w_g_t": c(np.asarray(i["L0_attn_w_g"]).T), "w_o_t": c(np.asarray(i["L0_attn_w_o"]).T),
        "w_gate_t": c(np.asarray(i["L0_attn_w_gate"]).T), "w_down_t": c(np.asarray(i["L0_attn_w_down"]).T),
    }


def kernel(**inputs):
    import concourse.bacc as bacc
    from concourse.bass_utils import run_bass_kernel_spmd

    nc = bacc.Bacc("TRN2", target_bir_lowering=False, num_devices=1, dynamic_dma_scratch_size=1024)
    arrays = {f"in_{name}": t for name, t in lay_out(inputs).items()}
    args = {name[3:]: nc.dram_tensor(name, t.shape, mybir.dt.from_np(t.dtype), kind="ExternalInput").ap()
            for name, t in arrays.items()}
    out = nc.dram_tensor("out_x", (B, P, D), F32, kind="ExternalOutput").ap()
    perceiver_block(nc, args, out)
    return run_bass_kernel_spmd(nc, [arrays], core_ids=[0]).results[0]["out_x"]
```

```python
from contextlib import ExitStack

import concourse.bass as bass
from concourse import mybir

F32 = mybir.dt.float32
F32R = mybir.dt.float32r
BF16 = mybir.dt.bfloat16
I32 = mybir.dt.int32
U32 = mybir.dt.uint32
ALU = mybir.AluOpType
ACT = mybir.ActivationFunctionType
AX = mybir.AxisListType

P = 128
B = 4
D = 512
DT = D // P
KEYS = 2048
HEADS = 16
DH = D // HEADS
QUAD = P // DH
CHUNK = 512
KTILES = KEYS // P
INNER = 1408
IT = INNER // P
CHUNKS = KEYS // CHUNK
BANK = 512
EXPERTS = 8
HID = 2048
HT = HID // P
STACKS = 3
PARTS = 3
SLOTS = 192
FEWER = tuple(range(P, SLOTS, 16))
ROUNDS = -(-B * P // SLOTS)
ROUND_MAGIC = 1.5 * 2.0 ** 23
LOWEST = -3.0e38
MATS = ("i", "f", "g", "o", "gate", "down")
COLS = {"i": DT * D, "f": DT * D, "g": DT * D, "o": DT * D, "gate": DT * 2 * INNER, "down": IT * D}
FIRST = {mat: sum(COLS[m] for m in MATS[:i]) for i, mat in enumerate(MATS)}
TERN_COLS = sum(COLS.values())
GROUPS = ((0,), (1,), (2,), (3,))


class Signal:

    def __init__(self, sem):
        self.sem = sem
        self.count = 0


EITHER = "either"


def narrowed(step, columns):
    method, args, named, signal, by = step
    if method is None:
        return step
    return (method, tuple(arg[:, 0:columns] if arg.shape[-1] == SLOTS else arg for arg in args), named, signal, by)


class Queue:

    def __init__(self, done):
        self.done = done
        self.steps = []
        self.waited = {}
        self.count_step = None
        self.branch = self.join = None

    def wait(self, *marks):
        for mark in marks:
            if mark is None:
                continue
            if isinstance(mark, list):
                self.wait(*mark)
                continue
            signal, count = mark
            if self.waited.get(id(signal), 0) < count:
                self.waited[id(signal)] = count
                self.steps.append((None, (signal, count), None, None, 0))

    def quiet(self, method, *args, **named):
        self.steps.append((method, args, named, None, 0))

    def begin_either(self):
        self.either = len(self.steps)

    def end_either(self, expert):
        inside = self.steps[self.either:]
        del self.steps[self.either:]
        self.steps.append((EITHER, inside, expert, None, 0))

    def op(self, method, *args, **named):
        self.steps.append((method, args, named, self.done, 1))
        self.done.count += 1
        return (self.done, self.done.count)

    def dma(self, signal, method, *args, **named):
        self.steps.append((method, args, named, signal, 16))
        signal.count += 16
        return (signal, signal.count)

    def last(self):
        return (self.done, self.done.count) if self.done.count else None

    def emit_either(self, engine, steps, tokens, widths):
        if not widths:
            self.emit(engine, steps)
            return
        with engine.If_cmp(tokens, widths[0], "IS_LE"):
            self.emit(engine, [narrowed(step, widths[0]) for step in steps])
        with engine.If_cmp(tokens, widths[0], "IS_GT"):
            self.emit_either(engine, steps, tokens, widths[1:])

    def emit(self, engine, steps):
        for method, args, named, signal, by in steps:
            if method is None:
                engine.wait_ge(args[0].sem, args[1])
                continue
            if method is EITHER:
                self.emit_either(engine, args, self.counts[named], FEWER)
                continue
            made = method(*args, **named)
            if signal is not None:
                made.then_inc(signal.sem, by)

    def replay(self, engine, load, counts):
        with ExitStack() as registers:
            self.counts = []
            if self.count_step is None:
                self.emit(engine, self.steps[:self.branch])
            else:
                self.emit(engine, self.steps[:self.count_step])
                for e in range(EXPERTS):
                    self.counts.append(registers.enter_context(engine.register(f"tokens{e}")))
                    engine.reg_load(self.counts[e], counts[0:1, e:e + 1])
                self.emit(engine, self.steps[self.count_step:self.branch])
        with engine.register("fullest") as fullest:
            engine.reg_load(fullest, load)
            with engine.If_cmp(fullest, SLOTS, "IS_GT"):
                self.emit(engine, self.steps[self.branch:self.join])
        self.emit(engine, self.steps[self.join:])


def perceiver_block(nc, a, out):
    with ExitStack() as life:
        def sb(name, shape, dt, stack=life):
            return stack.enter_context(nc.sbuf_tensor(name, shape, dt))

        def signal(name):
            return Signal(life.enter_context(nc.semaphore(name)))

        pe, dve, act, pool, sp = nc.tensor, nc.vector, nc.scalar, nc.gpsimd, nc.sync
        T = Queue(signal("tensor_done"))
        V = Queue(signal("vector_done"))
        A = Queue(signal("scalar_done"))
        G = Queue(signal("gpsimd_done"))
        S = Queue(signal("sync_done"))

        psum = life.enter_context(nc.psum_tensor("psum", [P, 8, BANK], F32))

        ident = sb("ident", [P, P], F32)
        identb = sb("identb", [P, P], BF16)
        region_bias = ExitStack()
        biasmap = sb("biasmap", [P, KEYS], F32, region_bias)
        region_bias.close()
        x1 = sb("x1", [P, B, D], F32)
        stats = sb("stats", [P, B, 6], F32)
        meanvar = sb("meanvar", [P, B, 2], F32)
        minus_half = sb("minus_half", [P, B], F32)
        ones = sb("ones", [P, P], F32)
        magic = sb("magic", [P, 2], F32)
        wsum = sb("wsum", [P, 4], F32)
        wmean = sb("wmean", [P, 2, len(MATS)], F32)
        col = sb("col", [P, 48, B], F32)
        names = {}

        def scalars(name):
            names.setdefault(name, len(names))
            assert len(names) <= 48
            return col[:, names[name], :]

        def cols(column, group):
            return column[:, group[0]:group[-1] + 1]

        m = G.op(pool.memset, ident[:, :], 0.0)
        G.wait(m)
        m = G.op(pool.affine_select, out=ident[:, :], in_=ident[:, :], compare_op=ALU.not_equal, fill=1.0, base=0,
                 pattern=[[-1, P]], channel_multiplier=1)
        G.wait(m)
        m = G.op(pool.tensor_copy, identb[:, :], ident[:, :])
        G.op(pool.memset, ones[:, :], 1.0)
        G.op(pool.memset, magic[:, 0:1], ROUND_MAGIC)
        G.op(pool.memset, magic[:, 1:2], -ROUND_MAGIC)
        constants = G.op(pool.memset, minus_half[:, :], -0.5)

        def rsqrt_cols(dst, src, scale, eps, after):
            G.wait(after, constants)
            m = G.op(pool.tensor_scalar, dst, src, scale, eps, ALU.mult, ALU.add)
            G.wait(m)
            return G.op(pool.tensor_tensor, dst, dst, minus_half[:, 0:dst.shape[1]], ALU.pow)

        def layernorm(dst, src, key, after):
            rstd = scalars(key)
            ready = []
            for group in GROUPS:
                for b in group:
                    V.wait(after[b], V.last())
                    m = V.op(dve.bn_stats, stats[:, b, :], src[:, b, :])
                    V.wait(m)
                    m = V.op(dve.bn_aggr, meanvar[:, b, :], stats[:, b, :])
                ready.append(rsqrt_cols(cols(rstd, group), meanvar[:, group[0]:group[-1] + 1, 1], 1.0, 1e-5, m))
            marks = []
            for group, m in zip(GROUPS, ready):
                V.wait(m)
                marks += [V.op(dve.tensor_scalar, dst[:, b, :], src[:, b, :], meanvar[:, b, 0:1], rstd[:, b:b + 1],
                               ALU.subtract, ALU.mult) for b in group]
            return marks

        def transpose_tile(dst, src, bank, after, bank_free, copier):
            T.wait(after, bank_free, constants)
            for k in range(DT):
                m = T.op(pe.transpose, psum[:, bank, k * P:(k + 1) * P], src[:, k * P:(k + 1) * P], ident[:, :])
            copied = psum[:, bank, :].rearrange("p (k t) -> p k t", k=DT)
            copier.wait(m)
            if copier is A:
                return A.op(act.copy, dst, copied)
            return V.op(dve.tensor_copy, dst, copied)

        region_kv, region_f, region_r = ExitStack(), ExitStack(), ExitStack()
        kT = sb("kT", [P, DT, KEYS], F32, region_kv)
        v = sb("v", [P, KTILES, D], F32, region_kv)
        region_kv.close()
        WSLOTS = 4
        wslot = [sb(f"wslot{i}", [P, DT * HID], F32) for i in range(2)]
        ternary = sb("ternary", [P, TERN_COLS], BF16, region_f)
        region_f.close()
        wk_hi = sb("wk_hi", [P, DT, D], F32R, region_r)
        wk_lo = sb("wk_lo", [P, DT, D], F32R, region_r)
        wv_hi = sb("wv_hi", [P, DT, D], F32R, region_r)
        wv_lo = sb("wv_lo", [P, DT, D], F32R, region_r)
        region_c = ExitStack()
        ctx_raw = sb("ctx_raw", [P, DT, CHUNK], F32, region_c)
        ctx_part = sb("ctx_part", [P, 2, 2, DT, CHUNK], F32R, region_c)
        region_c.close()
        keys_hi = sb("keys_hi", [P, KEYS], F32R, region_r)
        keys_lo = sb("keys_lo", [P, KEYS], F32R, region_r)
        stack = sb("stack", [P, STACKS, KEYS], F32R, region_r)

        PS = 2 * QUAD
        region_p = ExitStack()
        early_stack = sb("early_stack", [P, PS, KEYS], F32R, region_p)
        region_p.close()
        prob = sb("prob", [P, PS, KEYS], F32, region_r)
        qstack = sb("qstack", [P, 2, QUAD, P], F32R, region_r)
        oT = sb("oT", [P, 2, P], F32, region_r)
        PTS = 3
        probT = sb("probT", [P, PTS, QUAD * P], F32, region_r)
        top = sb("top", [P, HEADS, 4], F32, region_r)
        rinv = sb("rinv", [P, 2, QUAD], F32, region_r)
        rbc = sb("rbc", [P, P], F32, region_r)
        rT = sb("rT", [P, P], F32, region_r)
        region_r.close()

        view = lambda slot: prob[:, slot, :].rearrange("p (k n) -> p k n", k=DT)
        wq_sb, wk_sb, wv_sb, xhT, x_in, q_all, q_hi, q_lo = (view(s) for s in range(8))
        q_parts = nc.dram_tensor("q_parts", (2, D, B * P), F32, kind="Internal").ap()
        ternary_dram = nc.dram_tensor("ternary_weights", (P, TERN_COLS), BF16, kind="Internal").ap()
        attended = nc.dram_tensor("attended", (D, B * P), F32, kind="Internal").ap()
        rows = lambda w: w.rearrange("(k p) n -> p k n", p=P)

        s_x, s_wq, s_wk, s_wv, s_bias, s_ctx = (signal(n) for n in
                                                ("x_in", "wq_in", "wk_in", "wv_in", "bias_in", "ctx_in"))
        wk_loaded = S.dma(s_wk, sp.dma_start, wk_sb, rows(a["wk"]))

        def load_ctx(b, c, free):
            S.wait(free)
            return S.dma(s_ctx, sp.dma_start, ctx_raw[:, :, :],
                         a["ctx_t"][b].rearrange("(k p) n -> p k n", p=P)[:, :, c * CHUNK:(c + 1) * CHUNK])

        ctx_loaded = load_ctx(0, 0, None)
        wv_loaded = S.dma(s_wv, sp.dma_start, wv_sb, rows(a["wv"]))
        wq_loaded = S.dma(s_wq, sp.dma_start, wq_sb, rows(a["wq"]))
        x_loaded = S.dma(s_x, sp.dma_start, x_in, a["x"].rearrange("b s d -> s b d"))
        bias_loaded = S.dma(s_bias, sp.dma_start, biasmap[:, :], a["bias"])

        def split(hi, lo, raw, after):
            V.wait(after)
            m = V.op(dve.tensor_copy, hi, raw)
            V.wait(m)
            return V.op(dve.tensor_tensor, lo, raw, hi.bitcast(F32), ALU.subtract)

        wk_split = split(wk_hi[:, :, :], wk_lo[:, :, :], wk_sb, wk_loaded)
        WORK = (4, 5, 6)
        OUT_BANK = 7
        work_free = {w: None for w in WORK}
        turn = [0]

        def next_bank():
            w = WORK[turn[0] % len(WORK)]
            turn[0] += 1
            return w

        kT_read = [None] * DT
        v_read = [None] * KTILES
        ctx_read = [None, None]
        kT_ready = {}
        v_ready = {}

        def project_keys(c, half, ready, tiles=range(DT)):
            for m in tiles:
                w = next_bank()
                T.wait(work_free[w], ready, wk_split)
                for k in range(DT):
                    wh, wl = wk_hi[:, k, m * P:(m + 1) * P], wk_lo[:, k, m * P:(m + 1) * P]
                    T.quiet(pe.matmul, psum[:, w, :], wh, ctx_part[:, half, 0, k, :], start=(k == 0), stop=False)
                    T.quiet(pe.matmul, psum[:, w, :], wh, ctx_part[:, half, 1, k, :], start=False, stop=False)
                    done = T.op(pe.matmul, psum[:, w, :], wl, ctx_part[:, half, 0, k, :], start=False,
                                stop=(k == DT - 1))
                A.wait(done, kT_read[m])
                kT_ready[m, c] = work_free[w] = A.op(act.copy, kT[:, m, c * CHUNK:(c + 1) * CHUNK], psum[:, w, :])
                step()

        def project_values(c, half, tiles=range(CHUNK // P)):
            for t in tiles:
                w, kt = next_bank(), c * (CHUNK // P) + t
                T.wait(work_free[w], wv_split)
                for k in range(DT):
                    ch, cl = ctx_part[:, half, 0, k, t * P:(t + 1) * P], ctx_part[:, half, 1, k, t * P:(t + 1) * P]
                    T.quiet(pe.matmul, psum[:, w, :], ch, wv_hi[:, k, :], start=(k == 0), stop=False)
                    T.quiet(pe.matmul, psum[:, w, :], ch, wv_lo[:, k, :], start=False, stop=False)
                    done = T.op(pe.matmul, psum[:, w, :], cl, wv_hi[:, k, :], start=False, stop=(k == DT - 1))
                if c < CHUNKS - 1:
                    V.wait(done, v_read[kt])
                    v_ready[kt] = work_free[w] = V.op(dve.tensor_copy, v[:, kt, :], psum[:, w, :])
                    step()
                else:
                    A.wait(done, v_read[kt])
                    v_ready[kt] = work_free[w] = A.op(act.copy, v[:, kt, :], psum[:, w, :])
            return done

        slot_free = [None] * PS
        s_free = [None, None]
        stack_read = [None] * (STACKS + QUAD)
        stack_loaded = [None] * (STACKS + QUAD)
        queries_read = [None, None]
        queries_loaded = [None, None]
        out_read = [None, None]
        keys_moved = []
        s_stack = [signal(f"stack{i}_in") for i in range(STACKS + QUAD)]
        s_queries = [signal(f"queries{i}_in") for i in range(2)]

        def load_queries(n, b, g):
            S.wait(q_stored, queries_read[n % 2])
            for block, part in enumerate((0, 0, 1)):
                queries_loaded[n % 2] = S.dma(
                    s_queries[n % 2], sp.dma_start,
                    qstack[block * DH:(block + 1) * DH, n % 2, :, :].bitcast(F32),
                    q_parts[part, g * P:(g + 1) * P, b * P:(b + 1) * P].rearrange("(j d) t -> d j t", d=DH))

        def split_keys(g, free):
            V.wait(free, keys_moved, [kT_ready[g, c] for c in range(CHUNKS)])
            high = V.op(dve.tensor_copy, keys_hi[:, :], kT[:, g, :])
            G.wait(free, keys_moved, high)
            low = G.op(pool.tensor_tensor, keys_lo[:, :], kT[:, g, :], keys_hi[:, :].bitcast(F32), ALU.subtract)
            kT_read[g] = low
            keys_moved.clear()
            return high, low

        def stack_of(g, j):
            return STACKS + j if g == 0 else (QUAD * (g - 1) + j) % STACKS

        def stack_place(n, g, j):
            return early_stack[:, (QUAD * (n + 1) + j) % PS, :] if g == 0 else stack[:, stack_of(g, j), :]

        def load_stack(n, g, j, split_done, free=None):
            i = stack_of(g, j)
            high, low = split_done
            place = stack_place(n, g, j)
            S.wait(slot_free[(QUAD * (n + 1) + j) % PS] if g == 0 else [stack_read[i], free])
            for block, part, ready in ((0, keys_hi, high), (2, keys_hi, high), (1, keys_lo, low)):
                S.wait(ready)
                stack_loaded[i] = S.dma(s_stack[i], sp.dma_start,
                                        place[block * DH:(block + 1) * DH, :].bitcast(F32),
                                        part[j * DH:(j + 1) * DH, :].bitcast(F32))
            keys_moved.append(stack_loaded[i])

        def scores(n, g, j):
            h, slot, i = QUAD * g + j, (QUAD * n + j) % PS, stack_of(g, j)
            place = stack_place(n, g, j)
            T.wait(queries_loaded[n % 2], stack_loaded[i])
            V.wait(slot_free[slot], bias_loaded)
            done = [None] * 2
            for half in range(2):
                T.wait(s_free[half])
                for c in range(2 * half, 2 * half + 2):
                    done[half] = T.op(pe.matmul, psum[:, c, :], qstack[0:PARTS * DH, n % 2, j, :],
                                      place[0:PARTS * DH, c * CHUNK:(c + 1) * CHUNK], start=True, stop=True)
            stack_read[i] = queries_read[n % 2] = done[1]
            if g == 0:
                slot_free[(QUAD * (n + 1) + j) % PS] = done[1]

            def add_bias(half, lowest):
                keys = slice(half * 2 * CHUNK, (half + 1) * 2 * CHUNK)
                V.wait(done[half])
                s_free[half] = V.op(
                    dve.tensor_tensor_reduce, prob[:, slot, keys],
                    psum[:, 2 * half:2 * half + 2, :].rearrange("p a n -> p (a n)"), biasmap[:, keys], 1.0,
                    lowest, ALU.add, ALU.max, top[:, h, half:half + 1])
                return s_free[half]

            first = add_bias(0, LOWEST)

            def second_half():
                V.wait(first)
                V.wait(add_bias(1, top[:, h, 0:1]))
                return V.op(dve.tensor_scalar, top[:, h, 2:3], top[:, h, 1:2], -1.0, None, ALU.mult)

            return second_half

        def exponentials(n, g, j, negated):
            h, slot = QUAD * g + j, (QUAD * n + j) % PS
            A.wait(negated, sums_read.get(h))
            m = A.op(act.activation, prob[:, slot, :], prob[:, slot, :], ACT.Exp, bias=top[:, h, 2:3], scale=1.0,
                     accum_out=top[:, h, 3:4])
            return slot, m

        probT_read = [None] * PTS
        sums_read = {}

        def weighted_values(n, b, g, heads, quarter=None, meanwhile=None, exponentiate=None):
            half = n % 2
            outp = psum[:, OUT_BANK, half * P:(half + 1) * P]

            def turn_tile(kt):
                w, r = next_bank(), kt % PTS
                T.wait(work_free[w], [m for _, m in heads])
                for j, (slot, _) in enumerate(heads):
                    done = T.op(pe.transpose, psum[:, w, j * P:(j + 1) * P], prob[:, slot, kt * P:(kt + 1) * P],
                                ident[:, :])
                if kt == KTILES - 1:
                    for slot, _ in heads:
                        slot_free[slot] = done
                q = V if kt in STARTS else A
                q.wait(done, probT_read[r])
                if q is A:
                    work_free[w] = A.op(act.copy, probT[:, r, :], psum[:, w, :])
                else:
                    work_free[w] = V.op(dve.tensor_copy, probT[:, r, :], psum[:, w, :])
                moved[kt] = work_free[w]

            def multiply(kt):
                r = kt % PTS
                T.wait(moved[kt], v_ready[kt], out_read if kt == 0 else None)
                for j in range(QUAD):
                    cols = slice((QUAD * g + j) * DH, (QUAD * g + j + 1) * DH)
                    done = T.op(pe.matmul, outp[j * DH:(j + 1) * DH, :], v[:, kt, cols],
                                probT[:, r, j * P:(j + 1) * P], start=(kt == 0), stop=(kt == KTILES - 1),
                                tile_position=(0, j * DH))
                v_read[kt] = probT_read[r] = done
                return done

            result = None

            def spread_reciprocals():
                V.wait(heads[-1][1], rinv_read[half])
                m = V.op(dve.reciprocal, rinv[:, half, :], top[:, QUAD * g:QUAD * (g + 1), 3])
                for h in range(QUAD * g, QUAD * (g + 1)):
                    sums_read[h] = m
                V.wait(m, rbc_read[0])
                m = V.op(dve.tensor_copy, rbc[:, :].rearrange("p (j d) -> p j d", j=QUAD),
                         rinv[:, half, :].rearrange("p (j d) -> p j d", d=1).broadcast_to([P, QUAD, DH]))
                rinv_read[half] = m
                spread_ready[0] = m

            def turn_reciprocals():
                w = next_bank()
                T.wait(spread_ready[0], work_free[w])
                m = rbc_read[0] = T.op(pe.transpose, psum[:, w, 0:P], rbc[:, :], ident[:, :])
                A.wait(m, rT_read[0])
                rT_ready[0] = work_free[w] = A.op(act.copy, rT[:, :], psum[:, w, 0:P])

            def finish(direct=None):
                multiply(KTILES - 2)
                product = multiply(KTILES - 1)
                V.wait(rT_ready[0], product, attended_stored[half])
                dst = oT[:, half, :] if direct is None else direct
                m = rT_read[0] = out_read[half] = V.op(dve.tensor_tensor, dst, outp, rT[:, :], ALU.mult)
                if direct is not None:
                    return
                S.wait(m)
                attended_stored[half] = S.dma(s_attended[half], sp.dma_start,
                                              attended[g * P:(g + 1) * P, b * P:(b + 1) * P], oT[:, half, :])

            for kt in range(KTILES) if quarter is None else range(STARTS[quarter], STARTS[quarter + 1]):
                if kt == KTILES - 1 and exponentiate:
                    result = exponentiate(negated)
                turn_tile(kt)
                if kt in STARTS and meanwhile:
                    negated = meanwhile()
                if kt >= 2:
                    multiply(kt - 2)
                if kt == 1:
                    spread_reciprocals()
                if kt == QUAD + 2:
                    turn_reciprocals()
            if kt == KTILES - 1:
                unfinished.append(finish)
            elif exponentiate:
                result = exponentiate(negated)
            return result

        rinv_read, rbc_read, rT_read = [None] * 2, [None], [None]
        moved = {}
        unfinished = []

        def finish_quad(direct=None):
            if unfinished:
                unfinished.pop()(direct)

        STARTS = (0, 4, 8, 12, KTILES)
        rT_ready, spread_ready = [None], [None]
        attended_stored = [None] * 2
        s_attended = [signal(f"attended{i}_stored") for i in range(2)]

        weights_raw = {"i": "w_i_t", "f": "w_f_t", "g": "w_g_t", "o": "w_o_t", "gate": "w_gate_t", "down": "w_down_t"}
        s_raw, s_ternary = signal("raw_weights_in"), signal("ternary_stored")
        prob_flat = prob[:, :, :].rearrange("p s n -> p (s n)")

        def ternary_steps(mats, size):
            pieces = [(mat, lo) for mat in mats for lo in range(0, COLS[mat], size)]
            raw = lambda p: prob_flat[:, (p + 1) * size:(p + 2) * size]
            result = lambda p: prob_flat[:, p * size:(p + 1) * size].bitcast(BF16)[:, 0:size]
            first = {mat: min(p for p, (m, _) in enumerate(pieces) if m == mat) for mat in mats}
            mark = {}

            def load():
                S.wait(slot_free)
                for mat in mats:
                    source = rows(a[weights_raw[mat]])
                    at = (first[mat] + 1) * size
                    mark["raw"] = S.dma(s_raw, sp.dma_start,
                                        prob_flat[:, at:at + COLS[mat]].rearrange("p (k n) -> p k n",
                                                                                  n=source.shape[2]), source)

            def add_up(mat, part, parts):
                width = COLS[mat] // parts
                at = (first[mat] + 1) * size + part * width
                V.wait(mark["raw"])
                column = mats.index(mat) * parts + part
                mark["sum"] = V.op(dve.tensor_reduce, wsum[:, column:column + 1], prob_flat[:, at:at + width], AX.X,
                                   ALU.add, apply_absolute_value=True)

            def mean(parts):
                w, count, those = next_bank(), len(mats), slice(MATS.index(mats[0]), MATS.index(mats[-1]) + 1)
                T.wait(mark["sum"], work_free[w])
                m = T.op(pe.matmul, psum[:, w, 0:count * parts], ones[:, :], wsum[:, 0:count * parts], start=True,
                         stop=True)
                V.wait(m)
                m = work_free[w] = V.op(dve.tensor_reduce, wmean[:, 0, those],
                                        psum[:, w, 0:count * parts].rearrange("p (m s) -> p m s", m=count), AX.X,
                                        ALU.add)
                V.wait(m)
                m = V.op(dve.tensor_scalar, wmean[:, 0, those], wmean[:, 0, those], 1.0 / (P * COLS[mats[0]]), 1e-5,
                         ALU.mult, ALU.max)
                V.wait(m)
                mark["mean"] = V.op(dve.reciprocal, wmean[:, 1, those], wmean[:, 0, those])

            def round_piece(p):
                mat = pieces[p][0]
                i = MATS.index(mat)
                A.wait(mark["mean"])
                m = A.op(act.activation, raw(p), raw(p), ACT.Identity, bias=magic[:, 0:1], scale=wmean[:, 1, i:i + 1])
                V.wait(m)
                mark[p] = V.op(dve.tensor_scalar, raw(p), raw(p), ROUND_MAGIC - 1.0, ROUND_MAGIC + 1.0, ALU.max,
                               ALU.min)

            def finish_piece(p):
                A.wait(mark[p], A.last())
                mark["made"] = A.op(act.activation, result(p), raw(p), ACT.Identity, bias=magic[:, 1:2], scale=1.0)

            def store():
                nonlocal slot_free, ternary_stored
                n = len(pieces)
                S.wait(mark["made"])
                ternary_stored = S.dma(
                    s_ternary, sp.dma_start,
                    ternary_dram[:, FIRST[mats[0]]:FIRST[mats[0]] + n * size].rearrange("p (n s) -> p n s", n=n),
                    prob_flat[:, 0:n * size].rearrange("p (n s) -> p n s", n=n).bitcast(BF16)[:, :, 0:size])
                slot_free = [[ternary_stored, V.last(), A.last()]] * PS

            nothing = lambda: None
            parts = COLS[mats[0]] // (2 * INNER) or 1
            steps = [load] + [nothing] * 5
            steps += [lambda mat=mat, part=part: add_up(mat, part, parts) for mat in mats for part in range(parts)]
            steps += [nothing, lambda: mean(parts)]
            for p in range(len(pieces) + 1):
                def both(p=p):
                    if p < len(pieces):
                        round_piece(p)
                    if p:
                        finish_piece(p - 1)
                steps.append(both)
            return steps + [store]

        ternary_stored = None
        WINDOWS = {1: (("i", "f", "g", "o"), DT * D), 2: (("gate",), INNER), 3: (("down",), INNER)}
        steps = []

        def step():
            if steps:
                steps.pop(0)()

        def split_chunk(number):
            nonlocal ctx_loaded
            half = number % 2
            V.wait(ctx_read[half])
            ready = split(ctx_part[:, half, 0, :, :], ctx_part[:, half, 1, :, :], ctx_raw[:, :, :], ctx_loaded)
            if (number + 1) % CHUNKS:
                ctx_loaded = load_ctx(number // CHUNKS, (number + 1) % CHUNKS, ready)
            return ready

        pending = None
        n = 0
        chunk_ready = {0: split_chunk(0)}
        wv_split = split(wv_hi[:, :, :], wv_lo[:, :, :], wv_sb, wv_loaded)
        for b in range(B):
            for c in range(CHUNKS):
                number = b * CHUNKS + c
                half = number % 2
                if c == 0 and pending:
                    finish_quad()
                    weighted_values(*pending)
                    finish_quad()
                    pending = None
                    steps = ternary_steps(*WINDOWS[b])
                project_keys(c, half, chunk_ready[number], range(DT if c < CHUNKS - 1 else DT - 1))
                if c + 1 < CHUNKS:
                    chunk_ready[number + 1] = split_chunk(number + 1)
                else:
                    split_done = split_keys(0, [chunk_ready[number], ctx_read[0]])
                    load_queries(n, b, 0)
                    while steps:
                        step()
                    for j in range(QUAD):
                        load_stack(n, 0, j, split_done)
                if c < CHUNKS - 1:
                    ctx_read[half] = project_values(c, half)
                if b == 0 and c == 1:
                    normed = layernorm(x_in, x_in, "rstd0", [x_loaded] * B)
                    for t in range(B):
                        w = next_bank()
                        m = work_free[w] = transpose_tile(xhT[:, :, t * P:(t + 1) * P], x_in[:, t, :], w, normed[t],
                                                          work_free[w], A)
                    for g in range(DT):
                        w = next_bank()
                        T.wait(m, wq_loaded, work_free[w])
                        for k in range(DT):
                            done = T.op(pe.matmul, psum[:, w, :], wq_sb[:, k, g * P:(g + 1) * P], xhT[:, k, :],
                                        start=(k == 0), stop=(k == DT - 1))
                        A.wait(done)
                        m2 = work_free[w] = A.op(act.activation, q_all[:, g, :], psum[:, w, :], ACT.Copy,
                                                 scale=float(DH) ** -0.5)
                    m2 = split(q_hi.bitcast(F32R), q_lo.bitcast(F32R), q_all, m2)
                    S.wait(m2)
                    s_parts = signal("query_parts_stored")
                    for i, part in enumerate((q_hi, q_lo)):
                        q_stored = S.dma(s_parts, sp.dma_start,
                                         q_parts[i].rearrange("(k p) t -> p k t", p=P), part)
                    slot_free = [[q_stored, done, normed[-1], wv_split]] * PS
            for g in range(DT):
                heads = []
                for j in range(QUAD):
                    if g == 0:
                        done = project_values(CHUNKS - 1, 1, (j,))
                    second_half = scores(n, g, j)
                    if j == 0 and g + 1 < DT:
                        load_queries(n + 1, b, g + 1)
                    if g == 0 and j == QUAD - 1:
                        project_keys(CHUNKS - 1, 1, chunk_ready[number], (DT - 1,))
                        ctx_read[1] = T.last()
                    h = QUAD * g + j + STACKS - 1
                    if QUAD <= h < HEADS:
                        load_stack(n, h // QUAD, h % QUAD, split_done, None if h == QUAD else ctx_read[1])
                    if pending and j == QUAD - 1:
                        negated = second_half()
                        second_half = lambda negated=negated: negated
                    finish_quad()
                    if pending:
                        heads.append(weighted_values(
                            *pending, quarter=j, meanwhile=second_half,
                            exponentiate=lambda negated, where=(n, g, j): exponentials(*where, negated)))
                    else:
                        heads.append(exponentials(n, g, j, second_half()))
                    if j == 1 and g + 1 < DT:
                        split_done = split_keys(g + 1, None)
                    if g == DT - 1 and b + 1 < B:
                        if j == 1:
                            ctx_loaded = load_ctx(b + 1, 0, list(keys_moved))
                        if j == QUAD - 1:
                            ctx_read[0] = [list(keys_moved), stack_read[0]]
                            ctx_read[1] = [stack_read[1], stack_read[2]]
                            chunk_ready[(b + 1) * CHUNKS] = split_chunk((b + 1) * CHUNKS)
                pending = (n, b, g, heads)
                n += 1

        wo_sb, x_again, attended_sb = view(0), view(1), view(2)
        s_wo, s_again = signal("wo_in"), signal("attended_in")
        finish_quad()
        S.wait(slot_free[0], slot_free[1], slot_free[2], attended_stored)
        wo_loaded = S.dma(s_wo, sp.dma_start, wo_sb, rows(a["wo"]))
        S.dma(s_again, sp.dma_start, attended_sb[:, 0:DT - 1, :],
              attended[0:D - P, :].rearrange("(k p) t -> p k t", p=P))
        attended_loaded = S.dma(s_again, sp.dma_start, attended_sb[:, DT - 1, 0:(B - 1) * P],
                                attended[D - P:D, 0:(B - 1) * P])
        x_loaded = S.dma(s_x, sp.dma_start, x_again, a["x"].rearrange("b s d -> s b d"))
        s_ternary_in = signal("ternary_in")
        S.wait(ctx_read[0], ctx_read[1], stack_read, T.last(), ternary_stored)
        tern_loaded = S.dma(s_ternary_in, sp.dma_start, ternary[:, :], ternary_dram)
        x1_ready = []

        def add_attention(b):
            w = next_bank()
            T.wait(work_free[w], wo_loaded, attended_loaded, out_read if b == B - 1 else None)
            for g in range(DT):
                done = T.op(pe.matmul, psum[:, w, :], attended_sb[:, g, b * P:(b + 1) * P], wo_sb[:, g, :],
                            start=(g == 0), stop=(g == DT - 1))
            V.wait(done, x_loaded)
            m = work_free[w] = V.op(dve.tensor_tensor, x1[:, b, :], psum[:, w, :], x_again[:, b, :], ALU.add)
            x1_ready.append(m)

        for quarter in range(QUAD - 1):
            weighted_values(*pending, quarter=quarter)
        for b in range(B - 1):
            add_attention(b)
        weighted_values(*pending, quarter=QUAD - 1)
        finish_quad(attended_sb[:, DT - 1, (B - 1) * P:B * P])
        add_attention(B - 1)
        attention_over = [q.last() for q in (T, V, A, G)]


        region_2 = ExitStack()
        sb("place_of_ternary", [P, TERN_COLS], BF16, region_2)
        tern = {mat: ternary[:, FIRST[mat]:FIRST[mat] + COLS[mat]].rearrange(
            "p (k n) -> p k n", n=2 * INNER if mat == "gate" else D) for mat in MATS}
        z_int = sb("z_int", [P, B, INNER], BF16, region_2)
        z_intT = sb("z_intT", [P, IT, B * P], BF16, region_2)
        resid = sb("resid", [P, B, D], F32, region_2)
        work = sb("work", [P, B, D], F32, region_2)
        q_int = sb("q_int", [P, B, D], BF16, region_2)
        q_intT = sb("q_intT", [P, DT, B * P], BF16, region_2)
        step_row = sb("step_row", [P, B * P], F32, region_2)
        scan = sb("scan", [P, 3, DT, B * P], F32, region_2)
        swish_g = scan[:, 0]
        junk = sb("junk", [P, INNER], BF16, region_2)
        spread = sb("spread", [P, B, P], F32, region_2)
        gains = sb("gains", [P, 3, D], F32, region_2)
        lower = sb("lower", [P, 2, DT], F32, region_2)
        tok = sb("tok", [P, 4, B], F32, region_2)

        G.wait(*attention_over)
        V.wait(constants, *attention_over)
        A.wait(constants, *attention_over)
        S.wait(*attention_over)
        s_small = signal("small_in")
        for n_, key in enumerate(("attn_norm", "g_norm", "mlp_norm")):
            small = S.dma(s_small, sp.dma_start, gains[:, n_, :],
                          a[key].rearrange("(o d) -> o d", o=1).broadcast_to([P, D]))
        small = S.dma(s_small, sp.dma_start, lower[:, 0, :], a["lower"])

        bank_free = [attention_over] * 8
        bank_turn = [0]

        def bank():
            bank_turn[0] += 1
            return bank_turn[0] % 8

        def squares(key, src, width, marks):
            ready = []
            for group in GROUPS:
                for b in group:
                    A.wait(marks[b], A.last())
                    m = A.op(act.activation, junk[:, 0:width], src(b), ACT.Square,
                             accum_out=scalars(key)[:, b:b + 1])
                m = rsqrt_cols(cols(scalars(key), group), cols(scalars(key), group), 1.0 / width, 1e-6, m)
                ready += [m] * len(group)
            return ready

        def quantize(key, src, dst, width, marks, known=None):
            peak, quantum, factor = scalars(key + "_peak"), scalars(key + "_quantum"), scalars(key + "_factor")
            peaks = []
            if known:
                rn = []
                for group in GROUPS:
                    m = rsqrt_cols(cols(scalars(key + "_rn"), group), cols(scalars(key + "_rn"), group), 1.0 / width,
                                   1e-6, [known[b][0] for b in group])
                    rn += [m] * len(group)
                peaks = [peak_mark for _, peak_mark in known]
            else:
                rn = squares(key + "_rn", src, width, marks)
            for b in range(0 if known else B):
                V.wait(marks[b])
                peaks.append(V.op(dve.tensor_reduce, peak[:, b:b + 1], src(b), AX.X, ALU.max,
                                  apply_absolute_value=True))
            rounded, steps = [], []
            for group in GROUPS:
                part = lambda column: cols(column, group)
                V.wait([peaks[b] for b in group], rn[group[0]])
                m = V.op(dve.tensor_tensor, part(peak), part(peak), part(scalars(key + "_rn")), ALU.mult)
                V.wait(m)
                m = V.op(dve.tensor_scalar, part(quantum), part(peak), 1e-5, 1.0 / 127.0, ALU.max, ALU.mult)
                steps.append(m)
                V.wait(m)
                m = V.op(dve.reciprocal, part(factor), part(quantum))
                V.wait(m)
                m = V.op(dve.tensor_tensor, part(factor), part(factor), part(scalars(key + "_rn")), ALU.mult)
                A.wait(m)
                rounded += [A.op(act.activation, src(b), src(b), ACT.Identity, bias=magic[:, 0:1],
                                 scale=factor[:, b:b + 1]) for b in group]
            out_marks = []
            for b in range(B):
                V.wait(rounded[b])
                out_marks.append(V.op(dve.tensor_scalar, dst(b), src(b), ROUND_MAGIC, 127.0, ALU.subtract, ALU.min))
            return out_marks, quantum, steps

        def turn_integers(dst, src, tiles, marks):
            done = []
            for b in range(B):
                copied = []
                for k0 in range(0, tiles, 4):
                    ks = range(k0, min(k0 + 4, tiles))
                    w = bank()
                    T.wait(marks[b], bank_free[w], constants)
                    half = psum[:, w, :].bitcast(BF16)
                    for k in ks:
                        m = T.op(pe.transpose, half[:, (k - k0) * P:(k - k0 + 1) * P], src(b)[:, k * P:(k + 1) * P],
                                 identb[:, :])
                    q = V if (b + k0 // 4) % 2 else A
                    q.wait(m)
                    args = (dst[:, k0:ks[-1] + 1, b * P:(b + 1) * P],
                            half[:, 0:len(ks) * P].rearrange("p (k t) -> p k t", t=P))
                    m = bank_free[w] = (V.op(dve.tensor_copy, *args) if q is V else A.op(act.copy, *args))
                    copied.append(m)
                done.append(copied)
            return done

        def token_scale(i, quantum, mat, after):
            V.wait(after)
            k = MATS.index(mat)
            return V.op(dve.tensor_scalar, tok[:, i, :], quantum, wmean[:, 0, k:k + 1], None, ALU.mult)

        tern_ready = {n: tern_loaded for n in MATS}
        resid_ready = layernorm(resid, x1, "rstd1", x1_ready)

        def normalised(key, gain):
            rr, ready = squares(key, lambda b: resid[:, b, :], D, resid_ready), []
            for b in range(B):
                V.wait(rr[b], small)
                ready.append(V.op(dve.scalar_tensor_tensor, work[:, b, :], resid[:, b, :],
                                  scalars(key)[:, b:b + 1], gains[:, gain, :], ALU.mult, ALU.mult))
            return ready

        ready = normalised("rr", 0)
        ready, quantum, step = quantize("qa", lambda b: work[:, b, :], lambda b: q_int[:, b, :], D, ready)
        turned = turn_integers(q_intT, lambda b: q_int[:, b, :], DT, ready)

        w = bank()
        V.wait(step)
        m = V.op(dve.tensor_copy, spread[:, :, :],
                 quantum.rearrange("p (b t) -> p b t", t=1).broadcast_to([P, B, P]))
        T.wait(m, bank_free[w])
        for b in range(B):
            m = T.op(pe.transpose, psum[:, w, b * P:(b + 1) * P], spread[:, b, :], ident[:, :])
        A.wait(m)
        row_ready = bank_free[w] = A.op(act.copy, step_row[:, :], psum[:, w, :])
        m = V.op(dve.tensor_scalar, lower[:, 1, :], lower[:, 0, :], -1.0, 1.0, ALU.mult, ALU.add)
        lower_ready = m

        state_ready = []

        def recur(c, gated):
            V.wait(*gated)
            m = V.op(dve.scalar_tensor_tensor, scan[:, 0, c, :], scan[:, 1, c, :], 1.0, scan[:, 0, c, :],
                     ALU.subtract, ALU.mult, reverse0=True)
            V.wait(m)
            for b in range(B):
                span = slice(b * P, (b + 1) * P)
                m = V.op(dve.tensor_tensor_scan, scan[:, 2, c, span], scan[:, 1, c, span], scan[:, 0, c, span], 0.0,
                         ALU.mult, ALU.add)
            state_ready.append(m)

        for c in range(DT):
            raws = {}
            for n, place in (("f", 1), ("i", 0)):
                w = bank()
                T.wait(turned, tern_ready[n], bank_free[w])
                for k in range(DT):
                    m = T.op(pe.matmul, psum[:, w, :], tern[n][:, k, c * P:(c + 1) * P], q_intT[:, k, :],
                             start=(k == 0), stop=(k == DT - 1))
                V.wait(m, row_ready)
                raws[n] = bank_free[w] = V.op(
                    dve.scalar_tensor_tensor, scan[:, place, c, :], psum[:, w, :],
                    wmean[:, 0, MATS.index(n):MATS.index(n) + 1], step_row[:, :], ALU.mult, ALU.mult)
            A.wait(raws["f"])
            f = A.op(act.activation, scan[:, 1, c, :], scan[:, 1, c, :], ACT.Sigmoid)
            A.wait(raws["i"])
            si = A.op(act.activation, scan[:, 2, c, :], scan[:, 0, c, :], ACT.Sigmoid)
            G.wait(f, lower_ready)
            f = G.op(pool.tensor_scalar, scan[:, 1, c, :], scan[:, 1, c, :], lower[:, 1, c:c + 1],
                     lower[:, 0, c:c + 1], ALU.mult, ALU.add)
            G.wait(si)
            m = G.op(pool.tensor_tensor, scan[:, 0, c, :], scan[:, 0, c, :], scan[:, 2, c, :], ALU.mult)
            if c:
                recur(c - 1, gated)
            gated = (f, m)
        recur(DT - 1, gated)

        g_scaled = token_scale(0, quantum, "g", step)
        g_ready = {}
        for b in range(B):
            w = bank()
            T.wait(turned[b], tern_ready["g"], bank_free[w])
            for k in range(DT):
                m = T.op(pe.matmul, psum[:, w, :], q_intT[:, k, b * P:(b + 1) * P], tern["g"][:, k, :],
                         start=(k == 0), stop=(k == DT - 1))
            A.wait(m, g_scaled, state_ready)
            m = A.op(act.activation, swish_g[:, b, :], psum[:, w, :], ACT.Sigmoid, scale=tok[:, 0, b:b + 1])
            V.wait(m)
            g_ready[b] = bank_free[w] = V.op(dve.scalar_tensor_tensor, swish_g[:, b, :], psum[:, w, :],
                                          tok[:, 0, b:b + 1], swish_g[:, b, :], ALU.mult, ALU.mult)

        state_bank = [bank() for _ in range(B)]
        for b in range(B):
            T.wait(state_ready, bank_free[state_bank[b]])
            for c in range(DT):
                m = T.op(pe.transpose, psum[:, state_bank[b], c * P:(c + 1) * P], scan[:, 2, c, b * P:(b + 1) * P],
                         ident[:, :])
            state_ready[b] = m
        ro = squares("ro", lambda b: psum[:, state_bank[b], :], D, state_ready)
        ready = []
        for b in range(B):
            V.wait(ro[b], g_ready[b])
            m = bank_free[state_bank[b]] = V.op(dve.scalar_tensor_tensor, work[:, b, :], psum[:, state_bank[b], :],
                                                scalars("ro")[:, b:b + 1], gains[:, 1, :], ALU.mult, ALU.mult)
            V.wait(m)
            ready.append(V.op(dve.tensor_tensor, work[:, b, :], work[:, b, :], swish_g[:, b, :], ALU.mult))
        ready, quantum, step = quantize("qo", lambda b: work[:, b, :], lambda b: q_int[:, b, :], D, ready)
        turned = turn_integers(q_intT, lambda b: q_int[:, b, :], DT, ready)
        o_scaled = token_scale(1, quantum, "o", step)

        def ternary_product(mat, srcT, tiles, scaled, i, marks):
            out_marks = []
            for b in range(B):
                w = bank()
                T.wait(marks[b], tern_ready[mat], bank_free[w])
                for k in range(tiles):
                    m = T.op(pe.matmul, psum[:, w, :], srcT[:, k, b * P:(b + 1) * P], tern[mat][:, k, :],
                             start=(k == 0), stop=(k == tiles - 1))
                V.wait(m, scaled)
                m = bank_free[w] = V.op(dve.scalar_tensor_tensor, resid[:, b, :], psum[:, w, :], tok[:, i, b:b + 1],
                                        resid[:, b, :], ALU.mult, ALU.add)
                out_marks.append(m)
            return out_marks

        resid_ready = ternary_product("o", q_intT, DT, o_scaled, 1, turned)

        ready = normalised("rm", 2)
        ready, quantum, step = quantize("qm", lambda b: work[:, b, :], lambda b: q_int[:, b, :], D, ready)
        turned = turn_integers(q_intT, lambda b: q_int[:, b, :], DT, ready)
        gate_scaled = token_scale(2, quantum, "gate", step)
        A.wait(turned)
        z = scan[:, :, :, :].rearrange("p a c t -> p (a c t)")[:, 0:B * INNER].rearrange("p (b n) -> p b n", b=B)
        z_ready = []
        up_read = [None]
        up = work[:, 0, :]

        def z_sums(b):
            A.wait(z_ready[b], A.last())
            squared = A.op(act.activation, junk[:, 0:INNER], z[:, b, :], ACT.Square,
                           accum_out=scalars("qz_rn")[:, b:b + 1])
            V.wait(z_ready[b])
            z_known.append((squared, V.op(dve.tensor_reduce, scalars("qz_peak")[:, b:b + 1], z[:, b, :], AX.X,
                                          ALU.max, apply_absolute_value=True)))

        z_known = []
        for b in range(B):
            done = []
            for lo in range(0, INNER, BANK):
                n_ = min(BANK, INNER - lo)
                w_gate, w_up = bank(), bank()
                for w, base in ((w_gate, 0), (w_up, INNER)):
                    T.wait(turned[b], tern_ready["gate"], bank_free[w])
                    for k in range(DT):
                        m = T.op(pe.matmul, psum[:, w, 0:n_], q_intT[:, k, b * P:(b + 1) * P],
                                 tern["gate"][:, k, base + lo:base + lo + n_], start=(k == 0), stop=(k == DT - 1))
                A.wait(m, gate_scaled, state_ready)
                dst = z[:, b, lo:lo + n_]
                m = A.op(act.activation, dst, psum[:, w_gate, 0:n_], ACT.Sigmoid, scale=tok[:, 2, b:b + 1])
                V.wait(m)
                m = bank_free[w_gate] = V.op(dve.scalar_tensor_tensor, dst, psum[:, w_gate, 0:n_],
                                             tok[:, 2, b:b + 1], dst, ALU.mult, ALU.mult)
                if lo == BANK:
                    A.wait(up_read[0])
                    m2 = bank_free[w_up] = A.op(act.activation, up[:, 0:n_], psum[:, w_up, 0:n_], ACT.Copy,
                                                scale=tok[:, 2, b:b + 1])
                    G.wait(m, m2)
                    done.append(G.op(pool.tensor_tensor, dst, dst, up[:, 0:n_], ALU.mult))
                    up_read[0] = done[-1]
                else:
                    V.wait(m)
                    m = bank_free[w_up] = V.op(dve.scalar_tensor_tensor, dst, psum[:, w_up, 0:n_],
                                               tok[:, 2, b:b + 1], dst, ALU.mult, ALU.mult)
                    done.append(m)
            z_ready.append(done)
            if b:
                z_sums(b - 1)
        z_sums(B - 1)
        ready, quantum, step = quantize("qz", lambda b: z[:, b, :], lambda b: z_int[:, b, :], INNER, z_ready, z_known)
        turned = turn_integers(z_intT, lambda b: z_int[:, b, :], IT, ready)
        z_scaled = token_scale(3, quantum, "down", step)
        resid_ready = ternary_product("down", z_intT, IT, z_scaled, 3, turned)
        x2_ready = []
        for b in range(B):
            V.wait(resid_ready[b])
            x2_ready.append(V.op(dve.tensor_tensor, x1[:, b, :], x1[:, b, :], resid[:, b, :], ALU.add))
        region_2.close()
        x1_ready = x2_ready


        phase2_over = [q.last() for q in (T, V, A, G)]
        wslot += [sb(f"wslot{i}", [P, DT * HID], F32) for i in range(2, WSLOTS)]
        xm = sb("xm", [P, B, D], F32)
        xm_hi = sb("xm_hi", [P, B, D], F32R)
        xm_lo = sb("xm_lo", [P, B, D], F32R)
        route = ExitStack()
        xmT = sb("xmT", [P, DT, B * P], F32, route)
        route.close()
        hidden = sb("hidden", [P, HT, SLOTS], F32)
        wr = sb("wr", [P, DT, EXPERTS], F32)
        br = sb("br", [P, EXPERTS], F32)
        b1 = sb("b1", [P, EXPERTS, HT], F32)
        b2 = sb("b2", [EXPERTS, D], F32)
        iota_e = sb("iota_e", [P, EXPERTS], F32)
        iota_s = sb("iota_s", [P, SLOTS], F32)
        before = sb("before", [P, P], BF16)
        onesb = sb("onesb", [P, P], BF16)
        logits = sb("logits", [P, B, EXPERTS], F32)
        best = sb("best", [P, B, 8], F32)
        best_at = sb("best_at", [P, B, 8], U32)
        best_atf = sb("best_atf", [P, B, 2], F32)
        gates2 = sb("gates2", [P, B, 4], F32)
        onehot = sb("onehot", [P, B, 2, EXPERTS], F32)
        gate = sb("gate", [P, B, EXPERTS], F32)
        gateT = sb("gateT", [EXPERTS, B * P], F32)
        chosen = sb("chosen", [P, B, EXPERTS], F32)
        chosenb = sb("chosenb", [P, B, EXPERTS], BF16)
        place = sb("place", [P, B, EXPERTS], F32)
        counts = sb("counts", [P, EXPERTS], I32)
        load = sb("load", [P, 1], I32)
        pick = sb("pick", [P, 2, B, 2, SLOTS], F32R)
        picked = sb("picked", [P, 2, DT, SLOTS], F32)
        pickT = sb("pickT", [P, 2, B * P], F32R)
        slot_gate = sb("slot_gate", [P, 2, 2], F32)
        yT = sb("yT", [P, DT, SLOTS], F32)
        y_hi = sb("y_hi", [P, 2, D], F32R)
        y_lo = sb("y_lo", [P, 2, D], F32R)

        STILES = [(st, min(P, SLOTS - st * P)) for st in range(-(-SLOTS // P))]
        s_w = [signal(f"weights{i}_in") for i in range(WSLOTS)]
        w_free = [attention_over, attention_over, phase2_over, phase2_over]
        w_turn = [0]

        def load_weights(source):
            i = w_turn[0] % WSLOTS
            w_turn[0] += 1
            S.wait(w_free[i])
            return i, S.dma(s_w[i], sp.dma_start, wslot[i][:, :].rearrange("p (k n) -> p k n", n=source.shape[1]),
                            source.rearrange("(k p) n -> p k n", p=P))

        def expert_loads(e):
            return load_weights(a["w1"][e]), load_weights(a["w2"][e])

        loads = {(0, 0): expert_loads(0)}
        S.wait(phase2_over)
        s_route = signal("router_in")
        S.dma(s_route, sp.dma_start, wr[:, :, :], a["wr"].rearrange("(k p) e -> p k e", p=P))
        S.dma(s_route, sp.dma_start, br[:, :], a["br"].rearrange("(o e) -> o e", o=1).broadcast_to([P, EXPERTS]))
        S.dma(s_route, sp.dma_start, b1[:, :, :], a["b1_t"])
        route_loaded = S.dma(s_route, sp.dma_start, b2[:, :], a["b2"])
        loads[0, 1] = expert_loads(1)

        G.wait(phase2_over)
        A.wait(phase2_over)
        V.wait(phase2_over)
        G.op(pool.iota, iota_e[:, :], [[1, EXPERTS]], base=0, channel_multiplier=0,
             allow_small_or_imprecise_dtypes=True)
        G.op(pool.iota, iota_s[:, :], [[1, SLOTS]], base=1, channel_multiplier=0,
             allow_small_or_imprecise_dtypes=True)
        m = G.op(pool.memset, onesb[:, :], 1.0)
        G.wait(m)
        route_constants = G.op(pool.affine_select, out=before[:, :], in_=onesb[:, :], compare_op=ALU.is_gt, fill=0.0,
                               base=0, pattern=[[1, P]], channel_multiplier=-1)

        OUT = range(4)
        RING = (4, 5, 6, 7)
        bank_free = {w: phase2_over for w in range(8)}
        ring_turn = [0]

        def ring():
            ring_turn[0] += 1
            return RING[ring_turn[0] % len(RING)]

        normed = layernorm(xm, x1, "rstd2", x2_ready)
        logit_bank = ring()
        xmT_ready = []
        for b in range(B + 1):
            if b < B:
                w = RING[(RING.index(logit_bank) + 1 + b % 3) % len(RING)]
                bank_free[w] = transpose_tile(xmT[:, :, b * P:(b + 1) * P], xm[:, b, :], w, normed[b], bank_free[w],
                                              A)
                xmT_ready.append(bank_free[w])
            if b:
                T.wait(xmT_ready[b - 1], route_loaded, bank_free[logit_bank])
                for k in range(DT):
                    m = T.op(pe.matmul, psum[:, logit_bank, (b - 1) * EXPERTS:b * EXPERTS],
                             xmT[:, k, (b - 1) * P:b * P], wr[:, k, :], start=(k == 0), stop=(k == DT - 1))
        w = logit_bank
        V.wait(normed)
        hi = V.op(dve.tensor_copy, xm_hi[:, :, :], xm[:, :, :])
        V.wait(hi)
        xm_ready = V.op(dve.tensor_tensor, xm_lo[:, :, :], xm[:, :, :], xm_hi[:, :, :].bitcast(F32), ALU.subtract)
        V.wait(m, route_constants)
        for b in range(B):
            m = V.op(dve.tensor_tensor, logits[:, b, :], psum[:, w, b * EXPERTS:(b + 1) * EXPERTS], br[:, :], ALU.add)
        bank_free[w] = m
        V.wait(m)
        for b in range(B):
            m = V.op(dve.max, best[:, b, :], logits[:, b, :])
        V.wait(m)
        diff = V.op(dve.tensor_tensor, gates2[:, :, 0], best[:, :, 1], best[:, :, 0], ALU.subtract)
        for b in range(B):
            m = V.op(dve.max_index, best_at[:, b, :], best[:, b, :], logits[:, b, :])
        A.wait(diff)
        expd = A.op(act.activation, gates2[:, :, 1], gates2[:, :, 0], ACT.Exp)
        V.wait(m)
        m = V.op(dve.tensor_copy, best_atf[:, :, :], best_at[:, :, 0:2])
        V.wait(m)
        for b in range(B):
            for i in range(2):
                m = V.op(dve.tensor_scalar, onehot[:, b, i, :], iota_e[:, :], best_atf[:, b, i:i + 1], None,
                         ALU.is_equal)
        V.wait(m)
        m = V.op(dve.tensor_tensor, chosen[:, :, :], onehot[:, :, 0, :], onehot[:, :, 1, :], ALU.add)
        V.wait(m)
        chosen_ready = V.op(dve.tensor_copy, chosenb[:, :, :], chosen[:, :, :])
        V.wait(expd)
        m = V.op(dve.tensor_scalar, gates2[:, :, 2], gates2[:, :, 1], 1.0, None, ALU.add)
        V.wait(m)
        m = V.op(dve.reciprocal, gates2[:, :, 2], gates2[:, :, 2])
        V.wait(m)
        m = V.op(dve.tensor_tensor, gates2[:, :, 3], gates2[:, :, 1], gates2[:, :, 2], ALU.mult)
        V.wait(m)
        for b in range(B):
            m = V.op(dve.tensor_scalar, gate[:, b, :], onehot[:, b, 0, :], gates2[:, b, 2:3], None, ALU.mult)
        V.wait(m)
        for b in range(B):
            m = V.op(dve.scalar_tensor_tensor, gate[:, b, :], onehot[:, b, 1, :], gates2[:, b, 3:4], gate[:, b, :],
                     ALU.mult, ALU.add)
        gate_ready = m

        w = ring()
        T.wait(chosen_ready, bank_free[w])
        for b in range(B):
            for earlier in range(b):
                T.quiet(pe.matmul, psum[:, w, b * EXPERTS:(b + 1) * EXPERTS], onesb[:, :], chosenb[:, earlier, :],
                        start=(earlier == 0), stop=False)
            T.quiet(pe.matmul, psum[:, w, b * EXPERTS:(b + 1) * EXPERTS], before[:, :], chosenb[:, b, :],
                    start=(b == 0), stop=True)
        for b in range(B):
            m = T.op(pe.matmul, psum[:, w, B * EXPERTS:(B + 1) * EXPERTS], onesb[:, :], chosenb[:, b, :],
                     start=(b == 0), stop=(b == B - 1))
        V.wait(m)
        m = V.op(dve.scalar_tensor_tensor, place[:, :, :].rearrange("p b e -> p (b e)"), psum[:, w, 0:B * EXPERTS],
                 1.0, chosen[:, :, :].rearrange("p b e -> p (b e)"), ALU.add, ALU.mult)
        place_ready = m
        V.op(dve.tensor_copy, counts[:, :], psum[:, w, B * EXPERTS:(B + 1) * EXPERTS])
        load_ready = bank_free[w] = V.op(dve.tensor_reduce, load[:, :], psum[:, w, B * EXPERTS:(B + 1) * EXPERTS],
                                         AX.X, ALU.max)
        w = ring()
        T.wait(gate_ready, bank_free[w])
        for b in range(B):
            m = T.op(pe.transpose, psum[0:EXPERTS, w, b * P:(b + 1) * P], gate[:, b, :], ident[:, :])
        A.wait(m)
        gateT_ready = bank_free[w] = A.op(act.copy, gateT[:, :], psum[0:EXPERTS, w, :])

        class Last:
            pick = [None, None]
            picked = [None, None]
            pickT = slot_gate = hidden = yT = y = None

        def gather(pair, r, half):
            for b in range(B):
                for i in range(2):
                    V.wait(place_ready, Last.pick[half])
                    e = 2 * pair + i
                    picks = V.op(dve.tensor_scalar, pick[:, half, b, i, :], iota_s[:, :], float(r * SLOTS),
                                 place[:, b, e:e + 1], ALU.add, ALU.is_equal)
            for k in range(DT):
                w = ring()
                T.wait(picks, xm_ready, bank_free[w])
                for b in range(B):
                    for part in (xm_hi, xm_lo):
                        m = T.op(pe.matmul, psum[:, w, 0:2 * SLOTS], part[:, b, k * P:(k + 1) * P],
                                 pick[:, half, b, :, :].rearrange("p i s -> p (i s)"),
                                 start=(b == 0 and part is xm_hi), stop=(b == B - 1 and part is xm_lo))
                A.wait(m, Last.picked)
                m = bank_free[w] = A.op(act.copy, picked[:, :, k, :],
                                        psum[:, w, 0:2 * SLOTS].rearrange("p (i s) -> p i s", i=2))
            return m

        def hidden_layer(e, i, slot_mark, gathered, r, turn_output):
            slot, loaded = slot_mark
            if r == 0:
                T.begin_either()
            w1 = wslot[slot][:, :].rearrange("p (k n) -> p k n", k=DT)
            marks = []
            for h in range(HT):
                if h == HT - 3:
                    if r == 0:
                        T.end_either(e)
                    gated = turn_output()
                    if r == 0:
                        T.begin_either()
                w = ring()
                T.wait(loaded, gathered, bank_free[w])
                for k in range(DT):
                    m = T.op(pe.matmul, psum[:, w, 0:SLOTS], w1[:, k, h * P:(h + 1) * P], picked[:, i, k, :],
                             start=(k == 0), stop=(k == DT - 1))
                if h % 2:
                    A.wait(m, Last.hidden)
                    m2 = A.op(act.activation, hidden[:, h, :], psum[:, w, 0:SLOTS], ACT.Relu, bias=b1[:, e, h:h + 1])
                else:
                    V.wait(m, Last.hidden)
                    m2 = V.op(dve.tensor_scalar, hidden[:, h, :], psum[:, w, 0:SLOTS], b1[:, e, h:h + 1], 0.0,
                              ALU.add, ALU.max)
                bank_free[w] = m2
                marks.append(m2)
            w_free[slot] = Last.picked[i] = m
            if r == 0:
                T.end_either(e)
            return marks, gated

        def output_layer(slot_mark, hidden_ready, e, r):
            slot, loaded = slot_mark
            if r == 0:
                T.begin_either()
            w2 = wslot[slot][:, :].rearrange("p (h n) -> p h n", h=HT)
            for k in range(DT):
                w = ring()
                T.wait(loaded, bank_free[w])
                for h in range(HT):
                    T.wait(hidden_ready[h])
                    m = T.op(pe.matmul, psum[:, w, 0:SLOTS], w2[:, h, k * P:(k + 1) * P], hidden[:, h, :],
                             start=(h == 0), stop=(h == HT - 1))
                q = A if k % 2 else V
                q.wait(m, Last.yT)
                bank_free[w] = (A.op(act.copy, yT[:, k, :], psum[:, w, 0:SLOTS]) if q is A else
                                           V.op(dve.tensor_copy, yT[:, k, :], psum[:, w, 0:SLOTS]))
            w_free[slot] = Last.hidden = m
            if r == 0:
                T.end_either(e)
            return [V.last(), A.last()]

        first_scatter = [True]

        def slot_tables(e, i, half):
            for st, rows_ in STILES:
                w = ring()
                T.wait(bank_free[w])
                for b in range(B):
                    m = T.op(pe.transpose, psum[0:rows_, w, b * P:(b + 1) * P],
                             pick[:, half, b, i, st * P:st * P + rows_].bitcast(F32), ident[:, :])
                V.wait(m, Last.pickT)
                bank_free[w] = V.op(dve.tensor_copy, pickT[0:rows_, st, :], psum[0:rows_, w, :])
            w = ring()
            T.wait(gate_ready, bank_free[w])
            for st, rows_ in STILES:
                for b in range(B):
                    m = T.op(pe.matmul, psum[0:rows_, w, st:st + 1],
                             pick[:, half, b, i, st * P:st * P + rows_].bitcast(F32), gate[:, b, e:e + 1],
                             start=(b == 0), stop=(b == B - 1))
            Last.pick[half] = m
            V.wait(m, Last.slot_gate)
            for st, rows_ in STILES:
                m = bank_free[w] = V.op(dve.tensor_copy, slot_gate[0:rows_, st, i:i + 1], psum[0:rows_, w, st:st + 1])
            return m

        def turn_output(i, yT_ready, tables):
            for st, rows_ in STILES:
                w = ring()
                T.wait(yT_ready, bank_free[w])
                for k in range(DT):
                    m = Last.yT = T.op(pe.transpose, psum[0:rows_, w, k * P:(k + 1) * P],
                                       yT[:, k, st * P:st * P + rows_], ident[:, :])
                A.wait(m, tables, Last.y)
                m = A.op(act.activation, y_hi[0:rows_, st, :], psum[0:rows_, w, :], ACT.Copy,
                         scale=slot_gate[0:rows_, st, i:i + 1])
                V.wait(m, Last.y)
                m = bank_free[w] = V.op(dve.scalar_tensor_tensor, y_lo[0:rows_, st, :], psum[0:rows_, w, :],
                                        slot_gate[0:rows_, st, i:i + 1], y_hi[0:rows_, st, :].bitcast(F32),
                                        ALU.mult, ALU.subtract)
            Last.slot_gate = m
            return m

        def scatter(gated):
            T.wait(gated)
            for b in OUT:
                T.wait(bank_free[b])
                for st, rows_ in STILES:
                    for part in (y_hi, y_lo):
                        m = T.op(pe.matmul, psum[:, b, :], pickT[0:rows_, st, b * P:(b + 1) * P],
                                 part[0:rows_, st, :], start=(first_scatter[0] and st == 0 and part is y_hi),
                                 stop=False, skip_group_check=True)
            first_scatter[0] = False
            Last.y = Last.pickT = m

        def experts_round(r, preloaded):
            waiting = None
            for pair in range(EXPERTS // 2):
                half = pair % 2
                gathered = gather(pair, r, half)
                for i in range(2):
                    e = 2 * pair + i
                    w1_mark, w2_mark = preloaded.pop((r, e)) if (r, e) in preloaded else expert_loads(e)
                    hidden_ready, gated = hidden_layer(e, i, w1_mark, gathered, r,
                                                       lambda: turn_output(*waiting) if waiting else None)
                    if waiting:
                        scatter(gated)
                    tables = slot_tables(e, i, half)
                    yT_ready = output_layer(w2_mark, hidden_ready, e, r)
                    if e + 2 < EXPERTS:
                        preloaded[r, e + 2] = expert_loads(e + 2)
                    waiting = (i, yT_ready, tables)
            scatter(turn_output(*waiting))

        T.wait(load_ready)
        T.count_step = len(T.steps)
        experts_round(0, loads)

        everyone = (T, V, A, G, S)
        known = {q: dict(q.waited) for q in everyone}
        for q, name in zip(everyone, ("tensor", "vector", "scalar", "gpsimd", "sync")):
            q.wait(load_ready)
            q.branch = len(q.steps)
            known[q] = dict(q.waited)
            q.done = signal(name + "_extra_done")
        s_w = [signal(f"extra_weights{i}_in") for i in range(WSLOTS)]
        for r in range(1, ROUNDS):
            loads = {(r, 0): expert_loads(0), (r, 1): expert_loads(1)}
            experts_round(r, loads)
        for q, name in zip(everyone, ("tensor", "vector", "scalar", "gpsimd", "sync")):
            q.join = len(q.steps)
            q.waited = known[q]
            q.done = signal(name + "_end_done")

        T.wait(gateT_ready, route_loaded)
        out_ready = []
        for b in OUT:
            m = T.op(pe.matmul, psum[:, b, :], gateT[:, b * P:(b + 1) * P], b2[:, :], start=False, stop=True,
                     skip_group_check=True)
            V.wait(m)
            out_ready.append(V.op(dve.tensor_tensor, x1[:, b, :], psum[:, b, :], x1[:, b, :], ALU.add))
        s_out = signal("out_stored")
        for b in range(B):
            S.wait(out_ready[b])
            stored = S.dma(s_out, sp.dma_start, out[b], x1[:, b, :])
        S.wait(stored)

        block = life.enter_context(nc.Block())

        @block.tensor
        def _(engine):
            T.replay(engine, load[0:1, 0:1], counts)

        @block.vector
        def _(engine):
            V.replay(engine, load[0:1, 0:1], counts)

        @block.scalar
        def _(engine):
            A.replay(engine, load[0:1, 0:1], counts)

        @block.gpsimd
        def _(engine):
            G.replay(engine, load[0:1, 0:1], counts)

        @block.sync
        def _(engine):
            S.replay(engine, load[0:1, 0:1], counts)


def lay_out(i):
    import numpy as np
    c = lambda t: np.ascontiguousarray(np.asarray(t))
    return {
        "x": c(i["x"]), "ctx_t": c(np.asarray(i["ctx_1024"]).transpose(0, 2, 1)),
        "bias": c(np.asarray(i["fside_1x1xSxS2_0"]).reshape(P, KEYS)),
        "wq": c(i["L0_xattn_Wq"]), "wk": c(i["L0_xattn_Wk"]), "wv": c(i["L0_xattn_Wv"]), "wo": c(i["L0_xattn_Wo"]),
        "attn_norm": c(i["L0_attn_attn_norm_w"]), "g_norm": c(i["L0_attn_g_norm_w"]),
        "mlp_norm": c(i["L0_attn_mlp_norm_w"]), "lower": c(np.asarray(i["L0_attn_lower_bound"]).reshape(DT, P).T),
        "wr": c(i["L0_ffn_Wr"]), "br": c(i["L0_ffn_br"]), "w1": c(i["L0_ffn_W1"]), "w2": c(i["L0_ffn_W2"]),
        "b1_t": c(np.asarray(i["L0_ffn_b1"]).reshape(EXPERTS, HT, P).transpose(2, 0, 1)), "b2": c(i["L0_ffn_b2"]),
        "w_i_t": c(np.asarray(i["L0_attn_w_i"]).T), "w_f_t": c(np.asarray(i["L0_attn_w_f"]).T),
        "w_g_t": c(np.asarray(i["L0_attn_w_g"]).T), "w_o_t": c(np.asarray(i["L0_attn_w_o"]).T),
        "w_gate_t": c(np.asarray(i["L0_attn_w_gate"]).T), "w_down_t": c(np.asarray(i["L0_attn_w_down"]).T),
    }


def kernel(**inputs):
    import concourse.bacc as bacc
    from concourse.bass_utils import run_bass_kernel_spmd

    nc = bacc.Bacc("TRN2", target_bir_lowering=False, num_devices=1, dynamic_dma_scratch_size=1024)
    arrays = {f"in_{name}": t for name, t in lay_out(inputs).items()}
    args = {name[3:]: nc.dram_tensor(name, t.shape, mybir.dt.from_np(t.dtype), kind="ExternalInput").ap()
            for name, t in arrays.items()}
    out = nc.dram_tensor("out_x", (B, P, D), F32, kind="ExternalOutput").ap()
    perceiver_block(nc, args, out)
    return run_bass_kernel_spmd(nc, [arrays], core_ids=[0]).results[0]["out_x"]
```
